# Optimizing a Trainium2 kernel written in Bass

```python
import numpy as np
import jax
import jax.numpy as jnp

def _softmax(x, axis=-1):
    return jax.nn.softmax(x, axis=axis)

def _gelu(x):
    return jax.nn.gelu(x, approximate=True)

def _silu(x):
    return jax.nn.silu(x)

def _sigmoid(x):
    return jax.nn.sigmoid(x)

def _layernorm(x, axis=-1, eps=1e-05):
    m = jnp.mean(x, axis=axis, keepdims=True)
    v = jnp.var(x, axis=axis, keepdims=True)
    return (x - m) / jnp.sqrt(v + eps)

def _scatter_add(tgt, idx, src, axis=0):
    return tgt.at[idx].add(src)

def _segment_sum(src, seg, n):
    return jax.ops.segment_sum(src, seg, n)
kernel_name = 'mk_vit_tower_cls_d1_tok_img768_r4_cedf85'

def setup_inputs(seed: int=0):
    np.random.seed(seed)
    _w = jnp.asarray

    def _rec_inputs():
        import jax
        import jax.numpy as jnp
        _rk = jax.random.key(seed)
        x = -0.000596345 + 1.00056 * jax.random.normal(jax.random.fold_in(_rk, 1), (2, 3, 64, 64), jnp.float32)
        cls_tok = 0.02 * jax.random.normal(jax.random.fold_in(_rk, 5), (1, 1, 192), jnp.float32)
        return (x, cls_tok)
    x, cls_tok = _rec_inputs()

    def _L0_tok_setup():
        import jax, jax.numpy as jnp
        import numpy as np
        B = 16
        IMG = 64
        CH = 3
        EMBED = 64
        GP = 16
        PRE = [1, 2, 4]
        N_LEVELS = 3
        FUSED = EMBED * N_LEVELS

        def hilbert_flat_indices(n):
            t = np.arange(n * n, dtype=np.int64)
            x = np.zeros(n * n, dtype=np.int64)
            y = np.zeros(n * n, dtype=np.int64)
            s = 1
            while s < n:
                rx = 1 & t // 2
                ry = 1 & (t ^ rx)
                swap = ry == 0
                flip = swap & (rx == 1)
                x = np.where(flip, s - 1 - x, x)
                y = np.where(flip, s - 1 - y, y)
                x2 = np.where(swap, y, x)
                y2 = np.where(swap, x, y)
                x, y = (x2, y2)
                x = x + s * rx
                y = y + s * ry
                t = t // 4
                s *= 2
            return y * n + x

        def _level(x, idx, W, b, p, gp):
            Bsz, C, H, _ = x.shape
            h = H // p
            t = x.reshape(Bsz, C, h, p, h, p).transpose(0, 2, 4, 3, 5, 1).reshape(Bsz, h * h, p * p * C)
            t = t[:, idx]
            t = t.reshape(Bsz, h * h // gp, gp * p * p * C)
            return t @ W.T + b

        def _interp_linear(x, n_out):
            L = x.shape[1]
            pos = (jnp.arange(n_out, dtype=jnp.float32) + 0.5) * (L / n_out) - 0.5
            pos = jnp.clip(pos, 0.0, L - 1)
            i0 = jnp.floor(pos).astype(jnp.int32)
            i1 = jnp.minimum(i0 + 1, L - 1)
            w = (pos - i0).astype(x.dtype)
            return x[:, i0] * (1.0 - w)[None, :, None] + x[:, i1] * w[None, :, None]
        key = jax.random.key(seed)
        ks = jax.random.split(key, 9)
        inp = {'x': jax.random.normal(ks[0], (B, CH, IMG, IMG), jnp.float32)}
        for i, p in enumerate(PRE):
            din = CH * p * p * GP
            inp[f'W{i}'] = jax.random.normal(ks[1 + 2 * i], (EMBED, din), jnp.float32) * din ** (-0.5)
            inp[f'b{i}'] = jax.random.normal(ks[2 + 2 * i], (EMBED,), jnp.float32) * 0.02
        inp['Wf'] = jax.random.normal(ks[7], (FUSED, FUSED), jnp.float32) * FUSED ** (-0.5)
        inp['bf'] = jax.random.normal(ks[8], (FUSED,), jnp.float32) * 0.02
        for i, p in enumerate(PRE):
            inp[f'idx{i}'] = jnp.asarray(hilbert_flat_indices(IMG // p), jnp.int32)
        return inp
    _L0_tok_all = _L0_tok_setup()
    _L0_tok_in = {k: v for k, v in _L0_tok_all.items() if k in ('W0', 'b0', 'W1', 'b1', 'W2', 'b2', 'Wf', 'bf', 'idx0', 'idx1', 'idx2')}
    del _L0_tok_all

    def _L0_attn_setup():
        import jax, jax.numpy as jnp
        import numpy as np
        N_HEADS = 12
        HIDDEN = 192
        HEAD_DIM = HIDDEN // N_HEADS
        B, S = (4, 512)
        key = jax.random.key(seed)
        ks = jax.random.split(key, 7)
        bound = 1.0 / np.sqrt(HIDDEN)
        inputs = jax.random.normal(ks[0], (B, S, HIDDEN), dtype=jnp.float32)
        Wq = jax.random.uniform(ks[1], (HIDDEN, HIDDEN), jnp.float32, -bound, bound)
        bq = jax.random.uniform(ks[2], (HIDDEN,), jnp.float32, -bound, bound)
        Wk = jax.random.uniform(ks[3], (HIDDEN, HIDDEN), jnp.float32, -bound, bound)
        bk = jax.random.uniform(ks[4], (HIDDEN,), jnp.float32, -bound, bound)
        Wv = jax.random.uniform(ks[5], (HIDDEN, HIDDEN), jnp.float32, -bound, bound)
        bv = jax.random.uniform(ks[6], (HIDDEN,), jnp.float32, -bound, bound)
        return {'inputs': inputs, 'Wq': Wq, 'bq': bq, 'Wk': Wk, 'bk': bk, 'Wv': Wv, 'bv': bv}
    _L0_attn_all = _L0_attn_setup()
    _L0_attn_in = {k: v for k, v in _L0_attn_all.items() if k in ('Wq', 'bq', 'Wk', 'bk', 'Wv', 'bv')}
    del _L0_attn_all

    def _L0_ffn_setup():
        import jax, jax.numpy as jnp
        import numpy as np
        from jax import lax
        DIM = 192
        INTER = 128
        E = 8
        G = 4
        TOPK_G = 2
        TOPK = 2
        ROUTE_SCALE = 1.0

        def _gate(x2, gate_weight, gate_bias):
            T = x2.shape[0]
            scores = jax.nn.sigmoid(x2 @ gate_weight.T)
            s = scores + gate_bias
            sv = s.reshape(T, G, E // G)
            top2, _ = lax.top_k(sv, 2)
            group_scores = top2.sum(-1)
            _, gidx = lax.top_k(group_scores, TOPK_G)
            gmask = jnp.zeros((T, G), bool).at[jnp.arange(T)[:, None], gidx].set(True)
            masked = jnp.where(gmask[:, :, None], sv, -jnp.inf).reshape(T, E)
            _, idx = lax.top_k(masked, TOPK)
            w = jnp.take_along_axis(scores, idx, axis=1)
            w = w / (w.sum(-1, keepdims=True) + 1e-06) * ROUTE_SCALE
            return (w, idx)
        key = jax.random.key(seed)
        ks = jax.random.split(key, 9)
        s = 1.0 / np.sqrt(DIM)
        si = 1.0 / np.sqrt(INTER)
        return {'x': jax.random.normal(ks[0], (4, 1024, DIM), jnp.float32), 'gate_weight': jax.random.uniform(ks[1], (E, DIM), jnp.float32, -s, s), 'gate_bias': jnp.zeros((E,), jnp.float32), 'w1': jax.random.uniform(ks[2], (E, INTER, DIM), jnp.float32, -s, s), 'w2': jax.random.uniform(ks[3], (E, DIM, INTER), jnp.float32, -si, si), 'w3': jax.random.uniform(ks[4], (E, INTER, DIM), jnp.float32, -s, s), 'sw1': jax.random.uniform(ks[5], (INTER, DIM), jnp.float32, -s, s), 'sw2': jax.random.uniform(ks[6], (DIM, INTER), jnp.float32, -si, si), 'sw3': jax.random.uniform(ks[7], (INTER, DIM), jnp.float32, -s, s)}
    _L0_ffn_all = _L0_ffn_setup()
    _L0_ffn_in = {k: v for k, v in _L0_ffn_all.items() if k in ('gate_weight', 'gate_bias', 'w1', 'w2', 'w3', 'sw1', 'sw2', 'sw3')}
    del _L0_ffn_all
    return {'x': x, 'cls_tok': cls_tok, 'L0_tok_W0': _L0_tok_in['W0'], 'L0_tok_b0': _L0_tok_in['b0'], 'L0_tok_W1': _L0_tok_in['W1'], 'L0_tok_b1': _L0_tok_in['b1'], 'L0_tok_W2': _L0_tok_in['W2'], 'L0_tok_b2': _L0_tok_in['b2'], 'L0_tok_Wf': _L0_tok_in['Wf'], 'L0_tok_bf': _L0_tok_in['bf'], 'L0_tok_idx0': _L0_tok_in['idx0'], 'L0_tok_idx1': _L0_tok_in['idx1'], 'L0_tok_idx2': _L0_tok_in['idx2'], 'L0_attn_Wq': _L0_attn_in['Wq'], 'L0_attn_bq': _L0_attn_in['bq'], 'L0_attn_Wk': _L0_attn_in['Wk'], 'L0_attn_bk': _L0_attn_in['bk'], 'L0_attn_Wv': _L0_attn_in['Wv'], 'L0_attn_bv': _L0_attn_in['bv'], 'L0_ffn_gate_weight': _L0_ffn_in['gate_weight'], 'L0_ffn_gate_bias': _L0_ffn_in['gate_bias'], 'L0_ffn_w1': _L0_ffn_in['w1'], 'L0_ffn_w2': _L0_ffn_in['w2'], 'L0_ffn_w3': _L0_ffn_in['w3'], 'L0_ffn_sw1': _L0_ffn_in['sw1'], 'L0_ffn_sw2': _L0_ffn_in['sw2'], 'L0_ffn_sw3': _L0_ffn_in['sw3']}

def reference(x, cls_tok, L0_tok_W0, L0_tok_b0, L0_tok_W1, L0_tok_b1, L0_tok_W2, L0_tok_b2, L0_tok_Wf, L0_tok_bf, L0_tok_idx0, L0_tok_idx1, L0_tok_idx2, L0_attn_Wq, L0_attn_bq, L0_attn_Wk, L0_attn_bk, L0_attn_Wv, L0_attn_bv, L0_ffn_gate_weight, L0_ffn_gate_bias, L0_ffn_w1, L0_ffn_w2, L0_ffn_w3, L0_ffn_sw1, L0_ffn_sw2, L0_ffn_sw3):
    import jax
    import jax.numpy as jnp

    def _L0_tok_ref(x, W0, b0, W1, b1, W2, b2, Wf, bf, idx0, idx1, idx2):
        import jax, jax.numpy as jnp
        import numpy as np
        B = 16
        IMG = 64
        CH = 3
        EMBED = 64
        GP = 16
        PRE = [1, 2, 4]
        N_LEVELS = 3
        FUSED = EMBED * N_LEVELS

        def hilbert_flat_indices(n):
            t = np.arange(n * n, dtype=np.int64)
            x = np.zeros(n * n, dtype=np.int64)
            y = np.zeros(n * n, dtype=np.int64)
            s = 1
            while s < n:
                rx = 1 & t // 2
                ry = 1 & (t ^ rx)
                swap = ry == 0
                flip = swap & (rx == 1)
                x = np.where(flip, s - 1 - x, x)
                y = np.where(flip, s - 1 - y, y)
                x2 = np.where(swap, y, x)
                y2 = np.where(swap, x, y)
                x, y = (x2, y2)
                x = x + s * rx
                y = y + s * ry
                t = t // 4
                s *= 2
            return y * n + x

        def _level(x, idx, W, b, p, gp):
            Bsz, C, H, _ = x.shape
            h = H // p
            t = x.reshape(Bsz, C, h, p, h, p).transpose(0, 2, 4, 3, 5, 1).reshape(Bsz, h * h, p * p * C)
            t = t[:, idx]
            t = t.reshape(Bsz, h * h // gp, gp * p * p * C)
            return t @ W.T + b

        def _interp_linear(x, n_out):
            L = x.shape[1]
            pos = (jnp.arange(n_out, dtype=jnp.float32) + 0.5) * (L / n_out) - 0.5
            pos = jnp.clip(pos, 0.0, L - 1)
            i0 = jnp.floor(pos).astype(jnp.int32)
            i1 = jnp.minimum(i0 + 1, L - 1)
            w = (pos - i0).astype(x.dtype)
            return x[:, i0] * (1.0 - w)[None, :, None] + x[:, i1] * w[None, :, None]
        Ws = [(idx0, W0, b0, PRE[0]), (idx1, W1, b1, PRE[1]), (idx2, W2, b2, PRE[2])]
        outs = [_level(x, idx, W, b, p, GP) for idx, W, b, p in Ws]
        n_tokens = outs[0].shape[1]
        outs = [outs[0]] + [_interp_linear(o, n_tokens) for o in outs[1:]]
        y = jnp.concatenate(outs, axis=-1)
        return y @ Wf.T + bf

    def _L0_attn_ref(inputs, Wq, bq, Wk, bk, Wv, bv):
        import jax, jax.numpy as jnp
        import numpy as np
        N_HEADS = 12
        HIDDEN = 192
        HEAD_DIM = HIDDEN // N_HEADS
        B, S = (4, 512)
        b, s, d = inputs.shape
        h, hd = (N_HEADS, HEAD_DIM)

        def proj(W, bias):
            y = inputs @ W.T + bias
            return y.reshape(b, s, h, hd).transpose(0, 2, 1, 3)
        q = proj(Wq, bq)
        k = proj(Wk, bk)
        v = proj(Wv, bv)
        scale = 1.0 / jnp.sqrt(jnp.asarray(hd, inputs.dtype))
        scores = jnp.einsum('bhqd,bhkd->bhqk', q, k) * scale
        attn = jax.nn.softmax(scores, axis=-1)
        out = jnp.einsum('bhqk,bhkd->bhqd', attn, v)
        return out.transpose(0, 2, 1, 3).reshape(b, s, d)

    def _L0_ffn_ref(x, gate_weight, gate_bias, w1, w2, w3, sw1, sw2, sw3):
        import jax, jax.numpy as jnp
        import numpy as np
        from jax import lax
        DIM = 192
        INTER = 128
        E = 8
        G = 4
        TOPK_G = 2
        TOPK = 2
        ROUTE_SCALE = 1.0

        def _gate(x2, gate_weight, gate_bias):
            T = x2.shape[0]
            scores = jax.nn.sigmoid(x2 @ gate_weight.T)
            s = scores + gate_bias
            sv = s.reshape(T, G, E // G)
            top2, _ = lax.top_k(sv, 2)
            group_scores = top2.sum(-1)
            _, gidx = lax.top_k(group_scores, TOPK_G)
            gmask = jnp.zeros((T, G), bool).at[jnp.arange(T)[:, None], gidx].set(True)
            masked = jnp.where(gmask[:, :, None], sv, -jnp.inf).reshape(T, E)
            _, idx = lax.top_k(masked, TOPK)
            w = jnp.take_along_axis(scores, idx, axis=1)
            w = w / (w.sum(-1, keepdims=True) + 1e-06) * ROUTE_SCALE
            return (w, idx)
        B, S, D = x.shape
        x2 = x.reshape(-1, D)
        T = x2.shape[0]
        weights, indices = _gate(x2, gate_weight, gate_bias)
        cw = jnp.zeros((T, E), x.dtype).at[jnp.arange(T)[:, None], indices].add(weights)
        h1 = jnp.einsum('td,eid->tei', x2, w1)
        h3 = jnp.einsum('td,eid->tei', x2, w3)
        h = jax.nn.silu(h1) * h3
        y = jnp.einsum('tei,edi,te->td', h, w2, cw)
        z = jax.nn.silu(x2 @ sw1.T) * (x2 @ sw3.T) @ sw2.T
        return (y + z).reshape(B, S, D)
    h = _L0_tok_ref(x, L0_tok_W0, L0_tok_b0, L0_tok_W1, L0_tok_b1, L0_tok_W2, L0_tok_b2, L0_tok_Wf, L0_tok_bf, L0_tok_idx0, L0_tok_idx1, L0_tok_idx2)
    h = jnp.concatenate([jnp.broadcast_to(cls_tok, (h.shape[0], 1, h.shape[2])), h], axis=1)
    h = h + _L0_attn_ref(_layernorm(h, axis=-1), L0_attn_Wq, L0_attn_bq, L0_attn_Wk, L0_attn_bk, L0_attn_Wv, L0_attn_bv)
    h = h + _L0_ffn_ref(_layernorm(h, axis=-1), L0_ffn_gate_weight, L0_ffn_gate_bias, L0_ffn_w1, L0_ffn_w2, L0_ffn_w3, L0_ffn_sw1, L0_ffn_sw2, L0_ffn_sw3)
    return h

_drawn_inputs = setup_inputs


def setup_inputs(seed=0):
    import zlib

    import numpy as np

    out = dict(_drawn_inputs(seed))
    spreads = {'L0_ffn_gate_bias': (0.0, 0.1)}
    factors = {'cls_tok': 26.677,
     'L0_tok_b0': 3.393,
     'L0_tok_b1': 3.204,
     'L0_tok_b2': 2.925,
     'L0_attn_bq': 8.0,
     'L0_attn_bk': 64.0}
    for name, (base, spread) in spreads.items():
        noise = np.random.default_rng([zlib.crc32(name.encode()), seed]).standard_normal(out[name].shape)
        drawn = base * np.exp(spread * noise) if base else spread * noise
        out[name] = jnp.asarray(drawn.astype(out[name].dtype))
    for name, factor in factors.items():
        out[name] = (out[name] * factor).astype(out[name].dtype)
    return out
```

```python
from contextlib import ExitStack

import concourse.bass as bass
from concourse import mybir

F32 = mybir.dt.float32
F32R = mybir.dt.float32r
BF16 = mybir.dt.bfloat16
I32 = mybir.dt.int32
ALU = mybir.AluOpType
ACT = mybir.ActivationFunctionType
AX = mybir.AxisListType

P = 128
B = 2
CH = 3
D = 192
D2 = D - P
NH = 12
HD = D // NH
E = 8
INTER = 128
GROUPS = 4
GP = 16
TOK = 256
CLS = TOK
N = TOK + 2
CHUNKS = TOK // P
NPIX = 4096
LOW = 16
ROWS0 = B * CH * LOW
COLS0 = 512
STEPS0 = NPIX // COLS0
EMB = 64
TOK1, TOK2 = 64, 16
F1, F2 = 12, 48
EPS = 1e-5
SCALE = HD ** -0.5
FAR = 1e30
GATE = 2 * INTER * (E + 1)
WFF = GATE + E
RAW = WFF // 4
K_STACK = 96
PT_RING = 4
UNITS = CHUNKS * NH // 2
LAG = 3
LOG_EXP = "natural_log_exp_and_others"


def build(nc, t, out):
    ctx = ExitStack()
    with ctx:
        def sb(name, shape, dt=F32):
            return ctx.enter_context(nc.sbuf_tensor(name, shape, dt))

        class Signals:

            def __init__(self):
                self.made = {}

            def __call__(self, name):
                if name not in self.made:
                    self.made[name] = ctx.enter_context(nc.semaphore(name))
                return self.made[name]

        s = Signals()

        arena = sb("arena", [P, 10820])
        idx_all = arena[:, 0:NPIX].bitcast(I32)
        picked = arena[:, 4096:5632].rearrange("p (r n) -> p r n", r=3)
        hi_idx = arena[:, 5632:6656].bitcast(I32).rearrange("p (r n) -> p r n", r=2)
        lo_idx = arena[:, 6656:7680].bitcast(I32).rearrange("p (r n) -> p r n", r=2)
        onehot = arena[:, 7680:8704].bitcast(BF16).rearrange("p (r k n) -> p r k n", r=2, k=2)
        w_l0 = arena[0:ROWS0, 8704:10752].rearrange("p (g m) -> p g m", g=GP)
        probs = arena[:, 0:2048].rearrange("p (r k n) -> p r k n", r=PT_RING, k=CHUNKS)
        hidden = arena[:, 2048:6692].rearrange("p (b e n) -> p b e n", b=B, e=E + 1)
        share = arena[:, 6692:10820].rearrange("p (b m) -> p b m", b=B)

        arena2 = sb("arena2", [P, 4900])

        class Carve:

            def __init__(self):
                self.at = 0

            def __call__(self, shape, dt=F32):
                n = 1
                for d in shape[1:]:
                    n *= d
                words = n if dt == F32 else (n + 1) // 2
                tile = arena2[0:shape[0], self.at:self.at + words]
                self.at += words
                assert self.at <= 4900
                if dt != F32:
                    tile = tile.bitcast(dt)
                names = [f"a{i}" for i in range(len(shape) - 1)]
                sizes = dict(zip(names, shape[1:]))
                return tile.rearrange(f"p ({' '.join(names)}) -> p {' '.join(names)}", **sizes) \
                    if len(names) > 1 else tile

        early, late = Carve(), Carve()
        pix = early([P, 2, ROWS0])
        pix_rest = early([P, 2, 2, ROWS0])
        pix_part = early([P, 3, 2, ROWS0], BF16)
        cst = sb("cst", [P, 8])
        gidx_raw = sb("gidx_raw", [P, 10], I32)
        gidx = sb("gidx", [P, 10], I32)
        got1 = early([P, 8, B * F1])
        got2 = early([P, 2, B * F2])
        got_by_batch = early([P, 2, B, 96])
        got_t = early([96, 4, P])
        w_l1 = early([96, 2, EMB])
        w_l2 = early([96, 8, EMB])
        emb1 = early([EMB, P])
        emb2 = early([EMB, B * TOK2])
        bias_l = sb("bias_l", [P, 3])
        emb0 = early([P, TOK])
        w_fuse0 = early([P, B, D])
        w_fuse12 = early([EMB, 2, D])
        interp = early([P, TOK])
        coarse = early([P, B, D])
        ident = sb("ident", [P, P])
        hres = sb("hres", [P, B, 3, D])
        logvar = sb("logvar", [P, 3])
        stats = sb("stats", [P, 3, 6])
        meanvar = sb("meanvar", [P, 3, 2])
        rstd = sb("rstd", [P, 3])
        xn = sb("xn", [P, 3, D + D2])
        xt = sb("xt", [P, B, 3, N], F32R)
        w_raw = sb("w_raw", [P, 2, RAW])
        wq_hi = sb("wq_hi", [P, 2, 3 * D], F32R)
        wq_lo = sb("wq_lo", [P, 2, 3 * D], F32R)
        wf_hi = sb("wf_hi", [P, 2, WFF], F32R)
        wf_lo = sb("wf_lo", [P, 2, WFF], F32R)
        w_down = sb("w_down", [P, E + 1, D])
        bias_qk = sb("bias_qk", [P, 4])
        bias_v = sb("bias_v", [P, D])
        qk = sb("qk", [P, B, 4, N])
        qk_part = sb("qk_part", [P, 4, 2, N], F32R)
        q_stack = sb("q_stack", [P, B, NH, N], F32R)
        k_stack = sb("k_stack", [P, B, NH, N], F32R)
        vals = sb("vals", [P, B, CHUNKS, NH, HD + 1])
        headmask = sb("headmask", [P, 2, NH])
        blockmask = sb("blockmask", [NH, D])
        q_cls = sb("q_cls", [P, 2, NH])
        k_cls = sb("k_cls", [P, 2, NH])
        v_cls = sb("v_cls", [NH, D])
        v_block = sb("v_block", [K_STACK, NH, 32])
        negmax = sb("negmax", [P, B, CHUNKS, NH])
        nm_part = qk_part[0:NH, :, :, 0:TOK].rearrange("p (b a) k n -> p b a k n", b=B)[:, :, 0, :, :]
        nm_row = late([NH, B, TOK])
        cls_neg = sb("cls_neg", [NH, B])
        cls_sum = sb("cls_sum", [NH, B])
        cls_rsum = sb("cls_rsum", [NH, B])
        cls_probs = late([NH, B, TOK + 1])
        clskey_in = late([NH, TOK])
        clskey_probs = late([K_STACK, B, TOK])
        cls_probs_t = sb("cls_probs_t", [P, CHUNKS * NH])
        cls_sumv = late([NH, 2, D])
        ones = sb("ones", [NH, 1])
        attn_t = late([P, 3, TOK])
        rsum = sb("rsum", [P, CHUNKS, NH])
        attn = late([P, CHUNKS, D])
        gexp = sb("gexp", [P, 3, E])
        gden = sb("gden", [P, 3, E])
        gsc = sb("gsc", [P, 3, E])
        gsb = sb("gsb", [P, 3, E])
        gbias = sb("gbias", [P, 3, E])
        ggrp = sb("ggrp", [P, 3, GROUPS])
        gsel = sb("gsel", [P, 3, GROUPS])
        gpen = sb("gpen", [P, 3, GROUPS])
        gmsk = sb("gmsk", [P, 3, E])
        gge = late([P, 3, E * E])
        ggt = late([P, 3, E * E])
        grank = sb("grank", [P, 3, E])
        gsum = sb("gsum", [P, 3])
        cw = sb("cw", [P, 3, E])
        order = sb("order", [P, 2, GROUPS * GROUPS + E * E])
        cw_t = late([E, B, N])
        silu = late([P, 2, N])
        out_cls = sb("out_cls", [B, D])

        bank = ctx.enter_context(nc.psum_tensor("bank", [P, 8, 512], F32))

        qk_dram = nc.dram_tensor("qk_dram", (B, 2, 2 * D, N), F32, kind="Internal").ap()
        cw_dram = nc.dram_tensor("cw_dram", (B, E * N), F32, kind="Internal").ap()

        MISC, ACC, SCORE = (7, 3), (6, 2), ((4, 5), (0, 1))
        MAXB = ((0, 2, 4), (0, 2))
        TURN = ((6, 7), (0, 1), (6, 7), (2, 3))
        QKB = (2, 3, 4, 5)
        VB = (6, 0)
        GATEB = (7, 3)
        FFB = ((0, 1), (4, 5))
        YB, YCLS = (6, 2), 7
        QK_ROWS = (P, D2, P, D2)
        QK_AT = (0, P, D, D + P)

        PASSES = ((0, 0, 0), (1, 0, 0), (0, 0, 1), (0, 1, 2), (1, 1, 2))

        block = ctx.enter_context(nc.Block())

        @block.sync
        def _(sp):
            sp.dma_start(pix[:], t["pix"]).then_inc(s("ld_pix"), 16)
            sp.dma_start(cst[:], t["cst"]).then_inc(s("ld_cst"), 16)
            for q in range(4):
                cols = slice(q * NPIX // 4, (q + 1) * NPIX // 4)
                sp.dma_start(idx_all[:, cols], t["idx0"][cols].partition_broadcast(P))\
                    .then_inc(s(f"ld_idx{q}"), 16)
            sp.dma_start(w_l0, t["w_l0"]).then_inc(s("ld_l0"), 16)
            sp.dma_start(interp[:], t["interp"]).then_inc(s("ld_fuse"), 16)
            sp.dma_start(w_fuse0[:], t["w_fuse0"]).then_inc(s("ld_fuse"), 16)
            sp.wait_ge(s("p_zero"), 2)
            for b in range(B):
                sp.dma_start(hres[0:1, b, 2, :], t["cls"]).then_inc(s("ld_cls"), 16)
                sp.dma_start(coarse[96:97, b, :], t["bf"]).then_inc(s("ld_fuse"), 16)
            sp.dma_start(headmask[:], t["headmask"]).then_inc(s("ld_att"), 16)
            sp.dma_start(blockmask[:], t["blockmask"]).then_inc(s("ld_att"), 16)
            sp.dma_start(bias_v[:], t["bv"].partition_broadcast(P)).then_inc(s("ld_att"), 16)
            sp.dma_start(bias_qk[:], t["bqk"]).then_inc(s("ld_att"), 16)
            sp.dma_start(gbias[:].rearrange("p c e -> p (c e)"), t["gbias"].partition_broadcast(P)).then_inc(s("ld_gate"), 16)
            sp.dma_start(order[:].rearrange("p a n -> p (a n)"), t["order"].partition_broadcast(P)).then_inc(s("ld_gate"), 16)
            sp.dma_start(w_down[:], t["w_down"]).then_inc(s("ld_down"), 16)

            def scatter_qk(b):
                for i in range(4):
                    rows, at = QK_ROWS[i], QK_AT[i]
                    sp.wait_ge(s("a_qkhi"), 4 * b + i + 1)
                    sp.wait_ge(s("v_qklo"), 4 * b + i + 1)
                    sp.dma_start(qk_dram[b, :, at:at + rows, :].rearrange("p f n -> f p n"),
                                 qk_part[0:rows, i, :, :].bitcast(F32)).then_inc(s(f"qk_out{b}"), 16)
                sp.wait_ge(s(f"qk_out{b}"), 64)
                for i, (stack, parts) in enumerate(((q_stack, (0, 1, 0, 1)), (k_stack, (0, 0, 1, 1)))):
                    for r, part in enumerate(parts):
                        src = qk_dram[b, part, i * D:(i + 1) * D, :].rearrange("(h d) n -> d h n", d=HD)
                        sp.dma_start(stack[r * HD:(r + 1) * HD, b, :, :].bitcast(F32), src)\
                            .then_inc(s(f"stack_in{b}"), 16)

            def maxima_rows(b):
                sp.wait_ge(s("v_nm"), 2 * (b + 1))
                for part in range(2):
                    sp.dma_start(q_stack[64 + part:65 + part, b, :, 0:TOK].bitcast(F32),
                                 nm_part[:, b, part, :].bitcast(F32))\
                        .then_inc(s(f"nm_in{b}"), 16)

            def shares(b):
                sp.wait_ge(s("a_cw"), b + 1)
                sp.dma_start(cw_dram[b].rearrange("(e n) -> e n", e=E), cw_t[:, b, :])\
                    .then_inc(s(f"cw_out{b}"), 16)
                sp.wait_ge(s(f"cw_out{b}"), 16)
                sp.dma_start(share[:, b, :], cw_dram[b].partition_broadcast(P)).then_inc(s(f"cw_in{b}"), 16)

            def store(b):
                sp.wait_ge(s("v_out"), b + 1)
                sp.dma_start(out[b, 1:1 + TOK, :].rearrange("(c p) d -> p c d", p=P), hres[:, b, 0:2, :])\
                    .then_inc(s("stored"), 16)

            scatter_qk(0)
            scatter_qk(1)
            maxima_rows(0)
            maxima_rows(1)
            shares(0)
            shares(1)
            store(0)
            store(1)
            sp.wait_ge(s("v_outcls"), 1)
            sp.dma_start(out[:, 0, :], out_cls[:]).then_inc(s("stored"), 16)
            sp.wait_ge(s("stored"), 48)

        @block.gpsimd
        def _(pool):
            pool.memset(hres[:, :, 2, :], 0.0).then_inc(s("p_zero"), 1)
            pool.memset(coarse[:], 0.0).then_inc(s("p_zero"), 1)
            pool.wait_ge(s("v_gidx"), 2)
            for k in range(10):
                dst, src = (got1[:, k, :], t["pix1"]) if k < 8 else (got2[:, k - 8, :], t["pix2"])
                pool.indirect_dma_start(dst, None, src[:, :],
                                        bass.IndirectOffsetOnAxis(ap=gidx[:, k:k + 1], axis=0))\
                    .then_inc(s("gathered"), 16)

            pool.wait_ge(s("ld_qkv"), 32)
            pool.tensor_copy(wq_hi[:], w_raw[:, :, 0:3 * D]).then_inc(s("p_split"), 1)
            pool.wait_ge(s("p_split"), 1)
            pool.tensor_tensor(wq_lo[:], w_raw[:, :, 0:3 * D], wq_hi[:].bitcast(F32), ALU.subtract)\
                .then_inc(s("p_split"), 1)
            pool.memset(vals[:, :, :, :, HD:HD + 1], 1.0).then_inc(s("p_const"), 1)
            pool.memset(v_block[:], 0.0).then_inc(s("p_const"), 1)
            pool.memset(ones[:], 1.0).then_inc(s("p_const"), 1)
            pool.wait_ge(s("p_split"), 2)
            pool.wait_ge(s("p_const"), 3)
            for b in range(B):
                pool.memset(k_stack[64:K_STACK, b, :, :].bitcast(F32), 1.0).then_inc(s("p_stack"), 1)
                pool.memset(q_stack[64:K_STACK, b, :, :].bitcast(F32), 0.0).then_inc(s("p_stack"), 1)
            pool.wait_ge(s("p_stack"), 2 * B)
            pool.memset(gexp[:], 0.0).then_inc(s("p_const"), 1)
            pool.wait_ge(s("t_h"), 2)
            pool.memset(clskey_probs[:], 0.0).then_inc(s("p_const"), 1)
            for half in range(4):
                cols = slice(half * RAW, (half + 1) * RAW)
                pool.wait_ge(s("p_split"), 2 * (half + 1))
                pool.dma_start(w_raw[:], t["w_ff"][half]).then_inc(s(f"ld_ff{half}"), 16)
                pool.wait_ge(s(f"ld_ff{half}"), 16)
                pool.tensor_copy(wf_hi[:, :, cols], w_raw[:]).then_inc(s("p_split"), 1)
                pool.wait_ge(s("p_split"), 2 * half + 3)
                pool.tensor_tensor(wf_lo[:, :, cols], w_raw[:], wf_hi[:, :, cols].bitcast(F32),
                                   ALU.subtract).then_inc(s("p_split"), 1)
            for b in range(B):
                pool.wait_ge(s(f"cw_in{b}"), 16)
                for k in range(1, E + 1):
                    pool.wait_ge(s("v_gate_up"), (E + 1) * b + k + 1)
                    act = hidden[:, b, k, :]
                    pool.tensor_tensor(act, act, share[:, b, (k - 1) * N:k * N], ALU.mult)\
                        .then_inc(s("p_shared"), 1)

        @block.scalar
        def _(act):
            act.dma_start(gidx_raw[:], t["gidx"]).then_inc(s("ld_gidx"), 16)
            act.dma_start(w_raw[:, 0, 0:3 * D], t["w_qkv"][0]).then_inc(s("ld_qkv"), 16)
            act.dma_start(w_raw[:, 1, 0:3 * D], t["w_qkv"][1]).then_inc(s("ld_qkv"), 16)
            act.dma_start(ident[:], t["ident"]).then_inc(s("ld_ident"), 16)
            act.dma_start(w_l1[:], t["w_l1"]).then_inc(s("ld_l12"), 16)
            act.dma_start(w_l2[:], t["w_l2"]).then_inc(s("ld_l12"), 16)
            act.dma_start(w_fuse12[:], t["w_fuse12"]).then_inc(s("ld_l12"), 16)
            act.dma_start(bias_l[:], t["bias_l"]).then_inc(s("ld_l12"), 16)

            nc.scalar.preload_act_table_set(LOG_EXP)

            act.wait_ge(s("gathered"), 160)
            for n, (got, f) in enumerate(((got1, F1), (got2, F2))):
                nc.scalar.activation(got_by_batch[:, n, :, :].rearrange("p b (k f) -> p b k f", f=f),
                                     got[:].rearrange("p k (b f) -> p b k f", b=B), ACT.Copy)\
                    .then_inc(s("a_split"), 1)
            act.wait_ge(s("t_got"), 1)
            nc.scalar.activation(got_t[:].rearrange("p a n -> p (a n)"), bank[0:96, 3, :], ACT.Copy)\
                .then_inc(s("a_got"), 1)
            act.wait_ge(s("t_emb12"), 1)
            act.wait_ge(s("ld_l12"), 64)
            nc.scalar.activation(emb1[:], bank[0:EMB, 4, 0:P], ACT.Identity, bias=bias_l[0:EMB, 1:2])\
                .then_inc(s("a_emb12"), 1)
            nc.scalar.activation(emb2[:], bank[0:EMB, 4, P:P + B * TOK2], ACT.Identity,
                                 bias=bias_l[0:EMB, 2:3]).then_inc(s("a_emb12"), 1)
            act.wait_ge(s("t_coarse"), 1)
            act.wait_ge(s("p_zero"), 2)
            nc.scalar.activation(coarse[0:80, :, :].rearrange("p b d -> p (b d)"), bank[0:80, 5, 0:B * D],
                                 ACT.Copy).then_inc(s("a_coarse"), 1)
            act.wait_ge(s("t_emb0"), STEPS0)
            nc.scalar.activation(emb0[:], bank[:, 2, 0:TOK], ACT.Identity, bias=bias_l[:, 0:1])\
                .then_inc(s("a_emb0"), 1)

            def inv_std(i):
                act.wait_ge(s("v_meanvar"), 3 * (i + 1))
                nc.scalar.activation(logvar[:], meanvar[:, :, 1], ACT.Ln, bias=cst[:, 3:4])\
                    .then_inc(s("a_rstd"), 1)
                act.wait_ge(s("a_rstd"), 2 * i + 1)
                nc.scalar.activation(rstd[:], logvar[:], ACT.Exp, scale=-0.5).then_inc(s("a_rstd"), 1)

            def x_high(i):
                b = i % B
                act.wait_ge(s("t_turned"), i + 1)
                if i >= B:
                    act.wait_ge(s("t_v"), b + 1)
                nc.scalar.activation(xt[:, b, 0, :], bank[:, TURN[i][0], 0:N], ACT.Copy)\
                    .then_inc(s("a_xhi"), 1)
                nc.scalar.activation(xt[:, b, 2, :], bank[:, TURN[i][1], 0:N], ACT.Copy)\
                    .then_inc(s("a_xhi"), 1)

            def qk_high(b):
                for i in range(4):
                    act.wait_ge(s("v_qk"), 4 * b + i + 1)
                    if b:
                        act.wait_ge(s("qk_out0"), 64)
                    nc.scalar.activation(qk_part[0:QK_ROWS[i], i, 0, :], qk[0:QK_ROWS[i], b, i, :], ACT.Copy)\
                        .then_inc(s("a_qkhi"), 1)

            def cls_softmax(b):
                act.wait_ge(s("v_clsmax"), b + 1)
                nc.scalar.activation(cls_probs[:, b, :], bank[0:NH, SCORE[b][0], 0:TOK + 1], ACT.Exp,
                                     bias=cls_neg[:, b:b + 1], accum_out=cls_sum[:, b:b + 1])\
                    .then_inc(s("a_cls"), 1)

            def nm_copy(b):
                act.wait_ge(s("v_nm"), 2 * (b + 1))
                nc.scalar.activation(nm_row[:, b, :], bank[0:NH, MISC[b], 0:TOK], ACT.Copy)\
                    .then_inc(s("a_nm"), 1)

            def clskey(b):
                act.wait_ge(s("v_clskey"), b + 1)
                act.wait_ge(s("p_const"), 5)
                nc.scalar.activation(clskey_probs[0:NH, b, :], clskey_in[:], ACT.Exp).then_inc(s("a_clskey"), 1)

            def exps(b, h):
                n = NH * b + h
                act.wait_ge(s("t_scores"), n + 1)
                if n >= PT_RING:
                    act.wait_ge(s("t_pv"), n - PT_RING + 1)
                nc.scalar.activation(probs[:, h % PT_RING, :, :].rearrange("p k n -> p (k n)"),
                                     bank[:, SCORE[b][h % 2], :], ACT.Exp).then_inc(s("a_exp"), 1)

            def gate_exp(b):
                act.wait_ge(s("t_gate"), b + 1)
                act.wait_ge(s("p_const"), 4)
                if b:
                    act.wait_ge(s("v_gate"), 1)
                nc.scalar.activation(gexp[:, 0:2, :].rearrange("p c e -> p (c e)"),
                                     bank[:, GATEB[b], 0:2 * E], ACT.Exp, scale=-1.0)\
                    .then_inc(s("a_gate"), 1)
                nc.scalar.activation(gexp[0:2, 2, :], bank[0:2, GATEB[b], 2 * E:3 * E], ACT.Exp, scale=-1.0)\
                    .then_inc(s("a_gate"), 1)

            def cw_copy(b):
                act.wait_ge(s("t_cw"), b + 1)
                nc.scalar.activation(cw_t[:, b, :], bank[0:E, GATEB[b], 0:N], ACT.Copy)\
                    .then_inc(s("a_cw"), 1)

            def silus(b, k):
                n = (E + 1) * b + k
                act.wait_ge(s("t_up"), 2 * n + 1)
                if n >= 2:
                    act.wait_ge(s("v_gate_up"), n - 1)
                nc.scalar.activation(silu[:, n % 2, :], bank[:, FFB[n % 2][0], 0:N], ACT.Silu)\
                    .then_inc(s("a_silu"), 1)

            inv_std(0)
            inv_std(1)
            x_high(0)
            x_high(1)
            qk_high(0)
            qk_high(1)
            cls_softmax(0)
            nm_copy(0)
            clskey(0)
            for h in range(NH):
                exps(0, h)
            nm_copy(1)
            cls_softmax(1)
            clskey(1)
            for h in range(NH):
                exps(1, h)
                if h == 1:
                    inv_std(2)
                if h == 4:
                    x_high(2)
                if h == 8:
                    gate_exp(0)
            for k in range(E + 1):
                silus(0, k)
                if k == 1:
                    nc.scalar.preload_act_table_set(LOG_EXP)
                    inv_std(3)
                if k == 3:
                    x_high(3)
                    cw_copy(0)
                if k == 5:
                    gate_exp(1)
            for k in range(E + 1):
                silus(1, k)
                if k == 0:
                    cw_copy(1)

        @block.tensor
        def _(pe):
            def project(dst, w, x, weights_move):
                for n, (part, half, xpart) in enumerate(PASSES):
                    lhs, rhs = (x(xpart), w(part, half)) if weights_move else (w(part, half), x(xpart))
                    ins = pe.matmul(dst, lhs, rhs, start=(n == 0), stop=(n == len(PASSES) - 1))
                return ins

            def pick(c):
                pe.wait_ge(s("v_onehot"), 2 * c + 2)
                if c == 0:
                    pe.wait_ge(s("v_pix"), 5)
                if c >= 2:
                    pe.wait_ge(s("v_picked"), c - 1)
                for n in range(6):
                    ins = pe.matmul(bank[0:ROWS0, c % 2, :], pix_part[:, n // 2, n % 2, :],
                                    onehot[:, c % 2, n % 2, :], start=(n == 0), stop=(n == 5))
                ins.then_inc(s("t_picked"), 1)

            def embed0(c):
                pe.wait_ge(s("v_picked"), c + 1)
                if c == 0:
                    pe.wait_ge(s("ld_l0"), 16)
                for n in range(2):
                    g = 2 * c + n
                    ins = pe.matmul(bank[:, 2, 0:TOK], w_l0[:, g, :],
                                    picked[0:ROWS0, c % 3, n * TOK:(n + 1) * TOK],
                                    start=(g == 0), stop=(g == GP - 1))
                ins.then_inc(s("t_emb0"), 1)

            def turn_gathered():
                pe.wait_ge(s("ld_ident"), 16)
                pe.wait_ge(s("a_split"), 2)
                for n in range(2 * B):
                    ins = pe.transpose(bank[0:96, 3, n * P:(n + 1) * P], got_by_batch[:, n // B, n % B, :],
                                       ident[:])
                ins.then_inc(s("t_got"), 1)

            def embed12():
                pe.wait_ge(s("a_got"), 1)
                pe.wait_ge(s("ld_l12"), 64)
                for n in range(2):
                    pe.matmul(bank[0:EMB, 4, 0:P], w_l1[:, n, :], got_t[:, 0:2, n * TOK1:(n + 1) * TOK1],
                              start=(n == 0), stop=(n == 1))
                for n in range(8):
                    ins = pe.matmul(bank[0:EMB, 4, P:P + B * TOK2], w_l2[:, n, :],
                                    got_t[:, 2:4, n * TOK2:(n + 1) * TOK2], start=(n == 0), stop=(n == 7))
                ins.then_inc(s("t_emb12"), 1)

            def fuse_coarse():
                pe.wait_ge(s("a_emb12"), 2)
                for b in range(B):
                    pe.matmul(bank[0:TOK1, 5, b * D:(b + 1) * D], emb1[:, b * TOK1:(b + 1) * TOK1],
                              w_fuse12[:, 0, :], start=True, stop=True)
                    ins = pe.matmul(bank[64:64 + TOK2, 5, b * D:(b + 1) * D],
                                    emb2[:, b * TOK2:(b + 1) * TOK2], w_fuse12[:, 1, :],
                                    start=True, stop=True)
                ins.then_inc(s("t_coarse"), 1)

            def fuse(b):
                if b == 0:
                    pe.wait_ge(s("a_emb0"), 1)
                    pe.wait_ge(s("a_coarse"), 1)
                    pe.wait_ge(s("ld_fuse"), 64)
                for c in range(CHUNKS):
                    dst = bank[:, 4 + b, c * D:(c + 1) * D]
                    pe.matmul(dst, emb0[:, c * P:(c + 1) * P], w_fuse0[:, b, :], start=True, stop=False)
                    ins = pe.matmul(dst, interp[:, c * P:(c + 1) * P], coarse[:, b, :],
                                    start=False, stop=True)
                ins.then_inc(s("t_h"), 1)

            def turn(i):
                pe.wait_ge(s("v_xn"), 6 * (i + 1))
                for c in range(3):
                    rows = P if c < 2 else 2
                    cols = slice(c * P, c * P + rows)
                    pe.transpose(bank[:, TURN[i][0], cols], xn[0:rows, c, 0:P], ident[0:rows, 0:rows])
                    ins = pe.transpose(bank[:, TURN[i][1], cols], xn[0:rows, c, P:], ident[0:rows, 0:rows])
                ins.then_inc(s("t_turned"), 1)

            def w_att(cols):
                return lambda part, half: (wq_lo if part else wq_hi)[:, half, cols]

            def w_ffn(cols):
                return lambda part, half: (wf_lo if part else wf_hi)[:, half, cols]

            def x_of(b, cols):
                return lambda part: xt[:, b, part, cols]

            def proj_qk(b):
                pe.wait_ge(s("a_xhi"), 2 * (b + 1))
                pe.wait_ge(s("v_xlo"), 2 * (b + 1))
                pe.wait_ge(s("p_split"), 2)
                for i in range(4):
                    if b:
                        pe.wait_ge(s("v_qk"), i + 1)
                    cols = slice(QK_AT[i], QK_AT[i] + QK_ROWS[i])
                    project(bank[0:QK_ROWS[i], QKB[i], 0:N], w_att(cols), x_of(b, slice(0, N)), False)\
                        .then_inc(s("t_qk"), 1)

            def proj_v(b):
                cols = slice(2 * D, 3 * D)
                for c in range(CHUNKS):
                    ins = project(bank[:, VB[b], c * D:(c + 1) * D], w_att(cols),
                                  x_of(b, slice(c * P, (c + 1) * P)), True)
                ins.then_inc(s("t_v"), 1)
                if b == 0:
                    pe.wait_ge(s("v_xlo"), 4)
                    project(bank[0:NH, 7, 0:D], w_att(cols),
                            lambda part: xt[:, 0, part, CLS:CLS + 1].to_broadcast([P, NH]), True)\
                        .then_inc(s("t_vcls"), 1)

            def cls_scores(b):
                pe.wait_ge(s("v_qk"), 4 * (b + 1))
                pe.wait_ge(s("v_clsblk"), 4)
                pe.wait_ge(s("v_zero"), 4)
                if b == 0:
                    pe.wait_ge(s("v_v"), 2)
                if b:
                    pe.wait_ge(s("v_max"), UNITS * B)
                for half in range(2):
                    pe.matmul(bank[0:NH, SCORE[b][0], 0:N], q_cls[:, half, :], qk[:, b, 2 + half, :],
                              start=(half == 0), stop=(half == 1))
                for half in range(2):
                    ins = pe.matmul(bank[0:NH, ACC[b], 0:TOK], k_cls[:, half, :], qk[:, b, half, 0:TOK],
                                    start=(half == 0), stop=(half == 1))
                ins.then_inc(s("t_clsscores"), 1)

            def scores_for_max(b, u):
                n = UNITS * b + u
                c, pair = divmod(u, NH // 2)
                if u == 0:
                    pe.wait_ge(s(f"stack_in{b}"), 128)
                    pe.wait_ge(s("p_stack"), 4)
                if n == 0:
                    pe.wait_ge(s("v_v"), 4)
                    pe.wait_ge(s("v_qk"), 8)
                if n == 2:
                    pe.wait_ge(s("a_cls"), 1)
                if b or n >= 3:
                    pe.wait_ge(s("v_max"), n - (1 if b else 2))
                for j in range(2):
                    h = 2 * pair + j
                    ins = pe.matmul(bank[:, MAXB[b][u % len(MAXB[b])] + j, 0:N], q_stack[0:K_STACK, b, h, c * P:(c + 1) * P],
                                    k_stack[0:K_STACK, b, h, :], start=True, stop=True)
                ins.then_inc(s("t_formax"), 1)

            def turn_maxima(b):
                pe.wait_ge(s("v_max"), UNITS * (b + 1))
                if b == 0:
                    pe.wait_ge(s("v_vcls"), 1)
                for c in range(CHUNKS):
                    ins = pe.transpose(bank[0:NH, MISC[b], c * P:(c + 1) * P], negmax[:, b, c, :], ident[:])
                ins.then_inc(s("t_nm"), 1)

            def scores(b, h):
                n = NH * b + h
                if h == 0:
                    pe.wait_ge(s(f"nm_in{b}"), 32)
                    pe.wait_ge(s("a_cls"), b + 1)
                if h >= 2:
                    pe.wait_ge(s("a_exp"), n - 1)
                for c in range(CHUNKS):
                    ins = pe.matmul(bank[:, SCORE[b][h % 2], c * TOK:(c + 1) * TOK],
                                    k_stack[0:K_STACK, b, h, c * P:(c + 1) * P],
                                    q_stack[0:K_STACK, b, h, 0:TOK], start=True, stop=True)
                ins.then_inc(s("t_scores"), 1)

            def weigh(b, h):
                n = NH * b + h
                g, j = divmod(h, 4)
                if j == 0:
                    pe.wait_ge(s("a_clskey"), b + 1)
                    if b == 0 and g == 0:
                        pe.wait_ge(s("v_vcls"), 3)
                    if g:
                        pe.wait_ge(s("v_attn_t"), 3 * b + g)
                    pe.matmul(bank[:, ACC[b], 0:TOK],
                              v_block[:, 4 * g:4 * g + 4, :].rearrange("p j m -> p (j m)"),
                              clskey_probs[:, b, :], start=True, stop=False, skip_group_check=True)
                pe.wait_ge(s("a_exp"), n + 1)
                for c in range(CHUNKS):
                    ins = pe.matmul(bank[32 * j:32 * j + HD + 1, ACC[b], 0:TOK], vals[:, b, c, h, :],
                                    probs[:, h % PT_RING, c, :], start=False, stop=(c == CHUNKS - 1),
                                    skip_group_check=True)
                ins.then_inc(s("t_pv"), 1)

            def cls_turn(b):
                pe.wait_ge(s("a_nm"), b + 1)
                pe.wait_ge(s("a_cls"), b + 1)
                for c in range(CHUNKS):
                    ins = pe.transpose(bank[:, MISC[b], c * NH:(c + 1) * NH], cls_probs[:, b, c * P:(c + 1) * P],
                                       ident[0:NH, 0:NH])
                ins.then_inc(s("t_clsprobs"), 1)

            def cls_weigh(b):
                pe.wait_ge(s("v_clsprobs"), b + 1)
                for c in range(CHUNKS):
                    ins = pe.matmul(bank[0:NH, MISC[b], 0:D], cls_probs_t[:, c * NH:(c + 1) * NH],
                                    vals[:, b, c, :, 0:HD], start=(c == 0), stop=(c == CHUNKS - 1))
                ins.then_inc(s("t_clssum"), 1)

            def cls_row(b):
                pe.wait_ge(s("v_clssum"), 2 * (b + 1))
                pe.wait_ge(s("p_const"), 3)
                pe.matmul(bank[0:1, MISC[b], 0:D], ones[:], cls_sumv[:, 1, :], start=True, stop=True)\
                    .then_inc(s("t_clsrow"), 1)

            def turn_attn(b):
                pe.wait_ge(s("v_attn_t"), 3 * (b + 1))
                pe.wait_ge(s("v_clsrow"), b + 1)
                for c, into in enumerate((MISC[b], ACC[b])):
                    for g in range(3):
                        ins = pe.transpose(bank[:, into, g * P:(g + 1) * P], attn_t[:, g, c * P:(c + 1) * P],
                                           ident[:])
                    ins.then_inc(s("t_attn"), 1)

            def gate(b):
                pe.wait_ge(s("a_xhi"), 2 * (B + b + 1))
                pe.wait_ge(s("v_xlo"), 2 * (B + b + 1))
                pe.wait_ge(s("p_split"), 10)
                cols = slice(GATE, GATE + E)
                for c in range(3):
                    rows = P if c < 2 else 2
                    ins = project(bank[0:rows, GATEB[b], c * E:(c + 1) * E], w_ffn(cols),
                                  x_of(b, slice(c * P, c * P + rows)), True)
                ins.then_inc(s("t_gate"), 1)

            def turn_cw(b):
                pe.wait_ge(s("v_gate"), b + 1)
                pe.wait_ge(s("a_gate"), 2 * (b + 1))
                for c in range(3):
                    rows = P if c < 2 else 2
                    ins = pe.transpose(bank[0:E, GATEB[b], c * P:c * P + rows], cw[0:rows, c, :],
                                       ident[0:rows, 0:rows])
                ins.then_inc(s("t_cw"), 1)

            def up(b, k):
                n = (E + 1) * b + k
                if n == 0:
                    pe.wait_ge(s("a_exp"), B * NH)
                if n >= 2:
                    pe.wait_ge(s("v_gate_up"), n - 1)
                if k == 0:
                    pe.wait_ge(s("v_xlo"), 2 * (B + b + 1))
                for j in range(2):
                    cols = slice((2 * k + j) * INTER, (2 * k + j + 1) * INTER)
                    project(bank[:, FFB[n % 2][j], 0:N], w_ffn(cols), x_of(b, slice(0, N)), False)\
                        .then_inc(s("t_up"), 1)

            def down(b, k):
                if k == 0:
                    pe.wait_ge(s("ld_down"), 16)
                    pe.wait_ge(s("v_gate_up"), (E + 1) * b + 1)
                    pe.wait_ge(s("v_xlo"), 2 * (B + b + 1))
                    if b:
                        pe.wait_ge(s("a_cw"), 1)
                else:
                    pe.wait_ge(s("p_shared"), E * b + k)
                for c in range(CHUNKS):
                    ins = pe.matmul(bank[:, YB[b], c * D:(c + 1) * D], hidden[:, b, k, c * P:(c + 1) * P],
                                    w_down[:, k, :], start=(k == 0 and c == 0), stop=(k == E),
                                    skip_group_check=True)
                if k == E:
                    ins.then_inc(s("t_down"), 1)
                if b == B - 1:
                    ins = pe.matmul(bank[0:B, YCLS, 0:D], hidden[:, :, k, CLS], w_down[:, k, :],
                                    start=(k == 0), stop=False, skip_group_check=True)
                    if k == E:
                        for r in range(B):
                            ins = pe.matmul(bank[0:B, YCLS, 0:D], cst[0:1, 4 + B * r:4 + B * (r + 1)],
                                            hres[0:1, r, 2, :],
                                            start=False, stop=(r == B - 1), skip_group_check=True)
                        ins.then_inc(s("t_downcls"), 1)

            for c in range(STEPS0):
                pick(c)
                if c >= 1:
                    embed0(c - 1)
                if c == 5:
                    turn_gathered()
                if c == 6:
                    embed12()
                if c == 7:
                    fuse_coarse()
            embed0(STEPS0 - 1)
            fuse(0)
            fuse(1)
            turn(0)
            turn(1)
            proj_qk(0)
            proj_v(0)
            proj_qk(1)
            proj_v(1)
            cls_scores(0)
            for u in range(UNITS):
                scores_for_max(0, u)
            scores_for_max(1, 0)
            turn_maxima(0)
            for u in range(1, 4):
                scores_for_max(1, u)
            for h in range(NH):
                scores(0, h)
                if h >= 1:
                    weigh(0, h - 1)
                if h + 4 < UNITS:
                    scores_for_max(1, h + 4)
                if h == 3:
                    cls_turn(0)
                if h == 6:
                    cls_weigh(0)
                if h == 10:
                    cls_row(0)
            weigh(0, NH - 1)
            turn_maxima(1)
            cls_scores(1)
            turn_attn(0)
            for h in range(NH):
                scores(1, h)
                if h >= 1:
                    weigh(1, h - 1)
                if h == 3:
                    cls_turn(1)
                    turn(2)
                if h == 6:
                    cls_weigh(1)
                if h == 7:
                    gate(0)
                if h == 9:
                    cls_row(1)
            weigh(1, NH - 1)
            for n in range(B * (E + 1)):
                up(*divmod(n, E + 1))
                if n == 0:
                    turn_attn(1)
                if n == 3:
                    turn_cw(0)
                    turn(3)
                if n == 6:
                    gate(1)
                if n == 9:
                    turn_cw(1)
                if n >= LAG:
                    down(*divmod(n - LAG, E + 1))
            for n in range(B * (E + 1) - LAG, B * (E + 1)):
                down(*divmod(n, E + 1))

        @block.vector
        def _(dve):
            v = nc.vector
            for n in range(4):
                v.memset(qk[D2:P, n // 2, 2 * (n % 2) + 1, :], 0.0).then_inc(s("v_zero"), 1)
            dve.wait_ge(s("ld_gidx"), 16)
            for cols, last in ((slice(0, 8), TOK1 * GP - 1), (slice(8, 10), TOK2 * GP - 1)):
                v.tensor_scalar(gidx[:, cols], gidx_raw[:, cols], last, None, ALU.bitwise_and)\
                    .then_inc(s("v_gidx"), 1)
            dve.wait_ge(s("ld_pix"), 16)
            v.tensor_copy(pix_part[:, 0], pix[:]).then_inc(s("v_pix"), 1)
            dve.wait_ge(s("v_pix"), 1)
            v.tensor_tensor(pix_rest[:, 0], pix[:], pix_part[:, 0], ALU.subtract).then_inc(s("v_pix"), 1)
            dve.wait_ge(s("v_pix"), 2)
            v.tensor_copy(pix_part[:, 1], pix_rest[:, 0]).then_inc(s("v_pix"), 1)
            dve.wait_ge(s("v_pix"), 3)
            v.tensor_tensor(pix_rest[:, 1], pix_rest[:, 0], pix_part[:, 1], ALU.subtract)\
                .then_inc(s("v_pix"), 1)
            dve.wait_ge(s("v_pix"), 4)
            v.tensor_copy(pix_part[:, 2], pix_rest[:, 1]).then_inc(s("v_pix"), 1)

            def one_hot(c):
                cols = slice(c * COLS0, (c + 1) * COLS0)
                if c % 2 == 0:
                    dve.wait_ge(s(f"ld_idx{c // 2}"), 16)
                if c >= 2:
                    dve.wait_ge(s("v_onehot"), 2 * c - 2)
                    dve.wait_ge(s("v_picked"), c - 1)
                v.tensor_scalar(hi_idx[:, c % 2, :], idx_all[:, cols], NPIX - 1, 4, ALU.bitwise_and,
                                ALU.logical_shift_right).then_inc(s("v_parts"), 1)
                v.tensor_scalar(lo_idx[:, c % 2, :], idx_all[:, cols], LOW - 1, None, ALU.bitwise_and)\
                    .then_inc(s("v_parts"), 1)
                dve.wait_ge(s("v_parts"), 2 * c + 1)
                if c == 0:
                    dve.wait_ge(s("ld_cst"), 16)
                if c >= 2:
                    dve.wait_ge(s("t_picked"), c - 1)
                for half in range(2):
                    v.tensor_scalar(onehot[:, c % 2, half, :], hi_idx[:, c % 2, :], cst[:, half:half + 1],
                                    None, ALU.is_equal).then_inc(s("v_onehot"), 1)

            def choose(c):
                dve.wait_ge(s("t_picked"), c + 1)
                dve.wait_ge(s("v_parts"), 2 * c + 2)
                if c >= 3:
                    dve.wait_ge(s("t_emb0"), c - 2)
                v.scalar_tensor_tensor(out=picked[0:ROWS0, c % 3, :], in0=lo_idx[0:ROWS0, c % 2, :],
                                       scalar=cst[0:ROWS0, 2:3], in1=bank[0:ROWS0, c % 2, :],
                                       op0=ALU.is_equal, op1=ALU.mult).then_inc(s("v_picked"), 1)

            for c in range(STEPS0):
                one_hot(c)
                if c >= 1:
                    choose(c - 1)
            choose(STEPS0 - 1)

            def take_h(b):
                dve.wait_ge(s("t_h"), b + 1)
                v.tensor_copy(hres[:, b, 0:2, :].rearrange("p c d -> p (c d)"), bank[:, 4 + b, 0:2 * D])\
                    .then_inc(s("v_h"), 1)

            def mean_var(i):
                b = i % B
                if i < B:
                    dve.wait_ge(s("v_h"), b + 1)
                    dve.wait_ge(s("ld_cls"), 32)
                else:
                    dve.wait_ge(s("v_hattn"), 2 * (b + 1))
                    dve.wait_ge(s("v_clsrow"), b + 1)
                if i:
                    dve.wait_ge(s("v_xn"), 6 * i)
                for c in range(3):
                    v.bn_stats(stats[:, c, :], hres[:, b, c, :]).then_inc(s("v_stats"), 1)
                for c in range(3):
                    dve.wait_ge(s("v_stats"), 3 * i + c + 1)
                    v.bn_aggr(meanvar[:, c, :], stats[:, c, :]).then_inc(s("v_meanvar"), 1)

            def normalise(i):
                b = i % B
                dve.wait_ge(s("a_rstd"), 2 * (i + 1))
                if i:
                    dve.wait_ge(s("t_turned"), i)
                for c in range(3):
                    v.tensor_scalar(xn[:, c, 0:P], hres[:, b, c, 0:P], meanvar[:, c, 0:1], rstd[:, c:c + 1],
                                    ALU.subtract, ALU.mult).then_inc(s("v_xn"), 1)
                    v.tensor_scalar(xn[:, c, P:].rearrange("p (t f) -> p t f", t=2),
                                    hres[:, b, c, P:].unsqueeze(1).to_broadcast([P, 2, D2]),
                                    meanvar[:, c, 0:1], rstd[:, c:c + 1],
                                    ALU.subtract, ALU.mult).then_inc(s("v_xn"), 1)

            def x_low(i):
                b = i % B
                dve.wait_ge(s("a_xhi"), 2 * (i + 1))
                v.tensor_tensor(xt[:, b, 1, :], bank[:, TURN[i][0], 0:N], xt[:, b, 0, :].bitcast(F32),
                                ALU.subtract).then_inc(s("v_xlo"), 1)
                v.tensor_tensor(xt[D2:P, b, 2, :], bank[D2:P, TURN[i][1], 0:N],
                                xt[D2:P, b, 2, :].bitcast(F32), ALU.subtract).then_inc(s("v_xlo"), 1)

            def take_qk(b):
                if b == 0:
                    dve.wait_ge(s("ld_att"), 64)
                for i in range(4):
                    rows = QK_ROWS[i]
                    if i >= 2:
                        qk_low(b, i - 2)
                    dve.wait_ge(s("t_qk"), 4 * b + i + 1)
                    v.tensor_scalar(qk[0:rows, b, i, :], bank[0:rows, QKB[i], 0:N], bias_qk[0:rows, i:i + 1],
                                    SCALE if i < 2 else 1.0, ALU.add, ALU.mult).then_inc(s("v_qk"), 1)

            def qk_low(b, i):
                rows = QK_ROWS[i]
                dve.wait_ge(s("a_qkhi"), 4 * b + i + 1)
                v.tensor_tensor(qk_part[0:rows, i, 1, :], qk[0:rows, b, i, :],
                                qk_part[0:rows, i, 0, :].bitcast(F32), ALU.subtract)\
                    .then_inc(s("v_qklo"), 1)

            def take_v(b):
                dve.wait_ge(s("t_v"), b + 1)
                dve.wait_ge(s("p_const"), 1)
                for c in range(CHUNKS):
                    v.tensor_tensor(vals[:, b, c, :, 0:HD],
                                    bank[:, VB[b], c * D:(c + 1) * D].rearrange("p (h d) -> p h d", h=NH),
                                    bias_v[:].rearrange("p (h d) -> p h d", h=NH), ALU.add)\
                        .then_inc(s("v_v"), 1)

            def cls_blocks():
                dve.wait_ge(s("v_qk"), 4)
                dve.wait_ge(s("v_zero"), 4)
                for dst, first in ((q_cls, 0), (k_cls, 2)):
                    for half in range(2):
                        v.tensor_scalar(dst[:, half, :], headmask[:, half, :],
                                        qk[:, 0, first + half, CLS:CLS + 1], None, ALU.mult)\
                            .then_inc(s("v_clsblk"), 1)
                dve.wait_ge(s("t_vcls"), 1)
                v.tensor_tensor(v_cls[:], bank[0:NH, 7, 0:D], bias_v[0:NH, :], ALU.add)\
                    .then_inc(s("v_vcls"), 1)
                dve.wait_ge(s("v_vcls"), 1)
                dve.wait_ge(s("p_const"), 2)
                v.tensor_tensor(v_block[0:NH, :, 0:HD], v_cls[:].rearrange("p (h d) -> p h d", h=NH),
                                blockmask[:].rearrange("p (h d) -> p h d", h=NH), ALU.mult)\
                    .then_inc(s("v_vcls"), 1)
                dve.wait_ge(s("ld_ident"), 16)
                v.tensor_copy(v_block[0:NH, :, HD], ident[0:NH, 0:NH]).then_inc(s("v_vcls"), 1)

            def cls_max(b):
                dve.wait_ge(s("t_clsscores"), b + 1)
                v.tensor_reduce(cls_neg[:, b:b + 1], bank[0:NH, SCORE[b][0], 0:TOK + 1], AX.X, ALU.max,
                                negate=True).then_inc(s("v_clsmax"), 1)

            def maxima(b, u):
                n = UNITS * b + u
                c, pair = divmod(u, NH // 2)
                dve.wait_ge(s("t_formax"), n + 1)
                two = MAXB[b][u % len(MAXB[b])]
                v.tensor_reduce(negmax[:, b, c, 2 * pair:2 * pair + 2], bank[:, two:two + 2, 0:TOK + 1],
                                AX.X, ALU.max, negate=True).then_inc(s("v_max"), 1)

            def nm_parts(b):
                dve.wait_ge(s("t_nm"), b + 1)
                dve.wait_ge(s("qk_out1"), 64)
                src = bank[0:NH, MISC[b], 0:TOK]
                v.tensor_copy(nm_part[:, b, 0, :], src).then_inc(s("v_nm"), 1)
                dve.wait_ge(s("v_nm"), 2 * b + 1)
                v.tensor_tensor(nm_part[:, b, 1, :], src, nm_part[:, b, 0, :].bitcast(F32), ALU.subtract)\
                    .then_inc(s("v_nm"), 1)

            def clskey_arg(b):
                dve.wait_ge(s("a_nm"), b + 1)
                dve.wait_ge(s("t_clsscores"), b + 1)
                if b:
                    dve.wait_ge(s("a_clskey"), b)
                v.tensor_tensor(clskey_in[:], bank[0:NH, ACC[b], 0:TOK], nm_row[:, b, :], ALU.add)\
                    .then_inc(s("v_clskey"), 1)

            def take_attn(b, g):
                dve.wait_ge(s("t_pv"), NH * b + 4 * (g + 1))
                if b:
                    dve.wait_ge(s("t_attn"), 2 * b)
                v.tensor_copy(attn_t[:, g, :], bank[:, ACC[b], 0:TOK]).then_inc(s("v_attn_t"), 1)

            def cls_probs_copy(b):
                dve.wait_ge(s("t_clsprobs"), b + 1)
                v.tensor_copy(cls_probs_t[:], bank[:, MISC[b], 0:CHUNKS * NH]).then_inc(s("v_clsprobs"), 1)
                v.reciprocal(cls_rsum[:, b:b + 1], cls_sum[:, b:b + 1]).then_inc(s("v_clsrsum"), 1)

            def cls_sums(b):
                dve.wait_ge(s("t_clssum"), b + 1)
                v.scalar_tensor_tensor(out=cls_sumv[:, 0, :], in0=v_cls[:], scalar=cls_probs[:, b, CLS:CLS + 1],
                                       in1=bank[0:NH, MISC[b], 0:D], op0=ALU.mult, op1=ALU.add)\
                    .then_inc(s("v_clssum"), 1)
                dve.wait_ge(s("v_clssum"), 2 * b + 1)
                dve.wait_ge(s("v_clsrsum"), b + 1)
                v.scalar_tensor_tensor(out=cls_sumv[:, 1, :], in0=cls_sumv[:, 0, :], scalar=cls_rsum[:, b:b + 1],
                                       in1=blockmask[:], op0=ALU.mult, op1=ALU.mult)\
                    .then_inc(s("v_clssum"), 1)

            def cls_add(b):
                dve.wait_ge(s("t_clsrow"), b + 1)
                row = hres[0:1, b, 2, :]
                v.tensor_tensor(row, bank[0:1, MISC[b], 0:D], row, ALU.add).then_inc(s("v_clsrow"), 1)

            def add_attn(b):
                for c, into in enumerate((MISC[b], ACC[b])):
                    n = 2 * b + c
                    dve.wait_ge(s("t_attn"), n + 1)
                    src = bank[:, into, 0:3 * P].rearrange("p (h m) -> p h m", h=NH)
                    v.reciprocal(rsum[:, c, :], src[:, :, HD]).then_inc(s("v_rsum"), 1)
                    dve.wait_ge(s("v_rsum"), n + 1)
                    v.tensor_tensor(attn[:, c, :].rearrange("p (h d) -> p h d", h=NH), src[:, :, 0:HD],
                                    rsum[:, c, :].unsqueeze(2).to_broadcast([P, NH, HD]), ALU.mult)\
                        .then_inc(s("v_attn"), 1)
                for c in range(CHUNKS):
                    dve.wait_ge(s("v_attn"), 2 * b + c + 1)
                    v.tensor_tensor(hres[:, b, c, :], hres[:, b, c, :], attn[:, c, :], ALU.add)\
                        .then_inc(s("v_hattn"), 1)

            chain = [0]

            def link(ins):
                chain[0] += 1
                ins.then_inc(s("v_chain"), 1)
                dve.wait_ge(s("v_chain"), chain[0])

            def beaten_by(vals_, n, at):
                ge = gge[:, :, 0:n * n].rearrange("p c (i j) -> p c i j", i=n)
                gt = ggt[:, :, 0:n * n].rearrange("p c (i j) -> p c i j", i=n)
                other = vals_.unsqueeze(2).to_broadcast([P, 3, n, n])
                own = vals_.unsqueeze(3).to_broadcast([P, 3, n, n])
                lower, upper = (order[:, k, at:at + n * n].unsqueeze(1).to_broadcast([P, 3, n * n])
                                for k in range(2))
                link(v.tensor_tensor(ge, other, own, ALU.is_ge))
                link(v.tensor_tensor(gt, other, own, ALU.is_gt))
                link(v.tensor_tensor(gge[:, :, 0:n * n], gge[:, :, 0:n * n], lower, ALU.mult))
                link(v.tensor_tensor(ggt[:, :, 0:n * n], ggt[:, :, 0:n * n], upper, ALU.mult))
                link(v.tensor_tensor(gge[:, :, 0:n * n], gge[:, :, 0:n * n], ggt[:, :, 0:n * n], ALU.add))
                link(v.tensor_reduce(grank[:, :, 0:n], ge, AX.X, ALU.add))

            by_group = gsb[:].rearrange("p c (g k) -> p c g k", k=2)
            masked = gmsk[:].rearrange("p c (g k) -> p c g k", k=2)
            wide = [P, 3, GROUPS, 2]

            def route_scores(b):
                dve.wait_ge(s("a_gate"), 2 * (b + 1))
                dve.wait_ge(s("ld_gate"), 32)
                link(v.tensor_scalar(gden[:], gexp[:], 1.0, None, ALU.add))
                link(v.reciprocal(gsc[:], gden[:]))
                link(v.tensor_tensor(gsb[:], gsc[:], gbias[:], ALU.add))
                link(v.tensor_tensor(ggrp[:], by_group[:, :, :, 0], by_group[:, :, :, 1], ALU.add))

            def route_groups(b):
                beaten_by(ggrp[:], GROUPS, 0)
                link(v.tensor_scalar(gsel[:], grank[:, :, 0:GROUPS], 2.0, None, ALU.is_lt))
                link(v.tensor_scalar(gpen[:], gsel[:], -1.0, FAR, ALU.add, ALU.mult))
                link(v.tensor_tensor(masked, by_group, gsel[:].unsqueeze(3).to_broadcast(wide), ALU.mult))
                link(v.tensor_tensor(masked, masked, gpen[:].unsqueeze(3).to_broadcast(wide), ALU.add))

            def route_experts(b):
                beaten_by(gmsk[:], E, GROUPS * GROUPS)
                link(v.tensor_scalar(gmsk[:], grank[:], 2.0, None, ALU.is_lt))
                link(v.tensor_tensor(gmsk[:], gmsk[:], gsc[:], ALU.mult))
                link(v.tensor_reduce(gsum[:], gmsk[:], AX.X, ALU.add))
                link(v.tensor_scalar(gsum[:], gsum[:], 1e-6, None, ALU.add))
                link(v.reciprocal(gsum[:], gsum[:]))
                if b:
                    dve.wait_ge(s("t_cw"), b)
                v.tensor_tensor(cw[:], gmsk[:], gsum[:].unsqueeze(2).to_broadcast([P, 3, E]), ALU.mult)\
                    .then_inc(s("v_gate"), 1)

            def gate_up(b, k):
                n = (E + 1) * b + k
                dve.wait_ge(s("a_silu"), n + 1)
                dve.wait_ge(s("t_up"), 2 * n + 2)
                v.tensor_tensor(hidden[:, b, k, :], bank[:, FFB[n % 2][1], 0:N], silu[:, n % 2, :], ALU.mult)\
                    .then_inc(s("v_gate_up"), 1)

            def finish(b):
                dve.wait_ge(s("t_down"), b + 1)
                v.tensor_tensor(hres[:, b, 0:2, :].rearrange("p c d -> p (c d)"), bank[:, YB[b], 0:CHUNKS * D],
                                hres[:, b, 0:2, :].rearrange("p c d -> p (c d)"), ALU.add)\
                    .then_inc(s("v_out"), 1)

            take_h(0)
            mean_var(0)
            take_h(1)
            normalise(0)
            mean_var(1)
            normalise(1)
            x_low(0)
            x_low(1)
            take_qk(0)
            qk_low(0, 2)
            qk_low(0, 3)
            take_v(0)
            take_qk(1)
            qk_low(1, 2)
            qk_low(1, 3)
            cls_blocks()
            take_v(1)
            cls_max(0)
            for u in range(UNITS):
                maxima(0, u)
            nm_parts(0)
            clskey_arg(0)
            for u in range(UNITS):
                maxima(1, u)
                if u == 7:
                    take_attn(0, 0)
                if u == 8:
                    cls_probs_copy(0)
            cls_sums(0)
            take_attn(0, 1)
            cls_add(0)
            take_attn(0, 2)
            nm_parts(1)
            cls_max(1)
            clskey_arg(1)
            add_attn(0)
            mean_var(2)
            normalise(2)
            cls_probs_copy(1)
            take_attn(1, 0)
            x_low(2)
            cls_sums(1)
            take_attn(1, 1)
            route_scores(0)
            cls_add(1)
            take_attn(1, 2)
            route_groups(0)
            add_attn(1)
            gate_up(0, 0)
            mean_var(3)
            gate_up(0, 1)
            normalise(3)
            gate_up(0, 2)
            route_experts(0)
            gate_up(0, 3)
            x_low(3)
            gate_up(0, 4)
            gate_up(0, 5)
            route_scores(1)
            gate_up(0, 6)
            route_groups(1)
            gate_up(0, 7)
            route_experts(1)
            gate_up(0, 8)
            for k in range(E + 1):
                gate_up(1, k)
                if k == LAG:
                    finish(0)
            finish(1)
            dve.wait_ge(s("t_downcls"), 1)
            v.tensor_copy(out_cls[:], bank[0:B, YCLS, 0:D]).then_inc(s("v_outcls"), 1)


def kernel(**x):
    import numpy as np
    import concourse.bacc as bacc
    from concourse import mybir as _mybir
    from concourse.bass_utils import run_bass_kernel_spmd

    a = {k: np.asarray(v) for k, v in x.items()}
    f32 = np.float32

    def rows_twice(w):
        return np.stack([w[:P], np.concatenate([w[P:], w[P:]])])

    def pad_rows(w):
        return np.concatenate([w, np.zeros((P - w.shape[0],) + w.shape[1:], w.dtype)])

    img = a["x"]

    def patches(p):
        h = img.shape[2] // p
        q = img.reshape(B, CH, h, p, h, p).transpose(2, 4, 0, 3, 5, 1)
        return q.reshape(h * h, B * p * p * CH)

    t = {}
    t["pix"] = patches(1).reshape(2, P, LOW, B * CH).transpose(1, 0, 3, 2).reshape(P, 2, ROWS0)
    t["pix1"] = patches(2)
    t["pix2"] = patches(4)
    t["idx0"] = a["L0_tok_idx0"].reshape(TOK, GP).T.reshape(-1)
    idx1 = a["L0_tok_idx1"].reshape(TOK1, 2, 8).transpose(1, 0, 2).reshape(P, 8)
    idx2 = a["L0_tok_idx2"].reshape(TOK2, 8, 2).transpose(1, 0, 2).reshape(P, 2)
    t["gidx"] = np.concatenate([idx1, idx2], axis=1)
    w0 = a["L0_tok_W0"].reshape(EMB, GP, CH).transpose(2, 1, 0)
    big = np.zeros((B, CH, LOW, GP, B, EMB), f32)
    for b in range(B):
        big[b, :, :, :, b, :] = w0[:, None]
    t["w_l0"] = big.reshape(ROWS0, GP, B * EMB)
    t["w_l1"] = a["L0_tok_W1"].T.reshape(2, 96, EMB).transpose(1, 0, 2)
    t["w_l2"] = a["L0_tok_W2"].T.reshape(8, 96, EMB).transpose(1, 0, 2)
    b0 = a["L0_tok_b0"]
    t["bias_l"] = np.stack([np.concatenate([b0, b0]), pad_rows(a["L0_tok_b1"]), pad_rows(a["L0_tok_b2"])], axis=1)
    wf = a["L0_tok_Wf"].T.reshape(3, EMB, D)
    zero = np.zeros((EMB, D), f32)
    t["w_fuse0"] = np.stack([np.concatenate([wf[0], zero]), np.concatenate([zero, wf[0]])], axis=1)
    t["w_fuse12"] = wf[1:].transpose(1, 0, 2)
    t["bf"] = a["L0_tok_bf"][None]
    interp = np.zeros((P, TOK), f32)
    for at, n in ((0, TOK1), (64, TOK2)):
        pos = np.clip((np.arange(TOK) + 0.5) * (n / TOK) - 0.5, 0.0, n - 1)
        lo = np.floor(pos).astype(int)
        hi = np.minimum(lo + 1, n - 1)
        for i in range(TOK):
            interp[at + lo[i], i] += 1.0 - (pos[i] - lo[i])
            interp[at + hi[i], i] += pos[i] - lo[i]
    interp[96] = 1.0
    t["interp"] = interp
    t["cls"] = a["cls_tok"].reshape(1, D)
    wqkv = np.concatenate([a["L0_attn_Wq"], a["L0_attn_Wk"], a["L0_attn_Wv"]]).T
    t["w_qkv"] = rows_twice(wqkv)
    bq, bk = a["L0_attn_bq"], a["L0_attn_bk"]
    t["bqk"] = np.stack([bq[:P], pad_rows(bq[P:]), bk[:P], pad_rows(bk[P:])], axis=1)
    t["bv"] = a["L0_attn_bv"]
    ups = np.stack([np.concatenate([a["L0_ffn_sw1"][None], a["L0_ffn_w1"]]),
                    np.concatenate([a["L0_ffn_sw3"][None], a["L0_ffn_w3"]])], axis=1)
    wff = np.concatenate([ups.reshape(GATE, D), a["L0_ffn_gate_weight"]]).T
    t["w_ff"] = rows_twice(wff).reshape(2, P, WFF // RAW, RAW).transpose(2, 1, 0, 3)
    t["w_down"] = np.concatenate([a["L0_ffn_sw2"][None], a["L0_ffn_w2"]]).transpose(2, 0, 1)
    t["gbias"] = np.tile(a["L0_ffn_gate_bias"], 3)
    head = (np.arange(2 * P)[:, None] // HD == np.arange(NH)[None]).astype(f32)
    t["headmask"] = head.reshape(2, P, NH).transpose(1, 0, 2)
    t["blockmask"] = head[:D].T
    t["ident"] = np.eye(P, dtype=f32)
    lower = [np.tril(np.ones((n, n), f32), -1).reshape(-1) for n in (GROUPS, E)]
    upper = [np.triu(np.ones((n, n), f32), 1).reshape(-1) for n in (GROUPS, E)]
    t["order"] = np.stack([np.concatenate(m) for m in (lower, upper)]).reshape(-1)
    p = np.arange(P)
    cst = np.zeros((P, 8), f32)
    cst[:, 0], cst[:, 1], cst[:, 2], cst[:, 3] = p, p + P, p % LOW, EPS
    cst[0, 4], cst[0, 7] = 1.0, 1.0
    t["cst"] = cst

    nc = bacc.Bacc("TRN2", target_bir_lowering=False, num_devices=1)
    t = {k: np.ascontiguousarray(v) for k, v in t.items()}
    aps = {k: nc.dram_tensor(f"in_{k}", v.shape, _mybir.dt.from_np(v.dtype), kind="ExternalInput").ap()
           for k, v in t.items()}
    shape = (B, 1 + TOK, D)
    out = nc.dram_tensor("out_tokens", shape, _mybir.dt.float32, kind="ExternalOutput").ap()
    build(nc, aps, out)
    return run_bass_kernel_spmd(nc, [{f"in_{k}": v for k, v in t.items()}], core_ids=[0]).results[0]["out_tokens"]
```

```python
from contextlib import ExitStack

import concourse.bass as bass
from concourse import mybir

F32 = mybir.dt.float32
F32R = mybir.dt.float32r
BF16 = mybir.dt.bfloat16
I32 = mybir.dt.int32
ALU = mybir.AluOpType
ACT = mybir.ActivationFunctionType
AX = mybir.AxisListType

P = 128
B = 2
CH = 3
D = 192
D2 = D - P
NH = 12
HD = D // NH
E = 8
INTER = 128
GROUPS = 4
GP = 16
TOK = 256
CLS = TOK
N = TOK + 2
CHUNKS = TOK // P
NPIX = 4096
LOW = 16
ROWS0 = B * CH * LOW
COLS0 = 512
STEPS0 = NPIX // COLS0
EMB = 64
TOK1, TOK2 = 64, 16
F1, F2 = 12, 48
EPS = 1e-5
SCALE = HD ** -0.5
FAR = 1e30
GATE = 2 * INTER * (E + 1)
WFF = GATE + E
RAW = WFF // 4
K_STACK = 128
MAXROW = 3 * HD
PT_RING = 4
UNITS = CHUNKS * NH // 2
LAG = 6
AHEAD = 6
LOG_EXP = "natural_log_exp_and_others"


def build(nc, t, out):
    ctx = ExitStack()
    with ctx:
        def sb(name, shape, dt=F32):
            return ctx.enter_context(nc.sbuf_tensor(name, shape, dt))

        class Signals:

            def __init__(self):
                self.made = {}

            def __call__(self, name):
                if name not in self.made:
                    self.made[name] = ctx.enter_context(nc.semaphore(name))
                return self.made[name]

        s = Signals()

        arena = sb("arena", [P, 10240])
        idx_all = arena[:, 0:NPIX].bitcast(I32)
        picked = arena[:, 4096:5632].rearrange("p (r n) -> p r n", r=3)
        hi_idx = arena[:, 5632:6656].bitcast(I32).rearrange("p (r n) -> p r n", r=2)
        lo_idx = arena[:, 6656:7680].bitcast(I32).rearrange("p (r n) -> p r n", r=2)
        apart = arena[:, 7680:8192]
        w_l0 = arena[0:ROWS0, 8192:10240].rearrange("p (g m) -> p g m", g=GP)
        probs = arena[:, 0:2048].rearrange("p (r k n) -> p r k n", r=PT_RING, k=CHUNKS)
        w_down = arena[:, 6692:8420].rearrange("p (e d) -> p e d", e=E + 1)
        hidden = arena[:, 2048:6692].rearrange("p (b e n) -> p b e n", b=B, e=E + 1)

        arena2 = sb("arena2", [P, 4900])

        class Carve:

            def __init__(self):
                self.at = 0

            def __call__(self, shape, dt=F32):
                n = 1
                for d in shape[1:]:
                    n *= d
                words = n
                tile = arena2[0:shape[0], self.at:self.at + words]
                self.at += words
                assert self.at <= 4900
                if dt != F32:
                    tile = tile.bitcast(dt)
                names = [f"a{i}" for i in range(len(shape) - 1)]
                sizes = dict(zip(names, shape[1:]))
                return tile.rearrange(f"p ({' '.join(names)}) -> p {' '.join(names)}", **sizes) \
                    if len(names) > 1 else tile

        early, late = Carve(), Carve()
        pix = early([P, 2, ROWS0])
        cst = sb("cst", [P, 8])
        gidx_raw = sb("gidx_raw", [P, 10], I32)
        gidx = sb("gidx", [P, 10], I32)
        got1 = early([P, 8, B * F1])
        got2 = early([P, 2, B * F2])
        got_by_batch = early([P, 2, B, 96])
        got_t = early([96, 4, P])
        w_l1 = early([96, 2, EMB])
        w_l2 = early([96, 8, EMB])
        emb1 = early([EMB, P])
        emb2 = early([EMB, B * TOK2])
        bias_l = sb("bias_l", [P, 3])
        emb0 = early([P, TOK])
        w_fuse0 = early([P, B, D])
        w_fuse12 = early([EMB, 2, D])
        interp = early([P, TOK])
        coarse = early([P, B, D])
        ident = sb("ident", [P, P])
        hres = sb("hres", [P, B, 3, D])
        logvar = sb("logvar", [P, 3])
        stats = sb("stats", [P, 3, 6])
        meanvar = sb("meanvar", [P, 3, 2])
        rstd = sb("rstd", [P, 3])
        xn = sb("xn", [P, 3, D + D2])
        xt = sb("xt", [P, B, 3, N], F32R)
        w_raw = sb("w_raw", [P, 2, RAW])
        wq_hi = sb("wq_hi", [P, 2, 3 * D], F32R)
        wq_lo = sb("wq_lo", [P, 2, 3 * D], F32R)
        wf_hi = sb("wf_hi", [P, 2, WFF], F32R)
        wf_lo = sb("wf_lo", [P, 2, WFF], F32R)
        bias_qk = sb("bias_qk", [P, 4])
        bias_v = sb("bias_v", [P, D])
        qk = sb("qk", [P, B, 4, N])
        qk_part = sb("qk_part", [P, 4, 2, N], F32R)
        q_stack = sb("q_stack", [P, B, NH, N], F32R)
        k_stack = sb("k_stack", [P, B, NH, N], F32R)
        onehot = q_stack[:, 0, :, :].rearrange("p h n -> p (h n)")[:, 0:4 * COLS0]\
            .rearrange("p (r k n) -> p r k n", r=2, k=2)
        pix_part = k_stack[:, 0, :, :].rearrange("p h n -> p (h n)")[:, 0:4 * ROWS0]\
            .rearrange("p (a k m) -> p a k m", a=2, k=2)
        vals = sb("vals", [P, B, CHUNKS, NH, HD + 1])
        headmask = sb("headmask", [P, 2, NH])
        blockmask = sb("blockmask", [NH, D])
        q_cls = sb("q_cls", [P, 2, NH])
        k_cls = sb("k_cls", [P, 2, NH])
        v_cls = sb("v_cls", [NH, D])
        v_block = sb("v_block", [K_STACK, NH, 32])
        negmax = sb("negmax", [P, B, CHUNKS, NH])
        nm_part = qk_part[0:NH, :, :, 0:TOK].rearrange("p (b a) k n -> p b a k n", b=B)[:, :, 0, :, :]
        cls_neg = sb("cls_neg", [NH, B])
        cls_sum = sb("cls_sum", [NH, B])
        cls_rsum = sb("cls_rsum", [NH, B])
        cls_probs = late([NH, B, TOK + 1])
        clskey_raw = late([NH, B, TOK])
        clskey_in = late([NH, TOK])
        clskey_probs = late([K_STACK, B, TOK])
        cls_probs_t = sb("cls_probs_t", [P, CHUNKS * NH])
        cls_sumv = late([NH, 2, D])
        ones = sb("ones", [NH, P])
        attn_t = late([P, 3, TOK])
        rsum = sb("rsum", [P, CHUNKS, NH])
        attn = late([P, CHUNKS, D])
        gexp = sb("gexp", [P, 3, E])
        gden = sb("gden", [P, 3, E])
        gsc = sb("gsc", [P, 3, E])
        gsb = sb("gsb", [P, 3, E])
        gbias = sb("gbias", [P, 3, E])
        ggrp = sb("ggrp", [P, 3, GROUPS])
        gsel = sb("gsel", [P, 3, GROUPS])
        gpen = sb("gpen", [P, 3, GROUPS])
        gmsk = sb("gmsk", [P, 3, E])
        gpick = sb("gpick", [P, 3, E])
        grsum = sb("grsum", [P, 3])
        by_group = gsb[:].rearrange("p c (g k) -> p c g k", k=2)
        masked = gmsk[:].rearrange("p c (g k) -> p c g k", k=2)
        wide = [P, 3, GROUPS, 2]
        gge = late([P, 3, E * E])
        ggt = late([P, 3, E * E])
        grank = sb("grank", [P, 3, E])
        gsum = sb("gsum", [P, 3])
        cw = sb("cw", [P, B, 3, E])
        hidden_cls = sb("hidden_cls", [P, B, E])
        order = sb("order", [P, 2, GROUPS * GROUPS + E * E])
        silu = late([P, 2, N])
        out_cls = sb("out_cls", [B, D])

        bank = ctx.enter_context(nc.psum_tensor("bank", [P, 8, 512], F32))

        qk_dram = nc.dram_tensor("qk_dram", (B, 2, 2 * D, N), F32, kind="Internal").ap()

        CLSB = ((1, 6), (5, 7))
        MISC, ACC, SCORE = (7, 3), (6, 2), ((4, 5), (0, 1, 4, 5))
        MAXB = ((0, 2, 4), (0, 2))
        TURN = ((6, 7), (0, 1), (6, 7), (2, 3))
        QKB = (2, 3, 4, 5)
        VB = (6, 0)
        GATEB = (7, 3)
        FFB = ((0, 1), (4, 5))
        YB = (6, 7)
        SHAREB, YCLS = 2, 3
        QK_ROWS = (P, D2, P, D2)
        QK_AT = (0, P, D, D + P)

        PASSES = ((0, 0, 0), (1, 0, 0), (0, 0, 1), (0, 1, 2), (1, 1, 2))

        def summed(b, k, c):
            return (2 * E + 1) * b + (2 * k + c if k else 1)

        def write_qk(queue, b, i):
            rows, at = QK_ROWS[i], QK_AT[i]
            queue.wait_ge(s("a_qkhi"), 4 * b + i + 1)
            queue.wait_ge(s("v_qklo"), 4 * b + i + 1)
            queue.dma_start(qk_dram[b, :, at:at + rows, :].rearrange("p f n -> f p n"),
                            qk_part[0:rows, i, :, :].bitcast(F32)).then_inc(s(f"qk_out{b}"), 16)

        block = ctx.enter_context(nc.Block())

        @block.sync
        def _(sp):
            def load_idx(n, first, last):
                sp.dma_start(idx_all[:, first:last], t["idx0"][first:last].partition_broadcast(P))\
                    .then_inc(s(f"ld_idx{n}"), 16)

            def load_l0(half, first, last):
                sp.dma_start(w_l0[:, first:last, :], t["w_l0"][:, first:last, :]).then_inc(s(f"ld_l0_{half}"), 16)

            load_idx(0, 0, COLS0)
            sp.dma_start(cst[:], t["cst"]).then_inc(s("ld_cst"), 16)
            load_idx(1, COLS0, 2 * COLS0)
            load_l0(0, 0, 4)
            load_idx(2, 2 * COLS0, 4 * COLS0)
            load_l0(1, 4, GP)
            load_idx(3, 4 * COLS0, 8 * COLS0)
            sp.dma_start(ident[:], t["ident"]).then_inc(s("ld_ident"), 16)
            sp.dma_start(w_l1[:], t["w_l1"]).then_inc(s("ld_l12"), 16)
            sp.dma_start(w_l2[:], t["w_l2"]).then_inc(s("ld_l12"), 16)
            sp.dma_start(w_fuse12[:], t["w_fuse12"]).then_inc(s("ld_l12"), 16)
            sp.dma_start(bias_l[:], t["bias_l"]).then_inc(s("ld_l12"), 16)
            for half in range(2):
                sp.dma_start(w_raw[:, half, 0:3 * D], t["w_qkv"][half]).then_inc(s("ld_qkv"), 16)
            sp.dma_start(interp[:], t["interp"]).then_inc(s("ld_fuse"), 16)
            sp.dma_start(w_fuse0[:], t["w_fuse0"]).then_inc(s("ld_fuse"), 16)
            sp.wait_ge(s("p_zero"), 2)
            for b in range(B):
                sp.dma_start(hres[0:1, b, 2, :], t["cls"]).then_inc(s("ld_cls"), 16)
                sp.dma_start(coarse[96:97, b, :], t["bf"]).then_inc(s("ld_fuse"), 16)
            sp.dma_start(headmask[:], t["headmask"]).then_inc(s("ld_att"), 16)
            sp.dma_start(blockmask[:], t["blockmask"]).then_inc(s("ld_att"), 16)
            sp.dma_start(bias_v[:], t["bv"].partition_broadcast(P)).then_inc(s("ld_att"), 16)
            sp.dma_start(bias_qk[:], t["bqk"]).then_inc(s("ld_att"), 16)
            sp.dma_start(gbias[:].rearrange("p c e -> p (c e)"), t["gbias"].partition_broadcast(P)).then_inc(s("ld_gate"), 16)
            sp.dma_start(order[:].rearrange("p a n -> p (a n)"), t["order"].partition_broadcast(P)).then_inc(s("ld_gate"), 16)
            sp.wait_ge(s("t_emb0"), STEPS0)
            sp.dma_start(w_down[:], t["w_down"]).then_inc(s("ld_down"), 16)

            def stack_qk(b):
                sp.wait_ge(s(f"qk_out{b}"), 64)
                sp.wait_ge(s("p_stack"), 2 * (b + 1))
                for i, (stack, parts) in enumerate(((q_stack, (0, 1, 0)), (k_stack, (0, 0, 1)))):
                    for r, part in enumerate(parts):
                        src = qk_dram[b, part, i * D:(i + 1) * D, :].rearrange("(h d) n -> d h n", d=HD)
                        sp.dma_start(stack[r * HD:(r + 1) * HD, b, :, :].bitcast(F32), src)\
                            .then_inc(s(f"stack_in{b}"), 16)

            def maxima_rows(b):
                for part in range(2):
                    sp.wait_ge(s("v_nm"), 2 * b + part + 1)
                    sp.dma_start(q_stack[MAXROW + part:MAXROW + part + 1, b, :, 0:TOK].bitcast(F32),
                                 nm_part[:, b, part, :].bitcast(F32))\
                        .then_inc(s(f"nm_in{b}"), 16)

            def store(b, c):
                sp.wait_ge(s("v_acc"), summed(b, E, c))
                sp.dma_start(out[b, 1 + c * P:1 + (c + 1) * P, :], hres[:, b, c, :]).then_inc(s("stored"), 16)

            for i in range(4):
                write_qk(sp, 0, i)
            stack_qk(0)
            stack_qk(1)
            maxima_rows(0)
            maxima_rows(1)
            store(0, 0)
            store(0, 1)
            sp.wait_ge(s("v_outcls"), 1)
            sp.dma_start(out[:, 0, :], out_cls[:]).then_inc(s("stored"), 16)
            store(1, 0)
            store(1, 1)
            sp.wait_ge(s("stored"), 16 * (2 * B + 1))

        @block.gpsimd
        def _(pool):
            pool.memset(hres[:, :, 2, :], 0.0).then_inc(s("p_zero"), 1)
            pool.memset(coarse[:], 0.0).then_inc(s("p_zero"), 1)
            pool.wait_ge(s("v_gidx"), 2)
            for k in range(10):
                dst, src = (got1[:, k, :], t["pix1"]) if k < 8 else (got2[:, k - 8, :], t["pix2"])
                pool.indirect_dma_start(dst, None, src[:, :],
                                        bass.IndirectOffsetOnAxis(ap=gidx[:, k:k + 1], axis=0))\
                    .then_inc(s("gathered"), 16)

            pool.wait_ge(s("ld_qkv"), 32)
            pool.tensor_copy(wq_hi[:], w_raw[:, :, 0:3 * D]).then_inc(s("p_split"), 1)
            pool.wait_ge(s("p_split"), 1)
            pool.tensor_tensor(wq_lo[:], w_raw[:, :, 0:3 * D], wq_hi[:].bitcast(F32), ALU.subtract)\
                .then_inc(s("p_split"), 1)
            pool.memset(vals[:, :, :, :, HD:HD + 1], 1.0).then_inc(s("p_const"), 1)
            pool.memset(v_block[:], 0.0).then_inc(s("p_const"), 1)
            pool.memset(ones[:], 1.0).then_inc(s("p_const"), 1)
            pool.wait_ge(s("p_split"), 2)
            pool.wait_ge(s("p_const"), 3)
            pool.wait_ge(s("t_picked"), STEPS0)
            for b in range(B):
                pool.memset(k_stack[0:K_STACK, b, :, :].bitcast(F32), 1.0).then_inc(s("p_stack"), 1)
                pool.memset(q_stack[0:K_STACK, b, :, :].bitcast(F32), 0.0).then_inc(s("p_stack"), 1)
            pool.wait_ge(s("p_stack"), 2 * B)
            pool.memset(gexp[:], 0.0).then_inc(s("p_const"), 1)
            pool.wait_ge(s("t_h"), 2)
            pool.memset(clskey_probs[:], 0.0).then_inc(s("p_const"), 1)
            def split_ff(half):
                cols = slice(half * RAW, (half + 1) * RAW)
                pool.wait_ge(s("p_split"), 2 * (half + 1))
                pool.dma_start(w_raw[:], t["w_ff"][half]).then_inc(s(f"ld_ff{half}"), 16)
                pool.wait_ge(s(f"ld_ff{half}"), 16)
                pool.tensor_copy(wf_hi[:, :, cols], w_raw[:]).then_inc(s("p_split"), 1)
                pool.wait_ge(s("p_split"), 2 * half + 3)
                pool.tensor_tensor(wf_lo[:, :, cols], w_raw[:], wf_hi[:, :, cols].bitcast(F32),
                                   ALU.subtract).then_inc(s("p_split"), 1)

            split_ff(0)
            pool.wait_ge(s("stack_in0"), 96)
            for half in range(1, 4):
                split_ff(half)

            chain = [0]

            def link(ins):
                chain[0] += 1
                ins.then_inc(s("p_chain"), 1)
                pool.wait_ge(s("p_chain"), chain[0])

            def beaten_by(vals_, n, at):
                ge = gge[:, :, 0:n * n].rearrange("p c (i j) -> p c i j", i=n)
                gt = ggt[:, :, 0:n * n].rearrange("p c (i j) -> p c i j", i=n)
                other = vals_.unsqueeze(2).to_broadcast([P, 3, n, n])
                own = vals_.unsqueeze(3).to_broadcast([P, 3, n, n])
                lower, upper = (order[:, k, at:at + n * n].unsqueeze(1).to_broadcast([P, 3, n * n])
                                for k in range(2))
                link(pool.tensor_tensor(ge, other, own, ALU.subtract))
                link(pool.tensor_scalar(gt, ge, 0.0, None, ALU.is_gt))
                link(pool.tensor_scalar(ge, ge, 0.0, None, ALU.is_ge))
                link(pool.tensor_tensor(gge[:, :, 0:n * n], gge[:, :, 0:n * n], lower, ALU.mult))
                link(pool.tensor_tensor(ggt[:, :, 0:n * n], ggt[:, :, 0:n * n], upper, ALU.mult))
                link(pool.tensor_tensor(gge[:, :, 0:n * n], gge[:, :, 0:n * n], ggt[:, :, 0:n * n], ALU.add))
                half = n // 2
                while half > 1:
                    link(pool.tensor_tensor(ge[:, :, :, 0:half], ge[:, :, :, 0:half], ge[:, :, :, half:2 * half],
                                            ALU.add))
                    half //= 2
                link(pool.tensor_tensor(grank[:, :, 0:n], ge[:, :, :, 0], ge[:, :, :, 1], ALU.add))

            def route(b):
                pool.wait_ge(s("v_route"), b + 1)
                if b:
                    pool.wait_ge(s("v_gate"), b)
                beaten_by(ggrp[:], GROUPS, 0)
                link(pool.tensor_scalar(gsel[:], grank[:, :, 0:GROUPS], 2.0, None, ALU.is_lt))
                link(pool.tensor_scalar(gpen[:], gsel[:], -1.0, FAR, ALU.add, ALU.mult))
                link(pool.tensor_tensor(masked, by_group, gsel[:].unsqueeze(3).to_broadcast(wide), ALU.mult))
                link(pool.tensor_tensor(masked, masked, gpen[:].unsqueeze(3).to_broadcast(wide), ALU.add))
                beaten_by(gmsk[:], E, GROUPS * GROUPS)
                link(pool.tensor_scalar(gmsk[:], grank[:], 2.0, None, ALU.is_lt))
                link(pool.tensor_tensor(gpick[:], gmsk[:], gsc[:], ALU.mult))
                link(pool.tensor_tensor(gmsk[:, :, 0:4], gpick[:, :, 0:4], gpick[:, :, 4:8], ALU.add))
                link(pool.tensor_tensor(gmsk[:, :, 0:2], gmsk[:, :, 0:2], gmsk[:, :, 2:4], ALU.add))
                link(pool.tensor_tensor(gsum[:], gmsk[:, :, 0], gmsk[:, :, 1], ALU.add))
                pool.tensor_scalar(gsum[:], gsum[:], 1e-6, None, ALU.add).then_inc(s("p_picked"), 1)

            for b in range(B):
                route(b)

        @block.scalar
        def _(act):
            act.dma_start(pix[:], t["pix"]).then_inc(s("ld_pix"), 16)
            act.dma_start(gidx_raw[:], t["gidx"]).then_inc(s("ld_gidx"), 16)
            nc.scalar.preload_act_table_set(LOG_EXP)

            def one_hot_high(c):
                act.wait_ge(s("v_parts"), 2 * c + 1)
                if c == 0:
                    act.wait_ge(s("ld_cst"), 16)
                else:
                    act.wait_ge(s("a_onehot"), c)
                nc.scalar.activation(apart, hi_idx[:, c % 2, :], ACT.Abs, bias=cst[:, 1:2])\
                    .then_inc(s("a_apart"), 1)
                act.wait_ge(s("a_apart"), c + 1)
                if c >= 2:
                    act.wait_ge(s("t_picked"), c - 1)
                nc.scalar.activation(onehot[:, c % 2, 1, :], apart, ACT.Relu, bias=1.0, scale=-1.0)\
                    .then_inc(s("a_onehot"), 1)

            def got_rows():
                act.wait_ge(s("gathered"), 160)
                for n, (got, f) in enumerate(((got1, F1), (got2, F2))):
                    nc.scalar.activation(got_by_batch[:, n, :, :].rearrange("p b (k f) -> p b k f", f=f),
                                         got[:].rearrange("p k (b f) -> p b k f", b=B), ACT.Copy)\
                        .then_inc(s("a_split"), 1)

            def got_turned():
                act.wait_ge(s("t_got"), 1)
                nc.scalar.activation(got_t[:].rearrange("p a n -> p (a n)"), bank[0:96, 3, :], ACT.Copy)\
                    .then_inc(s("a_got"), 1)

            def embeddings12():
                act.wait_ge(s("t_emb12"), 1)
                act.wait_ge(s("ld_l12"), 64)
                nc.scalar.activation(emb1[:], bank[0:EMB, 4, 0:P], ACT.Identity, bias=bias_l[0:EMB, 1:2])\
                    .then_inc(s("a_emb12"), 1)
                nc.scalar.activation(emb2[:], bank[0:EMB, 4, P:P + B * TOK2], ACT.Identity,
                                     bias=bias_l[0:EMB, 2:3]).then_inc(s("a_emb12"), 1)

            def fused_coarse():
                act.wait_ge(s("t_coarse"), 1)
                act.wait_ge(s("p_zero"), 2)
                nc.scalar.activation(coarse[0:80, :, :].rearrange("p b d -> p (b d)"), bank[0:80, 5, 0:B * D],
                                     ACT.Copy).then_inc(s("a_coarse"), 1)

            for c in range(STEPS0):
                if c == 6:
                    got_rows()
                one_hot_high(c)
            got_turned()
            embeddings12()
            fused_coarse()
            act.wait_ge(s("t_emb0"), STEPS0)
            nc.scalar.activation(emb0[:], bank[:, 2, 0:TOK], ACT.Identity, bias=bias_l[:, 0:1])\
                .then_inc(s("a_emb0"), 1)

            def inv_std(i):
                act.wait_ge(s("v_meanvar"), 3 * (i + 1))
                nc.scalar.activation(logvar[:], meanvar[:, :, 1], ACT.Ln, bias=cst[:, 3:4])\
                    .then_inc(s("a_rstd"), 1)
                act.wait_ge(s("a_rstd"), 2 * i + 1)
                nc.scalar.activation(rstd[:], logvar[:], ACT.Exp, scale=-0.5).then_inc(s("a_rstd"), 1)

            def x_high(i):
                b = i % B
                act.wait_ge(s("t_turned"), i + 1)
                if i >= B:
                    act.wait_ge(s("t_v"), b + 1)
                nc.scalar.activation(xt[:, b, 0, :], bank[:, TURN[i][0], 0:N], ACT.Copy)\
                    .then_inc(s("a_xhi"), 1)
                nc.scalar.activation(xt[:, b, 2, :], bank[:, TURN[i][1], 0:N], ACT.Copy)\
                    .then_inc(s("a_xhi"), 1)

            def qk_high(b, i):
                act.wait_ge(s("v_qk"), 4 * b + i + 1)
                if b:
                    act.wait_ge(s("qk_out0"), 64)
                nc.scalar.activation(qk_part[0:QK_ROWS[i], i, 0, :], qk[0:QK_ROWS[i], b, i, :], ACT.Copy)\
                    .then_inc(s("a_qkhi"), 1)

            def cls_softmax(b):
                act.wait_ge(s("v_clsmax"), b + 1)
                nc.scalar.activation(cls_probs[:, b, :], bank[0:NH, CLSB[b][0], 0:TOK + 1], ACT.Exp,
                                     bias=cls_neg[:, b:b + 1], accum_out=cls_sum[:, b:b + 1])\
                    .then_inc(s("a_cls"), 1)

            def clskey(b):
                act.wait_ge(s("v_clskey"), b + 1)
                act.wait_ge(s("p_const"), 5)
                nc.scalar.activation(clskey_probs[0:NH, b, :], clskey_in[:], ACT.Exp).then_inc(s("a_clskey"), 1)

            def exps(b, h):
                n = NH * b + h
                act.wait_ge(s("t_scores"), n + 1)
                if n >= PT_RING:
                    act.wait_ge(s("t_pv"), n - PT_RING + 1)
                nc.scalar.activation(probs[:, h % PT_RING, :, :].rearrange("p k n -> p (k n)"),
                                     bank[:, SCORE[b][h % len(SCORE[b])], :], ACT.Exp).then_inc(s("a_exp"), 1)

            def gate_exp(b):
                act.wait_ge(s("t_gate"), b + 1)
                act.wait_ge(s("p_const"), 4)
                if b:
                    act.wait_ge(s("v_route"), 1)
                nc.scalar.activation(gexp[:, 0:2, :].rearrange("p c e -> p (c e)"),
                                     bank[:, GATEB[b], 0:2 * E], ACT.Exp, scale=-1.0)\
                    .then_inc(s("a_gate"), 1)
                nc.scalar.activation(gexp[0:2, 2, :], bank[0:2, GATEB[b], 2 * E:3 * E], ACT.Exp, scale=-1.0)\
                    .then_inc(s("a_gate"), 1)

            def silus(b, k):
                n = (E + 1) * b + k
                act.wait_ge(s("t_up"), 2 * n + 1)
                if n >= 2:
                    act.wait_ge(s("v_gate_up"), n - 1)
                nc.scalar.activation(silu[:, n % 2, :], bank[:, FFB[n % 2][0], 0:N], ACT.Silu)\
                    .then_inc(s("a_silu"), 1)

            inv_std(0)
            x_high(0)
            inv_std(1)
            for i in range(4):
                qk_high(0, i)
            x_high(1)
            for i in range(4):
                qk_high(1, i)
            for i in range(4):
                write_qk(act, 1, i)
            cls_softmax(0)
            cls_softmax(1)
            clskey(0)
            for h in range(NH):
                exps(0, h)
                if h == 9:
                    clskey(1)
            for h in range(NH):
                exps(1, h)
                if h == 3:
                    inv_std(2)
                if h == 6:
                    x_high(2)
                if h == 9:
                    gate_exp(0)
            for k in range(E + 1):
                silus(0, k)
                if k == 1:
                    nc.scalar.preload_act_table_set(LOG_EXP)
                    inv_std(3)
                if k == 3:
                    x_high(3)
                if k == 5:
                    gate_exp(1)
            for k in range(E + 1):
                silus(1, k)

        @block.tensor
        def _(pe):
            def project(dst, w, x, weights_move, x_low=None):
                for n, (part, half, xpart) in enumerate(PASSES):
                    if x_low and n in (2, 3):
                        pe.wait_ge(s("v_xlo"), x_low + n - 3)
                    lhs, rhs = (x(xpart), w(part, half)) if weights_move else (w(part, half), x(xpart))
                    ins = pe.matmul(dst, lhs, rhs, start=(n == 0), stop=(n == len(PASSES) - 1))
                return ins

            def pick(c):
                pe.wait_ge(s("v_onehot"), c + 1)
                if c == 0:
                    pe.wait_ge(s("v_pix"), 2)
                if c >= 2:
                    pe.wait_ge(s("v_picked"), c - 1)
                for half in range(2):
                    if half:
                        pe.wait_ge(s("a_onehot"), c + 1)
                    for part in range(2):
                        ins = pe.matmul(bank[0:ROWS0, c % 2, :], pix_part[:, part, half, :],
                                        onehot[:, c % 2, half, :], start=(half + part == 0),
                                        stop=(half + part == 2))
                ins.then_inc(s("t_picked"), 1)

            def embed0(c):
                pe.wait_ge(s("v_picked"), c + 1)
                if c in (0, 2):
                    pe.wait_ge(s(f"ld_l0_{c // 2}"), 16)
                for n in range(2):
                    g = 2 * c + n
                    ins = pe.matmul(bank[:, 2, 0:TOK], w_l0[:, g, :],
                                    picked[0:ROWS0, c % 3, n * TOK:(n + 1) * TOK],
                                    start=(g == 0), stop=(g == GP - 1))
                ins.then_inc(s("t_emb0"), 1)

            def turn_gathered():
                pe.wait_ge(s("ld_ident"), 16)
                pe.wait_ge(s("a_split"), 2)
                for n in range(2 * B):
                    ins = pe.transpose(bank[0:96, 3, n * P:(n + 1) * P], got_by_batch[:, n // B, n % B, :],
                                       ident[:])
                ins.then_inc(s("t_got"), 1)

            def embed12():
                pe.wait_ge(s("a_got"), 1)
                pe.wait_ge(s("ld_l12"), 64)
                for n in range(2):
                    pe.matmul(bank[0:EMB, 4, 0:P], w_l1[:, n, :], got_t[:, 0:2, n * TOK1:(n + 1) * TOK1],
                              start=(n == 0), stop=(n == 1))
                for n in range(8):
                    ins = pe.matmul(bank[0:EMB, 4, P:P + B * TOK2], w_l2[:, n, :],
                                    got_t[:, 2:4, n * TOK2:(n + 1) * TOK2], start=(n == 0), stop=(n == 7))
                ins.then_inc(s("t_emb12"), 1)

            def fuse_coarse():
                pe.wait_ge(s("a_emb12"), 2)
                for b in range(B):
                    pe.matmul(bank[0:TOK1, 5, b * D:(b + 1) * D], emb1[:, b * TOK1:(b + 1) * TOK1],
                              w_fuse12[:, 0, :], start=True, stop=True)
                    ins = pe.matmul(bank[64:64 + TOK2, 5, b * D:(b + 1) * D],
                                    emb2[:, b * TOK2:(b + 1) * TOK2], w_fuse12[:, 1, :],
                                    start=True, stop=True)
                ins.then_inc(s("t_coarse"), 1)

            def fuse(b):
                if b == 0:
                    pe.wait_ge(s("a_emb0"), 1)
                    pe.wait_ge(s("a_coarse"), 1)
                    pe.wait_ge(s("ld_fuse"), 64)
                for c in range(CHUNKS):
                    dst = bank[:, 4 + b, c * D:(c + 1) * D]
                    pe.matmul(dst, emb0[:, c * P:(c + 1) * P], w_fuse0[:, b, :], start=True, stop=False)
                    ins = pe.matmul(dst, interp[:, c * P:(c + 1) * P], coarse[:, b, :],
                                    start=False, stop=True)
                ins.then_inc(s("t_h"), 1)

            def turn(i):
                pe.wait_ge(s("v_xn"), 4 * (i + 1))
                for c in range(3):
                    rows = P if c < 2 else 2
                    cols = slice(c * P, c * P + rows)
                    pe.transpose(bank[:, TURN[i][0], cols], xn[0:rows, c, 0:P], ident[0:rows, 0:rows])
                    ins = pe.transpose(bank[:, TURN[i][1], cols], xn[0:rows, c, P:], ident[0:rows, 0:rows])
                ins.then_inc(s("t_turned"), 1)

            def w_att(cols):
                return lambda part, half: (wq_lo if part else wq_hi)[:, half, cols]

            def w_ffn(cols):
                return lambda part, half: (wf_lo if part else wf_hi)[:, half, cols]

            def x_of(b, cols):
                return lambda part: xt[:, b, part, cols]

            def proj_qk(b, i):
                if i == 0:
                    pe.wait_ge(s("a_xhi"), 2 * (b + 1))
                    pe.wait_ge(s("p_split"), 2)
                if b:
                    pe.wait_ge(s("v_qk"), i + 1)
                cols = slice(QK_AT[i], QK_AT[i] + QK_ROWS[i])
                project(bank[0:QK_ROWS[i], QKB[i], 0:N], w_att(cols), x_of(b, slice(0, N)), False,
                        2 * (b + 1) if i == 0 else None)\
                    .then_inc(s("t_qk"), 1)

            def proj_v(b):
                cols = slice(2 * D, 3 * D)
                for c in range(CHUNKS):
                    ins = project(bank[:, VB[b], c * D:(c + 1) * D], w_att(cols),
                                  x_of(b, slice(c * P, (c + 1) * P)), True)
                ins.then_inc(s("t_v"), 1)
                if b == 0:
                    pe.wait_ge(s("v_xlo"), 4)
                    project(bank[0:NH, 7, 0:D], w_att(cols),
                            lambda part: xt[:, 0, part, CLS:CLS + 1].to_broadcast([P, NH]), True)\
                        .then_inc(s("t_vcls"), 1)

            def cls_scores(b):
                pe.wait_ge(s("v_qk"), 4 * (b + 1))
                pe.wait_ge(s("v_clsblk"), 4)
                pe.wait_ge(s("v_zero"), 4)
                pe.wait_ge(s("v_v"), 2)
                pe.wait_ge(s("v_vcls"), 1)
                for half in range(2):
                    pe.matmul(bank[0:NH, CLSB[b][0], 0:N], q_cls[:, half, :], qk[:, b, 2 + half, :],
                              start=(half == 0), stop=(half == 1))
                for half in range(2):
                    ins = pe.matmul(bank[0:NH, CLSB[b][1], 0:TOK], k_cls[:, half, :], qk[:, b, half, 0:TOK],
                                    start=(half == 0), stop=(half == 1))
                ins.then_inc(s("t_clsscores"), 1)

            def scores_for_max(b, u):
                n = UNITS * b + u
                c, pair = divmod(u, NH // 2)
                if u == 0:
                    pe.wait_ge(s(f"stack_in{b}"), 96)
                    pe.wait_ge(s("p_stack"), 4)
                if n == 0:
                    pe.wait_ge(s("v_v"), 4)
                    pe.wait_ge(s("v_qk"), 8)
                    pe.wait_ge(s("a_cls"), 1)
                if n == 2:
                    pe.wait_ge(s("a_cls"), B)
                if b or n >= 3:
                    pe.wait_ge(s("v_max"), n - (1 if b else 2))
                for j in range(2):
                    h = 2 * pair + j
                    ins = pe.matmul(bank[:, MAXB[b][u % len(MAXB[b])] + j, 0:N], q_stack[0:K_STACK, b, h, c * P:(c + 1) * P],
                                    k_stack[0:K_STACK, b, h, :], start=True, stop=True)
                ins.then_inc(s("t_formax"), 1)

            def turn_maxima(b):
                pe.wait_ge(s("v_max"), UNITS * (b + 1))
                pe.wait_ge(s("v_clsraw"), B)
                for c in range(CHUNKS):
                    ins = pe.transpose(bank[0:NH, MISC[b], c * P:(c + 1) * P], negmax[:, b, c, :], ident[:])
                ins.then_inc(s("t_nm"), 1)

            def scores(b, h):
                n = NH * b + h
                if h == 0:
                    pe.wait_ge(s(f"nm_in{b}"), 32)
                    if b:
                        pe.wait_ge(s("a_exp"), NH)
                if h >= len(SCORE[b]):
                    pe.wait_ge(s("a_exp"), n - len(SCORE[b]) + 1)
                for c in range(CHUNKS):
                    ins = pe.matmul(bank[:, SCORE[b][h % len(SCORE[b])], c * TOK:(c + 1) * TOK],
                                    k_stack[0:K_STACK, b, h, c * P:(c + 1) * P],
                                    q_stack[0:K_STACK, b, h, 0:TOK], start=True, stop=True)
                ins.then_inc(s("t_scores"), 1)

            def weigh(b, h):
                n = NH * b + h
                g, j = divmod(h, 4)
                if j == 0:
                    pe.wait_ge(s("a_clskey"), b + 1)
                    if b == 0 and g == 0:
                        pe.wait_ge(s("v_vcls"), 3)
                    if g:
                        pe.wait_ge(s("v_attn_t"), 3 * b + g)
                    pe.matmul(bank[:, ACC[b], 0:TOK],
                              v_block[:, 4 * g:4 * g + 4, :].rearrange("p j m -> p (j m)"),
                              clskey_probs[:, b, :], start=True, stop=False, skip_group_check=True)
                pe.wait_ge(s("a_exp"), n + 1)
                for c in range(CHUNKS):
                    ins = pe.matmul(bank[32 * j:32 * j + HD + 1, ACC[b], 0:TOK], vals[:, b, c, h, :],
                                    probs[:, h % PT_RING, c, :], start=False, stop=(c == CHUNKS - 1),
                                    skip_group_check=True)
                ins.then_inc(s("t_pv"), 1)

            def cls_turn(b):
                pe.wait_ge(s("v_clskey"), b + 1)
                pe.wait_ge(s("a_cls"), b + 1)
                for c in range(CHUNKS):
                    ins = pe.transpose(bank[:, MISC[b], c * NH:(c + 1) * NH], cls_probs[:, b, c * P:(c + 1) * P],
                                       ident[0:NH, 0:NH])
                ins.then_inc(s("t_clsprobs"), 1)

            def cls_weigh(b):
                pe.wait_ge(s("v_clsprobs"), b + 1)
                for c in range(CHUNKS):
                    ins = pe.matmul(bank[0:NH, MISC[b], 0:D], cls_probs_t[:, c * NH:(c + 1) * NH],
                                    vals[:, b, c, :, 0:HD], start=(c == 0), stop=(c == CHUNKS - 1))
                ins.then_inc(s("t_clssum"), 1)

            def cls_row(b):
                pe.wait_ge(s("v_clssum"), 2 * (b + 1))
                pe.wait_ge(s("p_const"), 3)
                pe.matmul(bank[0:1, MISC[b], 0:D], ones[:, 0:1], cls_sumv[:, 1, :], start=True, stop=True)\
                    .then_inc(s("t_clsrow"), 1)

            def turn_attn(b):
                pe.wait_ge(s("v_attn_t"), 3 * (b + 1))
                pe.wait_ge(s("v_clsrow"), b + 1)
                for c, into in enumerate((MISC[b], ACC[b])):
                    for g in range(3):
                        ins = pe.transpose(bank[:, into, g * P:(g + 1) * P], attn_t[:, g, c * P:(c + 1) * P],
                                           ident[:])
                    ins.then_inc(s("t_attn"), 1)

            def gate(b):
                pe.wait_ge(s("a_xhi"), 2 * (B + b + 1))
                pe.wait_ge(s("v_xlo"), 2 * (B + b + 1))
                pe.wait_ge(s("p_split"), 10)
                cols = slice(GATE, GATE + E)
                for c in range(3):
                    rows = P if c < 2 else 2
                    ins = project(bank[0:rows, GATEB[b], c * E:(c + 1) * E], w_ffn(cols),
                                  x_of(b, slice(c * P, c * P + rows)), True)
                ins.then_inc(s("t_gate"), 1)

            def cls_shares(b):
                pe.wait_ge(s("v_gate"), b + 1)
                pe.wait_ge(s("v_xlo"), 2 * B * B)
                pe.matmul(bank[:, SHAREB, b * E:(b + 1) * E], ones[0:1, :], cw[0:1, b, 2, :],
                          start=True, stop=True).then_inc(s("t_share"), 1)

            def up(b, k):
                n = (E + 1) * b + k
                if n == 0:
                    pe.wait_ge(s("a_exp"), B * NH)
                if n >= 2:
                    pe.wait_ge(s("v_gate_up"), n - 1)
                if k == 0:
                    pe.wait_ge(s("v_xlo"), 2 * (B + b + 1))
                for j in range(2):
                    cols = slice((2 * k + j) * INTER, (2 * k + j + 1) * INTER)
                    project(bank[:, FFB[n % 2][j], 0:N], w_ffn(cols), x_of(b, slice(0, N)), False)\
                        .then_inc(s("t_up"), 1)

            def down(b, k):
                n = (E + 1) * b + k
                pe.wait_ge(s("v_gate_up"), n + 1)
                if n == 0:
                    pe.wait_ge(s("ld_down"), 16)
                if n == 1:
                    pe.wait_ge(s("a_gate"), 2)
                if n >= 2:
                    pe.wait_ge(s("v_acc"), summed(*divmod(n - 2, E + 1), 1))
                for c in range(CHUNKS):
                    ins = pe.matmul(bank[:, YB[n % 2], c * D:(c + 1) * D], hidden[:, b, k, c * P:(c + 1) * P],
                                    w_down[:, k, :], start=True, stop=True)
                ins.then_inc(s("t_down"), 1)

            def down_cls():
                pe.wait_ge(s("a_gate"), 2 * B)
                pe.wait_ge(s("v_hcls"), B)
                for r in range(B):
                    pe.matmul(bank[0:B, YCLS, 0:D], cst[0:1, 4 + B * r:4 + B * (r + 1)], hres[0:1, r, 2, :],
                              start=(r == 0), stop=False)
                for k in range(E + 1):
                    ins = pe.matmul(bank[0:B, YCLS, 0:D], hidden_cls[:, :, k - 1] if k else hidden[:, :, 0, CLS],
                                    w_down[:, k, :], start=False, stop=(k == E))
                ins.then_inc(s("t_downcls"), 1)

            for c in range(STEPS0):
                pick(c)
                if c >= 1:
                    embed0(c - 1)
                if c == 6:
                    turn_gathered()
            embed12()
            embed0(STEPS0 - 1)
            fuse_coarse()
            fuse(0)
            fuse(1)
            turn(0)
            proj_qk(0, 0)
            proj_qk(0, 1)
            proj_qk(0, 2)
            proj_qk(0, 3)
            turn(1)
            proj_v(0)
            for i in range(4):
                proj_qk(1, i)
            proj_v(1)
            cls_scores(0)
            cls_scores(1)
            for u in range(UNITS):
                scores_for_max(0, u)
            turn_maxima(0)
            for u in range(AHEAD):
                scores_for_max(1, u)
            for h in range(NH + 2):
                if h < NH:
                    scores(0, h)
                if AHEAD + 2 * h < UNITS:
                    scores_for_max(1, AHEAD + 2 * h)
                if h >= 2:
                    weigh(0, h - 2)
                if AHEAD + 2 * h + 1 < UNITS:
                    scores_for_max(1, AHEAD + 2 * h + 1)
                if h == 4:
                    turn_maxima(1)
                    cls_turn(0)
                if h == 6:
                    cls_weigh(0)
                if h == 10:
                    cls_row(0)
            turn_attn(0)
            for h in range(NH + 2):
                if h < NH:
                    scores(1, h)
                if h >= 2:
                    weigh(1, h - 2)
                if h == 4:
                    cls_turn(1)
                if h == 6:
                    turn(2)
                if h == 7:
                    cls_weigh(1)
                if h == 9:
                    gate(0)
                if h == 12:
                    cls_row(1)
            for n in range(B * (E + 1)):
                up(*divmod(n, E + 1))
                if n == 0:
                    turn_attn(1)
                if n == 3:
                    turn(3)
                if n == 6:
                    gate(1)
                if n == 15:
                    cls_shares(0)
                    cls_shares(1)
                if n >= LAG:
                    down(*divmod(n - LAG, E + 1))
            for n in range(B * (E + 1) - LAG, B * (E + 1) - 1):
                down(*divmod(n, E + 1))
            down_cls()
            down(B - 1, E)

        @block.vector
        def _(dve):
            v = nc.vector
            for n in range(4):
                v.memset(qk[D2:P, n // 2, 2 * (n % 2) + 1, :], 0.0).then_inc(s("v_zero"), 1)
            dve.wait_ge(s("ld_gidx"), 16)
            for cols, last in ((slice(0, 8), TOK1 * GP - 1), (slice(8, 10), TOK2 * GP - 1)):
                v.tensor_scalar(gidx[:, cols], gidx_raw[:, cols], last, None, ALU.bitwise_and)\
                    .then_inc(s("v_gidx"), 1)
            dve.wait_ge(s("ld_pix"), 16)
            v.tensor_copy(pix_part[:, 0], pix[:]).then_inc(s("v_pix"), 1)
            dve.wait_ge(s("v_pix"), 1)
            v.tensor_tensor(pix_part[:, 1], pix[:], pix_part[:, 0].bitcast(F32), ALU.subtract)\
                .then_inc(s("v_pix"), 1)

            def one_hot(c):
                cols = slice(c * COLS0, (c + 1) * COLS0)
                if c in (0, 1, 2, 4):
                    dve.wait_ge(s(f"ld_idx{(0, 1, 2, 0, 3)[c]}"), 16)
                if c >= 2:
                    dve.wait_ge(s("v_onehot"), c - 1)
                    dve.wait_ge(s("a_apart"), c - 1)
                    dve.wait_ge(s("v_picked"), c - 1)
                v.tensor_scalar(hi_idx[:, c % 2, :], idx_all[:, cols], NPIX - 1, 4, ALU.bitwise_and,
                                ALU.logical_shift_right).then_inc(s("v_parts"), 1)
                v.tensor_scalar(lo_idx[:, c % 2, :], idx_all[:, cols], LOW - 1, None, ALU.bitwise_and)\
                    .then_inc(s("v_parts"), 1)
                dve.wait_ge(s("v_parts"), 2 * c + 1)
                if c == 0:
                    dve.wait_ge(s("ld_cst"), 16)
                if c >= 2:
                    dve.wait_ge(s("t_picked"), c - 1)
                v.tensor_scalar(onehot[:, c % 2, 0, :], hi_idx[:, c % 2, :], cst[:, 0:1], None, ALU.is_equal)\
                    .then_inc(s("v_onehot"), 1)

            def choose(c):
                dve.wait_ge(s("t_picked"), c + 1)
                dve.wait_ge(s("v_parts"), 2 * c + 2)
                if c >= 3:
                    dve.wait_ge(s("t_emb0"), c - 2)
                v.scalar_tensor_tensor(out=picked[0:ROWS0, c % 3, :], in0=lo_idx[0:ROWS0, c % 2, :],
                                       scalar=cst[0:ROWS0, 2:3], in1=bank[0:ROWS0, c % 2, :],
                                       op0=ALU.is_equal, op1=ALU.mult).then_inc(s("v_picked"), 1)

            for c in range(STEPS0):
                one_hot(c)
                if c >= 1:
                    choose(c - 1)
            choose(STEPS0 - 1)

            def take_h(b):
                dve.wait_ge(s("t_h"), b + 1)
                v.tensor_copy(hres[:, b, 0:2, :].rearrange("p c d -> p (c d)"), bank[:, 4 + b, 0:2 * D])\
                    .then_inc(s("v_h"), 1)

            def mean_var(i):
                b = i % B
                if i < B:
                    dve.wait_ge(s("t_h"), b + 1)
                    dve.wait_ge(s("ld_cls"), 32)
                else:
                    dve.wait_ge(s("v_hattn"), 2 * (b + 1))
                    dve.wait_ge(s("v_clsrow"), b + 1)
                if i:
                    dve.wait_ge(s("v_xn"), 4 * i)
                for c in range(3):
                    h = bank[:, 4 + b, c * D:(c + 1) * D] if i < B and c < CHUNKS else hres[:, b, c, :]
                    v.bn_stats(stats[:, c, :], h).then_inc(s("v_stats"), 1)
                for c in range(3):
                    dve.wait_ge(s("v_stats"), 3 * i + c + 1)
                    v.bn_aggr(meanvar[:, c, :], stats[:, c, :]).then_inc(s("v_meanvar"), 1)

            def normalise(i):
                b = i % B
                dve.wait_ge(s("a_rstd"), 2 * (i + 1))
                if i < B:
                    dve.wait_ge(s("v_h"), b + 1)
                if i:
                    dve.wait_ge(s("t_turned"), i)
                for c in range(3):
                    v.tensor_scalar(xn[:, c, 0:D], hres[:, b, c, :], meanvar[:, c, 0:1], rstd[:, c:c + 1],
                                    ALU.subtract, ALU.mult).then_inc(s("v_xn"), 1)
                dve.wait_ge(s("v_xn"), 4 * i + 3)
                v.tensor_copy(xn[:, :, D:], xn[:, :, P:D]).then_inc(s("v_xn"), 1)

            def x_low(i):
                b = i % B
                dve.wait_ge(s("a_xhi"), 2 * (i + 1))
                v.tensor_tensor(xt[:, b, 1, :], bank[:, TURN[i][0], 0:N], xt[:, b, 0, :].bitcast(F32),
                                ALU.subtract).then_inc(s("v_xlo"), 1)
                v.tensor_tensor(xt[D2:P, b, 2, :], bank[D2:P, TURN[i][1], 0:N],
                                xt[D2:P, b, 2, :].bitcast(F32), ALU.subtract).then_inc(s("v_xlo"), 1)

            def take_qk(b, i):
                if b == 0 and i == 0:
                    dve.wait_ge(s("ld_att"), 64)
                rows = QK_ROWS[i]
                dve.wait_ge(s("t_qk"), 4 * b + i + 1)
                v.tensor_scalar(qk[0:rows, b, i, :], bank[0:rows, QKB[i], 0:N], bias_qk[0:rows, i:i + 1],
                                SCALE if i < 2 else 1.0, ALU.add, ALU.mult).then_inc(s("v_qk"), 1)

            def qk_low(b, i):
                rows = QK_ROWS[i]
                dve.wait_ge(s("a_qkhi"), 4 * b + i + 1)
                v.tensor_tensor(qk_part[0:rows, i, 1, :], qk[0:rows, b, i, :],
                                qk_part[0:rows, i, 0, :].bitcast(F32), ALU.subtract)\
                    .then_inc(s("v_qklo"), 1)

            def take_v(b):
                dve.wait_ge(s("t_v"), b + 1)
                dve.wait_ge(s("p_const"), 1)
                for c in range(CHUNKS):
                    v.tensor_tensor(vals[:, b, c, :, 0:HD],
                                    bank[:, VB[b], c * D:(c + 1) * D].rearrange("p (h d) -> p h d", h=NH),
                                    bias_v[:].rearrange("p (h d) -> p h d", h=NH), ALU.add)\
                        .then_inc(s("v_v"), 1)

            def cls_blocks():
                dve.wait_ge(s("v_qk"), 4)
                dve.wait_ge(s("v_zero"), 4)
                for dst, first in ((q_cls, 0), (k_cls, 2)):
                    for half in range(2):
                        v.tensor_scalar(dst[:, half, :], headmask[:, half, :],
                                        qk[:, 0, first + half, CLS:CLS + 1], None, ALU.mult)\
                            .then_inc(s("v_clsblk"), 1)
                dve.wait_ge(s("t_vcls"), 1)
                v.tensor_tensor(v_cls[:], bank[0:NH, 7, 0:D], bias_v[0:NH, :], ALU.add)\
                    .then_inc(s("v_vcls"), 1)
                dve.wait_ge(s("v_vcls"), 1)
                dve.wait_ge(s("p_const"), 2)
                v.tensor_tensor(v_block[0:NH, :, 0:HD], v_cls[:].rearrange("p (h d) -> p h d", h=NH),
                                blockmask[:].rearrange("p (h d) -> p h d", h=NH), ALU.mult)\
                    .then_inc(s("v_vcls"), 1)
                dve.wait_ge(s("ld_ident"), 16)
                v.tensor_copy(v_block[0:NH, :, HD], ident[0:NH, 0:NH]).then_inc(s("v_vcls"), 1)

            def cls_max(b):
                dve.wait_ge(s("t_clsscores"), b + 1)
                v.tensor_reduce(cls_neg[:, b:b + 1], bank[0:NH, CLSB[b][0], 0:TOK + 1], AX.X, ALU.max,
                                negate=True).then_inc(s("v_clsmax"), 1)
                v.tensor_copy(clskey_raw[:, b, :], bank[0:NH, CLSB[b][1], 0:TOK]).then_inc(s("v_clsraw"), 1)

            def maxima(b, u):
                n = UNITS * b + u
                c, pair = divmod(u, NH // 2)
                dve.wait_ge(s("t_formax"), n + 1)
                two = MAXB[b][u % len(MAXB[b])]
                v.tensor_reduce(negmax[:, b, c, 2 * pair:2 * pair + 2], bank[:, two:two + 2, 0:TOK + 1],
                                AX.X, ALU.max, negate=True).then_inc(s("v_max"), 1)

            def nm_parts(b):
                dve.wait_ge(s("t_nm"), b + 1)
                dve.wait_ge(s("qk_out1"), 64)
                src = bank[0:NH, MISC[b], 0:TOK]
                v.tensor_copy(nm_part[:, b, 0, :], src).then_inc(s("v_nm"), 1)
                dve.wait_ge(s("v_nm"), 2 * b + 1)
                v.tensor_tensor(nm_part[:, b, 1, :], src, nm_part[:, b, 0, :].bitcast(F32), ALU.subtract)\
                    .then_inc(s("v_nm"), 1)

            def clskey_arg(b):
                dve.wait_ge(s("v_clsraw"), b + 1)
                if b:
                    dve.wait_ge(s("a_clskey"), b)
                v.tensor_tensor(clskey_in[:], bank[0:NH, MISC[b], 0:TOK], clskey_raw[:, b, :], ALU.add)\
                    .then_inc(s("v_clskey"), 1)

            def take_attn(b, g):
                dve.wait_ge(s("t_pv"), NH * b + 4 * (g + 1))
                if b:
                    dve.wait_ge(s("t_attn"), 2 * b)
                v.tensor_copy(attn_t[:, g, :], bank[:, ACC[b], 0:TOK]).then_inc(s("v_attn_t"), 1)

            def cls_probs_copy(b):
                dve.wait_ge(s("t_clsprobs"), b + 1)
                v.tensor_copy(cls_probs_t[:], bank[:, MISC[b], 0:CHUNKS * NH]).then_inc(s("v_clsprobs"), 1)
                v.reciprocal(cls_rsum[:, b:b + 1], cls_sum[:, b:b + 1]).then_inc(s("v_clsrsum"), 1)

            def cls_sums(b):
                dve.wait_ge(s("t_clssum"), b + 1)
                v.scalar_tensor_tensor(out=cls_sumv[:, 0, :], in0=v_cls[:], scalar=cls_probs[:, b, CLS:CLS + 1],
                                       in1=bank[0:NH, MISC[b], 0:D], op0=ALU.mult, op1=ALU.add)\
                    .then_inc(s("v_clssum"), 1)
                dve.wait_ge(s("v_clssum"), 2 * b + 1)
                dve.wait_ge(s("v_clsrsum"), b + 1)
                v.scalar_tensor_tensor(out=cls_sumv[:, 1, :], in0=cls_sumv[:, 0, :], scalar=cls_rsum[:, b:b + 1],
                                       in1=blockmask[:], op0=ALU.mult, op1=ALU.mult)\
                    .then_inc(s("v_clssum"), 1)

            def cls_add(b):
                dve.wait_ge(s("t_clsrow"), b + 1)
                row = hres[0:1, b, 2, :]
                v.tensor_tensor(row, bank[0:1, MISC[b], 0:D], row, ALU.add).then_inc(s("v_clsrow"), 1)

            def add_attn(b):
                for c, into in enumerate((MISC[b], ACC[b])):
                    n = 2 * b + c
                    dve.wait_ge(s("t_attn"), n + 1)
                    src = bank[:, into, 0:3 * P].rearrange("p (h m) -> p h m", h=NH)
                    v.reciprocal(rsum[:, c, :], src[:, :, HD]).then_inc(s("v_rsum"), 1)
                    dve.wait_ge(s("v_rsum"), n + 1)
                    v.tensor_tensor(attn[:, c, :].rearrange("p (h d) -> p h d", h=NH), src[:, :, 0:HD],
                                    rsum[:, c, :].unsqueeze(2).to_broadcast([P, NH, HD]), ALU.mult)\
                        .then_inc(s("v_attn"), 1)
                for c in range(CHUNKS):
                    dve.wait_ge(s("v_attn"), 2 * b + c + 1)
                    v.tensor_tensor(hres[:, b, c, :], hres[:, b, c, :], attn[:, c, :], ALU.add)\
                        .then_inc(s("v_hattn"), 1)

            chain = [0]

            def link(ins):
                chain[0] += 1
                ins.then_inc(s("v_chain"), 1)
                dve.wait_ge(s("v_chain"), chain[0])

            def route_scores(b):
                dve.wait_ge(s("a_gate"), 2 * (b + 1))
                dve.wait_ge(s("ld_gate"), 32)
                if b:
                    dve.wait_ge(s("p_picked"), b)
                link(v.tensor_scalar(gden[:], gexp[:], 1.0, None, ALU.add))
                link(v.reciprocal(gsc[:], gden[:]))
                link(v.tensor_tensor(gsb[:], gsc[:], gbias[:], ALU.add))
                v.tensor_tensor(ggrp[:], by_group[:, :, :, 0], by_group[:, :, :, 1], ALU.add)\
                    .then_inc(s("v_route"), 1)

            def shares(b):
                dve.wait_ge(s("p_picked"), b + 1)
                link(v.reciprocal(grsum[:], gsum[:]))
                v.tensor_tensor(cw[:, b, :, :], gpick[:], grsum[:].unsqueeze(2).to_broadcast([P, 3, E]), ALU.mult)\
                    .then_inc(s("v_gate"), 1)

            def gate_up(b, k):
                n = (E + 1) * b + k
                dve.wait_ge(s("a_silu"), n + 1)
                dve.wait_ge(s("t_up"), 2 * n + 2)
                v.tensor_tensor(hidden[:, b, k, :], bank[:, FFB[n % 2][1], 0:N], silu[:, n % 2, :], ALU.mult)\
                    .then_inc(s("v_gate_up"), 1)

            def add_down(b, k):
                dve.wait_ge(s("t_down"), (E + 1) * b + k + 1)
                y = bank[:, YB[((E + 1) * b + k) % 2], 0:CHUNKS * D]
                if k == 0:
                    res = hres[:, b, 0:2, :].rearrange("p c d -> p (c d)")
                    v.tensor_tensor(res, y, res, ALU.add).then_inc(s("v_acc"), 1)
                    return
                dve.wait_ge(s("v_gate"), b + 1)
                for c in range(CHUNKS):
                    dve.wait_ge(s("v_acc"), summed(b, k - 1, c))
                    v.scalar_tensor_tensor(out=hres[:, b, c, :], in0=y[:, c * D:(c + 1) * D],
                                           scalar=cw[:, b, c, k - 1:k], in1=hres[:, b, c, :],
                                           op0=ALU.mult, op1=ALU.add).then_inc(s("v_acc"), 1)

            def share_cls(b):
                dve.wait_ge(s("t_share"), b + 1)
                dve.wait_ge(s("v_gate_up"), (E + 1) * (b + 1))
                v.tensor_tensor(hidden_cls[:, b, :], hidden[:, b, 1:, CLS], bank[:, SHAREB, b * E:(b + 1) * E],
                                ALU.mult).then_inc(s("v_hcls"), 1)

            mean_var(0)
            take_h(0)
            take_h(1)
            normalise(0)
            mean_var(1)
            x_low(0)
            normalise(1)
            take_qk(0, 0)
            take_qk(0, 1)
            qk_low(0, 0)
            take_qk(0, 2)
            qk_low(0, 1)
            take_qk(0, 3)
            qk_low(0, 2)
            qk_low(0, 3)
            x_low(1)
            take_v(0)
            cls_blocks()
            for i in range(4):
                take_qk(1, i)
            take_v(1)
            for i in range(4):
                qk_low(1, i)
            cls_max(0)
            cls_max(1)
            for u in range(UNITS):
                maxima(0, u)
            nm_parts(0)
            maxima(1, 0)
            maxima(1, 1)
            clskey_arg(0)
            for u in range(2, UNITS):
                maxima(1, u)
            take_attn(0, 0)
            nm_parts(1)
            clskey_arg(1)
            cls_probs_copy(0)
            cls_sums(0)
            take_attn(0, 1)
            cls_add(0)
            take_attn(0, 2)
            add_attn(0)
            mean_var(2)
            take_attn(1, 0)
            normalise(2)
            cls_probs_copy(1)
            x_low(2)
            take_attn(1, 1)
            cls_sums(1)
            route_scores(0)
            cls_add(1)
            take_attn(1, 2)
            add_attn(1)
            gate_up(0, 0)
            mean_var(3)
            gate_up(0, 1)
            normalise(3)
            gate_up(0, 2)
            gate_up(0, 3)
            x_low(3)
            for n in range(4, B * (E + 1)):
                gate_up(*divmod(n, E + 1))
                if n == 6:
                    shares(0)
                if n == 7:
                    route_scores(1)
                if n == 14:
                    shares(1)
                if n == 16:
                    share_cls(0)
                if n >= LAG:
                    add_down(*divmod(n - LAG, E + 1))
            share_cls(1)
            for n in range(B * (E + 1) - LAG, B * (E + 1) - 1):
                add_down(*divmod(n, E + 1))
            dve.wait_ge(s("t_downcls"), 1)
            v.tensor_copy(out_cls[:], bank[0:B, YCLS, 0:D]).then_inc(s("v_outcls"), 1)
            add_down(B - 1, E)


def kernel(**x):
    import numpy as np
    import concourse.bacc as bacc
    from concourse import mybir as _mybir
    from concourse.bass_utils import run_bass_kernel_spmd

    a = {k: np.asarray(v) for k, v in x.items()}
    f32 = np.float32

    def rows_twice(w):
        return np.stack([w[:P], np.concatenate([w[P:], w[P:]])])

    def pad_rows(w):
        return np.concatenate([w, np.zeros((P - w.shape[0],) + w.shape[1:], w.dtype)])

    img = a["x"]

    def patches(p):
        h = img.shape[2] // p
        q = img.reshape(B, CH, h, p, h, p).transpose(2, 4, 0, 3, 5, 1)
        return q.reshape(h * h, B * p * p * CH)

    t = {}
    t["pix"] = patches(1).reshape(2, P, LOW, B * CH).transpose(1, 0, 3, 2).reshape(P, 2, ROWS0)
    t["pix1"] = patches(2)
    t["pix2"] = patches(4)
    t["idx0"] = a["L0_tok_idx0"].reshape(TOK, GP).T.reshape(-1)
    idx1 = a["L0_tok_idx1"].reshape(TOK1, 2, 8).transpose(1, 0, 2).reshape(P, 8)
    idx2 = a["L0_tok_idx2"].reshape(TOK2, 8, 2).transpose(1, 0, 2).reshape(P, 2)
    t["gidx"] = np.concatenate([idx1, idx2], axis=1)
    w0 = a["L0_tok_W0"].reshape(EMB, GP, CH).transpose(2, 1, 0)
    big = np.zeros((B, CH, LOW, GP, B, EMB), f32)
    for b in range(B):
        big[b, :, :, :, b, :] = w0[:, None]
    t["w_l0"] = big.reshape(ROWS0, GP, B * EMB)
    t["w_l1"] = a["L0_tok_W1"].T.reshape(2, 96, EMB).transpose(1, 0, 2)
    t["w_l2"] = a["L0_tok_W2"].T.reshape(8, 96, EMB).transpose(1, 0, 2)
    b0 = a["L0_tok_b0"]
    t["bias_l"] = np.stack([np.concatenate([b0, b0]), pad_rows(a["L0_tok_b1"]), pad_rows(a["L0_tok_b2"])], axis=1)
    wf = a["L0_tok_Wf"].T.reshape(3, EMB, D)
    zero = np.zeros((EMB, D), f32)
    t["w_fuse0"] = np.stack([np.concatenate([wf[0], zero]), np.concatenate([zero, wf[0]])], axis=1)
    t["w_fuse12"] = wf[1:].transpose(1, 0, 2)
    t["bf"] = a["L0_tok_bf"][None]
    interp = np.zeros((P, TOK), f32)
    for at, n in ((0, TOK1), (64, TOK2)):
        pos = np.clip((np.arange(TOK) + 0.5) * (n / TOK) - 0.5, 0.0, n - 1)
        lo = np.floor(pos).astype(int)
        hi = np.minimum(lo + 1, n - 1)
        for i in range(TOK):
            interp[at + lo[i], i] += 1.0 - (pos[i] - lo[i])
            interp[at + hi[i], i] += pos[i] - lo[i]
    interp[96] = 1.0
    t["interp"] = interp
    t["cls"] = a["cls_tok"].reshape(1, D)
    wqkv = np.concatenate([a["L0_attn_Wq"], a["L0_attn_Wk"], a["L0_attn_Wv"]]).T
    t["w_qkv"] = rows_twice(wqkv)
    bq, bk = a["L0_attn_bq"], a["L0_attn_bk"]
    t["bqk"] = np.stack([bq[:P], pad_rows(bq[P:]), bk[:P], pad_rows(bk[P:])], axis=1)
    t["bv"] = a["L0_attn_bv"]
    ups = np.stack([np.concatenate([a["L0_ffn_sw1"][None], a["L0_ffn_w1"]]),
                    np.concatenate([a["L0_ffn_sw3"][None], a["L0_ffn_w3"]])], axis=1)
    wff = np.concatenate([ups.reshape(GATE, D), a["L0_ffn_gate_weight"]]).T
    t["w_ff"] = rows_twice(wff).reshape(2, P, WFF // RAW, RAW).transpose(2, 1, 0, 3)
    t["w_down"] = np.concatenate([a["L0_ffn_sw2"][None], a["L0_ffn_w2"]]).transpose(2, 0, 1)
    t["gbias"] = np.tile(a["L0_ffn_gate_bias"], 3)
    head = (np.arange(2 * P)[:, None] // HD == np.arange(NH)[None]).astype(f32)
    t["headmask"] = head.reshape(2, P, NH).transpose(1, 0, 2)
    t["blockmask"] = head[:D].T
    t["ident"] = np.eye(P, dtype=f32)
    lower = [np.tril(np.ones((n, n), f32), -1).reshape(-1) for n in (GROUPS, E)]
    upper = [np.triu(np.ones((n, n), f32), 1).reshape(-1) for n in (GROUPS, E)]
    t["order"] = np.stack([np.concatenate(m) for m in (lower, upper)]).reshape(-1)
    p = np.arange(P)
    cst = np.zeros((P, 8), f32)
    cst[:, 0], cst[:, 1], cst[:, 2], cst[:, 3] = p, -(p + P), p % LOW, EPS
    cst[0, 4], cst[0, 7] = 1.0, 1.0
    t["cst"] = cst

    nc = bacc.Bacc("TRN2", target_bir_lowering=False, num_devices=1)
    t = {k: np.ascontiguousarray(v) for k, v in t.items()}
    aps = {k: nc.dram_tensor(f"in_{k}", v.shape, _mybir.dt.from_np(v.dtype), kind="ExternalInput").ap()
           for k, v in t.items()}
    shape = (B, 1 + TOK, D)
    out = nc.dram_tensor("out_tokens", shape, _mybir.dt.float32, kind="ExternalOutput").ap()
    build(nc, aps, out)
    return run_bass_kernel_spmd(nc, [{f"in_{k}": v for k, v in t.items()}], core_ids=[0]).results[0]["out_tokens"]
```

```python
from contextlib import ExitStack

import concourse.bass as bass
from concourse import mybir

F32 = mybir.dt.float32
F32R = mybir.dt.float32r
I32 = mybir.dt.int32
ALU = mybir.AluOpType
ACT = mybir.ActivationFunctionType
AX = mybir.AxisListType

P = 128
B = 2
CH = 3
D = 192
D2 = D - P
NH = 12
HD = D // NH
E = 8
INTER = 128
GROUPS = 4
GP = 16
TOK = 256
CLS = TOK
N = TOK + 2
CHUNKS = TOK // P
NPIX = 4096
LOW = 16
ROWS0 = B * CH * LOW
COLS0 = 512
STEPS0 = NPIX // COLS0
EMB = 64
TOK1, TOK2 = 64, 16
F1, F2 = 12, 48
EPS = 1e-5
SCALE = HD ** -0.5
FAR = 1e30
GATE = 2 * INTER * (E + 1)
WFF = GATE + E
SLICES = 4
RAW = WFF // SLICES
K_STACK = 128
QKT = 3
EARLY = P // HD
MAXROW = 3 * HD
PT_RING = 4
UNITS = CHUNKS * NH // 2
LAG = 5
AHEAD = 6
ARENA2 = 4900
LOG_EXP = "natural_log_exp_and_others"


def build(nc, t, out):
    ctx = ExitStack()
    with ctx:
        def sb(name, shape, dt=F32):
            return ctx.enter_context(nc.sbuf_tensor(name, shape, dt))

        class Signals:

            def __init__(self):
                self.made = {}

            def __call__(self, name):
                if name not in self.made:
                    self.made[name] = ctx.enter_context(nc.semaphore(name))
                return self.made[name]

        s = Signals()

        arena = sb("arena", [P, 10240])
        idx_all = arena[:, 0:NPIX].bitcast(I32)
        picked = arena[:, 4096:5632].rearrange("p (r n) -> p r n", r=3)
        hi_idx = arena[:, 5632:6656].bitcast(I32).rearrange("p (r n) -> p r n", r=2)
        lo_idx = arena[:, 6656:7680].bitcast(I32).rearrange("p (r n) -> p r n", r=2)
        apart = arena[:, 7680:8192]
        w_l0 = arena[0:ROWS0, 8192:10240].rearrange("p (g m) -> p g m", g=GP)
        probs = arena[:, 0:2048].rearrange("p (r k n) -> p r k n", r=PT_RING, k=CHUNKS)
        w_down = arena[:, 6692:8420].rearrange("p (e d) -> p e d", e=E + 1)
        hidden = arena[:, 2048:6692].rearrange("p (b e n) -> p b e n", b=B, e=E + 1)

        w_ff_raw = arena[:, 2048:2048 + SLICES * 2 * RAW].rearrange("p (s a n) -> p s a n", s=SLICES, a=2)

        arena2 = sb("arena2", [P, ARENA2])

        class Carve:

            def __init__(self):
                self.at = 0

            def __call__(self, shape):
                words = 1
                for d in shape[1:]:
                    words *= d
                tile = arena2[0:shape[0], self.at:self.at + words]
                self.at += words
                assert self.at <= ARENA2
                names = [f"a{i}" for i in range(len(shape) - 1)]
                sizes = dict(zip(names, shape[1:]))
                return tile.rearrange(f"p ({' '.join(names)}) -> p {' '.join(names)}", **sizes) \
                    if len(names) > 1 else tile

        early, late = Carve(), Carve()
        pix = early([P, 2, ROWS0])
        cst = sb("cst", [P, 9])
        gidx_raw = sb("gidx_raw", [P, 10], I32)
        gidx = sb("gidx", [P, 10], I32)
        got1 = early([P, 8, B * F1])
        got2 = early([P, 2, B * F2])
        got_by_batch = early([P, 2, B, 96])
        got_t = early([96, 4, P])
        w_l1 = early([96, 2, EMB])
        w_l2 = early([96, 8, EMB])
        emb1 = early([EMB, P])
        emb2 = early([EMB, B * TOK2])
        bias_l = sb("bias_l", [P, 3])
        emb0 = early([P, TOK])
        w_fuse0 = early([P, B, D])
        w_fuse12 = early([EMB, 2, D])
        interp = early([P, TOK])
        coarse = early([P, B, D])
        ident = sb("ident", [P, P])
        hres = sb("hres", [P, B, 3, D])
        logvar = sb("logvar", [P, 3])
        stats = sb("stats", [P, 3, 6])
        meanvar = sb("meanvar", [P, 3, 2])
        rstd = sb("rstd", [P, 3])
        xn = sb("xn", [P, 3, D + D2])
        xt = sb("xt", [P, B, 3, N], F32R)
        w_raw = sb("w_raw", [P, 2, 3 * D])
        wq_hi = sb("wq_hi", [P, 2, 3 * D], F32R)
        wq_lo = sb("wq_lo", [P, 2, 3 * D], F32R)
        wf_hi = sb("wf_hi", [P, 2, WFF], F32R)
        wf_lo = sb("wf_lo", [P, 2, WFF], F32R)
        bias_qk = sb("bias_qk", [P, QKT])
        bias_v = sb("bias_v", [P, D])
        qk = sb("qk", [P, B, QKT, N])
        qk_part = sb("qk_part", [P, QKT, 2, N], F32R)
        q_stack = sb("q_stack", [P, B, NH, N], F32R)
        k_stack = sb("k_stack", [P, B, NH, N], F32R)
        onehot = q_stack[:, 0, :, :].rearrange("p h n -> p (h n)")[:, 0:4 * COLS0]\
            .rearrange("p (r k n) -> p r k n", r=2, k=2)
        pix_part = k_stack[:, 0, :, :].rearrange("p h n -> p (h n)")[:, 0:4 * ROWS0]\
            .rearrange("p (a k m) -> p a k m", a=2, k=2)
        vals = sb("vals", [P, B, CHUNKS, NH, HD + 1])
        headmask = sb("headmask", [P, 3, NH])
        blockmask = sb("blockmask", [NH, D])
        cls_rest = sb("cls_rest", [P, 1])
        q_cls = sb("q_cls", [P, 2, NH])
        k_cls = sb("k_cls", [P, 2, NH])
        v_cls = sb("v_cls", [NH, D])
        v_block = sb("v_block", [K_STACK, NH, 32])
        negmax = sb("negmax", [P, B, CHUNKS, NH])
        nm_part = qk_part[0:NH, 0:B, :, 0:TOK]
        cls_neg = sb("cls_neg", [NH, B])
        cls_sum = sb("cls_sum", [NH, B])
        cls_rsum = sb("cls_rsum", [NH, B])
        cls_probs = late([NH, B, TOK + 1])
        clskey_raw = late([NH, B, TOK])
        clskey_in = late([NH, TOK])
        clskey_probs = late([K_STACK, B, TOK])
        cls_probs_t = sb("cls_probs_t", [P, CHUNKS * NH])
        cls_sumv = late([NH, 2, D])
        ones = sb("ones", [NH, P])
        attn_t = late([P, 3, TOK])
        rsum = sb("rsum", [P, CHUNKS, NH])
        attn = late([P, CHUNKS, D])
        gexp = sb("gexp", [P, 3, E])
        gden = sb("gden", [P, 3, E])
        gsc = sb("gsc", [P, 3, E])
        gsb = sb("gsb", [P, 3, E])
        gbias = sb("gbias", [P, 3, E])
        ggrp = sb("ggrp", [P, 3, GROUPS])
        gsel = sb("gsel", [P, 3, GROUPS])
        gpen = sb("gpen", [P, 3, GROUPS])
        gmsk = sb("gmsk", [P, 3, E])
        gpick = sb("gpick", [P, 3, E])
        grsum = sb("grsum", [P, 3])
        by_group = gsb[:].rearrange("p c (g k) -> p c g k", k=2)
        masked = gmsk[:].rearrange("p c (g k) -> p c g k", k=2)
        wide = [P, 3, GROUPS, 2]
        gge = late([P, 3, E * E])
        ggt = late([P, 3, E * E])
        grank = sb("grank", [P, 3, E])
        gsum = sb("gsum", [P, 3])
        cw = sb("cw", [P, B, 3, E])
        hidden_cls = sb("hidden_cls", [P, E + 1, 32])
        order = sb("order", [P, 2, GROUPS * GROUPS + E * E])
        silu = late([P, 2, N])
        out_cls = sb("out_cls", [B, D])
        down_rows = sb("down_rows", [P, D])
        res_cls = sb("res_cls", [B, D])

        bank = ctx.enter_context(nc.psum_tensor("bank", [P, 8, 512], F32))

        CLSB = (6, 7)
        MISC, ACC, SCORE = (7, 3), (6, 2), ((4, 5), (0, 4, 5))
        ACC_OF = tuple((acc, 1, acc) for acc in ACC)
        MAXB = ((0, 2, 4), (0, 2))
        TURN = ((6, 7), (0, 1), (6, 7), (2, 3))
        QKB = (2, 3, 4)
        VB = (6, 0)
        GATEB = (7, 3)
        FFB = ((0, 1), (4, 5))
        YB = (6, 7, 2)
        SHAREB, YCLS = 3, 3

        PASSES = ((0, 0, 0), (1, 0, 0), (0, 0, 1), (0, 1, 2), (1, 1, 2))

        MAX_UNITS = [(c, pair) for pairs in (range(EARLY // 2), range(EARLY // 2, NH // 2))
                     for c in range(CHUNKS) for pair in pairs]

        def summed(b, k, c):
            return (2 * E + 1) * b + (2 * k + c if k else 1)

        qk_dram = nc.dram_tensor("qk_dram", (B, 2, D, 3, N), F32, kind="Internal").ap()

        block = ctx.enter_context(nc.Block())

        @block.sync
        def _(sp):
            def load_idx(n, first, last):
                sp.dma_start(idx_all[:, first:last], t["idx0"][first:last].partition_broadcast(P))\
                    .then_inc(s(f"ld_idx{n}"), 16)

            def load_l0(half, first, last):
                sp.dma_start(w_l0[:, first:last, :], t["w_l0"][:, first:last, :]).then_inc(s(f"ld_l0_{half}"), 16)

            load_idx(0, 0, COLS0)
            sp.dma_start(cst[:], t["cst"]).then_inc(s("ld_cst"), 16)
            load_idx(1, COLS0, 2 * COLS0)
            load_l0(0, 0, 4)
            load_idx(2, 2 * COLS0, 4 * COLS0)
            load_l0(1, 4, GP)
            load_idx(3, 4 * COLS0, 8 * COLS0)
            sp.dma_start(ident[:], t["ident"]).then_inc(s("ld_ident"), 16)
            sp.dma_start(w_l1[:], t["w_l1"]).then_inc(s("ld_l12"), 16)
            sp.dma_start(w_l2[:], t["w_l2"]).then_inc(s("ld_l12"), 16)
            sp.dma_start(w_fuse12[:], t["w_fuse12"]).then_inc(s("ld_l12"), 16)
            sp.dma_start(bias_l[:], t["bias_l"]).then_inc(s("ld_l12"), 16)
            for half in range(2):
                sp.dma_start(w_raw[:, half, :], t["w_qkv"][half]).then_inc(s("ld_qkv"), 16)
            sp.dma_start(interp[:], t["interp"]).then_inc(s("ld_fuse"), 16)
            sp.dma_start(w_fuse0[:], t["w_fuse0"]).then_inc(s("ld_fuse"), 16)
            sp.wait_ge(s("p_zero"), 2)
            for b in range(B):
                sp.dma_start(hres[0:1, b, 2, :], t["cls"]).then_inc(s("ld_cls"), 16)
                sp.dma_start(coarse[96:97, b, :], t["bf"]).then_inc(s("ld_fuse"), 16)
            sp.dma_start(headmask[:], t["headmask"]).then_inc(s("ld_att"), 16)
            sp.dma_start(blockmask[:], t["blockmask"]).then_inc(s("ld_att"), 16)
            sp.dma_start(bias_v[:], t["bv"].partition_broadcast(P)).then_inc(s("ld_att"), 16)
            sp.dma_start(bias_qk[:], t["bqk"]).then_inc(s("ld_att"), 16)
            sp.dma_start(gbias[:].rearrange("p c e -> p (c e)"), t["gbias"].partition_broadcast(P))\
                .then_inc(s("ld_gate"), 16)
            sp.dma_start(order[:].rearrange("p a n -> p (a n)"), t["order"].partition_broadcast(P))\
                .then_inc(s("ld_gate"), 16)
            sp.wait_ge(s("t_emb0"), STEPS0)
            for n in range(SLICES):
                sp.dma_start(w_ff_raw[:, n, :, :], t["w_ff"][n]).then_inc(s(f"ld_ff{n}"), 16)
            sp.dma_start(w_down[:], t["w_down"]).then_inc(s("ld_down"), 16)

            def write_qk(b, i):
                n = QKT * b + i + 1
                row = 3 * N
                for both in range(2):
                    sp.wait_ge(s("v_qklo") if both else s("a_qkhi"), n)
                    in_q, in_k = (0, 1) if both else (2, 0)
                    start = b * 2 * D * row
                    if i == 0:
                        dst = [start + in_q * N, [row, P]]
                    elif i == 1:
                        dst = [start + D * row + in_k * N, [row, P]]
                    else:
                        dst = [start + P * row + in_q * N, [D * row + (in_k - in_q) * N, 2], [row, D2]]
                    piece = (1 + both) * N
                    sp.dma_start(bass.AP(qk_dram.tensor, dst[0], dst[1:] + [[1, piece]]),
                                 qk_part[:, i, 0:1 + both, :].rearrange("p k n -> p (k n)").bitcast(F32))\
                        .then_inc(s(f"qk_out{b}_{i // 2}"), 16)

            def stack_qk(b, group):
                if group == 0:
                    sp.wait_ge(s("p_stack"), 2 * (b + 1))
                sp.wait_ge(s(f"qk_out{b}_{group}"), 32 * (2 - group))
                heads = slice(EARLY, NH) if group else slice(0, EARLY)
                for i, stack in enumerate((q_stack, k_stack)):
                    rows = qk_dram[b, i, heads.start * HD:heads.stop * HD, :, :]
                    sp.dma_start(stack[0:3 * HD, b, heads, :].bitcast(F32),
                                 rows.rearrange("(h d) k n -> (d k) h n", d=HD))\
                        .then_inc(s(f"stack_in{b}_{group}"), 16)

            def maxima_rows(b):
                for part in range(2):
                    sp.wait_ge(s("v_nm") if part else s("a_nm"), b + 1)
                    sp.dma_start(q_stack[MAXROW + part:MAXROW + part + 1, b, :, 0:TOK].bitcast(F32),
                                 nm_part[:, b, part, :].bitcast(F32))\
                        .then_inc(s(f"nm_in{b}"), 16)

            def store(b, c):
                sp.wait_ge(s("v_acc"), summed(b, E, c))
                sp.dma_start(out[b, 1 + c * P:1 + (c + 1) * P, :], hres[:, b, c, :]).then_inc(s("stored"), 16)

            for b in range(B):
                for i in range(QKT):
                    write_qk(b, i)
                for group in range(2):
                    stack_qk(b, group)
            maxima_rows(0)
            maxima_rows(1)
            sp.wait_ge(s("v_clsrow"), B)
            sp.dma_start(res_cls[:], hres[0:1, :, 2, :]).then_inc(s("cls_in"), 16)
            store(0, 0)
            store(0, 1)
            sp.wait_ge(s("v_outcls"), 1)
            sp.dma_start(out[:, 0, :], out_cls[:]).then_inc(s("stored"), 16)
            store(1, 0)
            store(1, 1)
            sp.wait_ge(s("stored"), 16 * (2 * B + 1))

        @block.gpsimd
        def _(pool):
            pool.memset(hres[:, :, 2, :], 0.0).then_inc(s("p_zero"), 1)
            pool.memset(coarse[:], 0.0).then_inc(s("p_zero"), 1)
            pool.wait_ge(s("v_gidx"), 2)
            for k in range(10):
                dst, src = (got1[:, k, :], t["pix1"]) if k < 8 else (got2[:, k - 8, :], t["pix2"])
                pool.indirect_dma_start(dst, None, src[:, :],
                                        bass.IndirectOffsetOnAxis(ap=gidx[:, k:k + 1], axis=0))\
                    .then_inc(s("gathered"), 16)

            pool.wait_ge(s("ld_qkv"), 32)
            pool.tensor_copy(wq_hi[:], w_raw[:]).then_inc(s("p_split"), 1)
            pool.wait_ge(s("p_split"), 1)
            pool.tensor_tensor(wq_lo[:], w_raw[:], wq_hi[:].bitcast(F32), ALU.subtract)\
                .then_inc(s("p_split"), 1)
            pool.memset(vals[:, :, :, :, HD:HD + 1], 1.0).then_inc(s("p_const"), 1)
            pool.memset(v_block[:], 0.0).then_inc(s("p_const"), 1)
            pool.memset(ones[:], 1.0).then_inc(s("p_const"), 1)
            pool.wait_ge(s("p_split"), 2)
            pool.wait_ge(s("p_const"), 3)
            pool.wait_ge(s("t_picked"), STEPS0)
            for b in range(B):
                pool.memset(k_stack[0:K_STACK, b, :, :].bitcast(F32), 1.0).then_inc(s("p_stack"), 1)
                pool.memset(q_stack[0:K_STACK, b, :, :].bitcast(F32), 0.0).then_inc(s("p_stack"), 1)
            pool.wait_ge(s("p_stack"), 2 * B)
            pool.memset(gexp[:], 0.0).then_inc(s("p_const"), 1)
            pool.wait_ge(s("t_h"), 2)
            pool.memset(clskey_probs[:], 0.0).then_inc(s("p_const"), 1)
            pool.memset(hidden_cls[:], 0.0).then_inc(s("p_const"), 1)

            for n in range(SLICES):
                cols = slice(n * RAW, (n + 1) * RAW)
                pool.wait_ge(s(f"ld_ff{n}"), 16)
                pool.tensor_copy(wf_hi[:, :, cols], w_ff_raw[:, n, :, :]).then_inc(s("p_split"), 1)
                pool.wait_ge(s("p_split"), 2 * n + 3)
                pool.tensor_tensor(wf_lo[:, :, cols], w_ff_raw[:, n, :, :], wf_hi[:, :, cols].bitcast(F32),
                                   ALU.subtract).then_inc(s("p_split"), 1)

            chain = [0]

            def link(ins):
                chain[0] += 1
                ins.then_inc(s("p_chain"), 1)
                pool.wait_ge(s("p_chain"), chain[0])

            def beaten_by(vals_, n, at):
                ge = gge[:, :, 0:n * n].rearrange("p c (i j) -> p c i j", i=n)
                gt = ggt[:, :, 0:n * n].rearrange("p c (i j) -> p c i j", i=n)
                other = vals_.unsqueeze(2).to_broadcast([P, 3, n, n])
                own = vals_.unsqueeze(3).to_broadcast([P, 3, n, n])
                lower, upper = (order[:, k, at:at + n * n].unsqueeze(1).to_broadcast([P, 3, n * n])
                                for k in range(2))
                link(pool.tensor_tensor(ge, other, own, ALU.subtract))
                link(pool.tensor_scalar(gt, ge, 0.0, None, ALU.is_gt))
                link(pool.tensor_scalar(ge, ge, 0.0, None, ALU.is_ge))
                link(pool.tensor_tensor(gge[:, :, 0:n * n], gge[:, :, 0:n * n], lower, ALU.mult))
                link(pool.tensor_tensor(ggt[:, :, 0:n * n], ggt[:, :, 0:n * n], upper, ALU.mult))
                link(pool.tensor_tensor(gge[:, :, 0:n * n], gge[:, :, 0:n * n], ggt[:, :, 0:n * n], ALU.add))
                half = n // 2
                while half > 1:
                    link(pool.tensor_tensor(ge[:, :, :, 0:half], ge[:, :, :, 0:half], ge[:, :, :, half:2 * half],
                                            ALU.add))
                    half //= 2
                link(pool.tensor_tensor(grank[:, :, 0:n], ge[:, :, :, 0], ge[:, :, :, 1], ALU.add))

            def route(b):
                pool.wait_ge(s("v_route"), b + 1)
                if b:
                    pool.wait_ge(s("v_gate"), b)
                beaten_by(ggrp[:], GROUPS, 0)
                link(pool.tensor_scalar(gsel[:], grank[:, :, 0:GROUPS], 2.0, None, ALU.is_lt))
                link(pool.tensor_scalar(gpen[:], gsel[:], -1.0, FAR, ALU.add, ALU.mult))
                link(pool.tensor_tensor(masked, by_group, gsel[:].unsqueeze(3).to_broadcast(wide), ALU.mult))
                link(pool.tensor_tensor(masked, masked, gpen[:].unsqueeze(3).to_broadcast(wide), ALU.add))
                beaten_by(gmsk[:], E, GROUPS * GROUPS)
                link(pool.tensor_scalar(gmsk[:], grank[:], 2.0, None, ALU.is_lt))
                link(pool.tensor_tensor(gpick[:], gmsk[:], gsc[:], ALU.mult))
                link(pool.tensor_tensor(gmsk[:, :, 0:4], gpick[:, :, 0:4], gpick[:, :, 4:8], ALU.add))
                link(pool.tensor_tensor(gmsk[:, :, 0:2], gmsk[:, :, 0:2], gmsk[:, :, 2:4], ALU.add))
                link(pool.tensor_tensor(gsum[:], gmsk[:, :, 0], gmsk[:, :, 1], ALU.add))
                pool.tensor_scalar(gsum[:], gsum[:], 1e-6, None, ALU.add).then_inc(s("p_picked"), 1)

            for b in range(B):
                route(b)

        @block.scalar
        def _(act):
            act.dma_start(pix[:], t["pix"]).then_inc(s("ld_pix"), 16)
            act.dma_start(gidx_raw[:], t["gidx"]).then_inc(s("ld_gidx"), 16)
            nc.scalar.preload_act_table_set(LOG_EXP)

            def one_hot_high(c):
                act.wait_ge(s("v_parts"), 2 * c + 1)
                if c == 0:
                    act.wait_ge(s("ld_cst"), 16)
                else:
                    act.wait_ge(s("a_onehot"), c)
                nc.scalar.activation(apart, hi_idx[:, c % 2, :], ACT.Abs, bias=cst[:, 1:2])\
                    .then_inc(s("a_apart"), 1)
                act.wait_ge(s("a_apart"), c + 1)
                if c >= 2:
                    act.wait_ge(s("t_picked"), c - 1)
                nc.scalar.activation(onehot[:, c % 2, 1, :], apart, ACT.Relu, bias=1.0, scale=-1.0)\
                    .then_inc(s("a_onehot"), 1)

            def got_rows():
                act.wait_ge(s("gathered"), 160)
                for n, (got, f) in enumerate(((got1, F1), (got2, F2))):
                    nc.scalar.activation(got_by_batch[:, n, :, :].rearrange("p b (k f) -> p b k f", f=f),
                                         got[:].rearrange("p k (b f) -> p b k f", b=B), ACT.Copy)\
                        .then_inc(s("a_split"), 1)

            def got_turned():
                act.wait_ge(s("t_got"), 1)
                nc.scalar.activation(got_t[:].rearrange("p a n -> p (a n)"), bank[0:96, 3, :], ACT.Copy)\
                    .then_inc(s("a_got"), 1)

            def embeddings12():
                act.wait_ge(s("t_emb12"), 1)
                act.wait_ge(s("ld_l12"), 64)
                nc.scalar.activation(emb1[:], bank[0:EMB, 4, 0:P], ACT.Identity, bias=bias_l[0:EMB, 1:2])\
                    .then_inc(s("a_emb12"), 1)
                nc.scalar.activation(emb2[:], bank[0:EMB, 4, P:P + B * TOK2], ACT.Identity,
                                     bias=bias_l[0:EMB, 2:3]).then_inc(s("a_emb12"), 1)

            def fused_coarse():
                act.wait_ge(s("t_coarse"), 1)
                act.wait_ge(s("p_zero"), 2)
                nc.scalar.activation(coarse[0:80, :, :].rearrange("p b d -> p (b d)"), bank[0:80, 5, 0:B * D],
                                     ACT.Copy).then_inc(s("a_coarse"), 1)

            for c in range(STEPS0):
                one_hot_high(c)
            got_rows()
            got_turned()
            embeddings12()
            act.wait_ge(s("t_emb0"), STEPS0)
            nc.scalar.activation(emb0[:], bank[:, 2, 0:TOK], ACT.Identity, bias=bias_l[:, 0:1])\
                .then_inc(s("a_emb0"), 1)
            fused_coarse()

            def inv_std(i):
                act.wait_ge(s("v_meanvar"), 3 * (i + 1))
                nc.scalar.activation(logvar[:], meanvar[:, :, 1], ACT.Ln, bias=cst[:, 3:4])\
                    .then_inc(s("a_rstd"), 1)
                act.wait_ge(s("a_rstd"), 2 * i + 1)
                nc.scalar.activation(rstd[:], logvar[:], ACT.Exp, scale=-0.5).then_inc(s("a_rstd"), 1)

            def x_high(i):
                b = i % B
                act.wait_ge(s("t_turned"), i + 1)
                if i >= B:
                    act.wait_ge(s("t_v"), b + 1)
                nc.scalar.activation(xt[:, b, 0, :], bank[:, TURN[i][0], 0:N], ACT.Copy)\
                    .then_inc(s("a_xhi"), 1)
                nc.scalar.activation(xt[:, b, 2, :], bank[:, TURN[i][1], 0:N], ACT.Copy)\
                    .then_inc(s("a_xhi"), 1)

            def qk_high(b, i):
                act.wait_ge(s("v_qk"), QKT * b + i + 1)
                if b:
                    act.wait_ge(s(f"qk_out0_{i // 2}"), 32 * (2 - i // 2))
                nc.scalar.activation(qk_part[:, i, 0, :], qk[:, b, i, :], ACT.Copy)\
                    .then_inc(s("a_qkhi"), 1)

            def cls_softmax(b):
                act.wait_ge(s("v_clsmax"), b + 1)
                nc.scalar.activation(cls_probs[:, b, :], bank[0:NH, CLSB[0], 0:TOK + 1], ACT.Exp,
                                     bias=cls_neg[:, b:b + 1], accum_out=cls_sum[:, b:b + 1])\
                    .then_inc(s("a_cls"), 1)
                nc.scalar.activation(clskey_raw[:, b, :], bank[0:NH, CLSB[1], 0:TOK], ACT.Copy)\
                    .then_inc(s("a_clsraw"), 1)

            def clskey(b):
                act.wait_ge(s("v_clskey"), b + 1)
                act.wait_ge(s("p_const"), 5)
                nc.scalar.activation(clskey_probs[0:NH, b, :], clskey_in[:], ACT.Exp).then_inc(s("a_clskey"), 1)

            def nm_high(b):
                act.wait_ge(s("t_nm"), b + 1)
                act.wait_ge(s("qk_out1_0"), 64)
                act.wait_ge(s("qk_out1_1"), 32)
                nc.scalar.activation(nm_part[:, b, 0, :], bank[0:NH, MISC[b], 0:TOK], ACT.Copy)\
                    .then_inc(s("a_nm"), 1)

            def exps(b, h):
                n = NH * b + h
                act.wait_ge(s("t_scores"), n + 1)
                if n >= PT_RING:
                    act.wait_ge(s("t_pv"), n - PT_RING + 1)
                nc.scalar.activation(probs[:, h % PT_RING, :, :].rearrange("p k n -> p (k n)"),
                                     bank[:, SCORE[b][h % len(SCORE[b])], :], ACT.Exp).then_inc(s("a_exp"), 1)

            def gate_exp(b):
                act.wait_ge(s("t_gate"), b + 1)
                act.wait_ge(s("p_const"), 4)
                if b:
                    act.wait_ge(s("v_route"), 1)
                nc.scalar.activation(gexp[:, 0:2, :].rearrange("p c e -> p (c e)"),
                                     bank[:, GATEB[b], 0:2 * E], ACT.Exp, scale=-1.0)\
                    .then_inc(s("a_gate"), 1)
                nc.scalar.activation(gexp[0:2, 2, :], bank[0:2, GATEB[b], 2 * E:3 * E], ACT.Exp, scale=-1.0)\
                    .then_inc(s("a_gate"), 1)

            def silus(b, k):
                n = (E + 1) * b + k
                act.wait_ge(s("t_up"), 2 * n + 1)
                if n >= 2:
                    act.wait_ge(s("v_gate_up"), n - 1)
                nc.scalar.activation(silu[:, n % 2, :], bank[:, FFB[n % 2][0], 0:N], ACT.Silu)\
                    .then_inc(s("a_silu"), 1)

            inv_std(0)
            x_high(0)
            inv_std(1)
            for i in range(QKT):
                qk_high(0, i)
            x_high(1)
            for i in range(QKT):
                qk_high(1, i)
            cls_softmax(0)
            cls_softmax(1)
            nm_high(0)
            clskey(0)
            for h in range(NH):
                exps(0, h)
                if h == 5:
                    nm_high(1)
                if h == 9:
                    clskey(1)
            for h in range(NH):
                exps(1, h)
                if h == 4:
                    inv_std(2)
                if h == 6:
                    x_high(2)
                if h == 10:
                    gate_exp(0)
            for k in range(E + 1):
                silus(0, k)
                if k == 1:
                    nc.scalar.preload_act_table_set(LOG_EXP)
                    inv_std(3)
                if k == 3:
                    x_high(3)
                if k == 5:
                    gate_exp(1)
            for k in range(E + 1):
                silus(1, k)

        @block.tensor
        def _(pe):
            def project(dst, w, x, weights_move, low_made=None):
                for n, (part, half, xpart) in enumerate(PASSES):
                    if low_made and n in (2, 3):
                        pe.wait_ge(s("v_xlo"), low_made + n - 3)
                    lhs, rhs = (x(xpart), w(part, half)) if weights_move else (w(part, half), x(xpart))
                    ins = pe.matmul(dst, lhs, rhs, start=(n == 0), stop=(n == len(PASSES) - 1))
                return ins

            def pick(c):
                pe.wait_ge(s("v_onehot"), c + 1)
                if c == 0:
                    pe.wait_ge(s("v_pix"), 2)
                if c >= 2:
                    pe.wait_ge(s("v_picked"), c - 1)
                for half in range(2):
                    if half:
                        pe.wait_ge(s("a_onehot"), c + 1)
                    for part in range(2):
                        ins = pe.matmul(bank[0:ROWS0, c % 2, :], pix_part[:, part, half, :],
                                        onehot[:, c % 2, half, :], start=(half + part == 0),
                                        stop=(half + part == 2))
                ins.then_inc(s("t_picked"), 1)

            def embed0(c):
                pe.wait_ge(s("v_picked"), c + 1)
                if c in (0, 2):
                    pe.wait_ge(s(f"ld_l0_{c // 2}"), 16)
                for n in range(2):
                    g = 2 * c + n
                    ins = pe.matmul(bank[:, 2, 0:TOK], w_l0[:, g, :],
                                    picked[0:ROWS0, c % 3, n * TOK:(n + 1) * TOK],
                                    start=(g == 0), stop=(g == GP - 1))
                ins.then_inc(s("t_emb0"), 1)

            def turn_gathered():
                pe.wait_ge(s("ld_ident"), 16)
                pe.wait_ge(s("a_split"), 2)
                for n in range(2 * B):
                    ins = pe.transpose(bank[0:96, 3, n * P:(n + 1) * P], got_by_batch[:, n // B, n % B, :],
                                       ident[:])
                ins.then_inc(s("t_got"), 1)

            def embed12():
                pe.wait_ge(s("a_got"), 1)
                pe.wait_ge(s("ld_l12"), 64)
                for n in range(2):
                    pe.matmul(bank[0:EMB, 4, 0:P], w_l1[:, n, :], got_t[:, 0:2, n * TOK1:(n + 1) * TOK1],
                              start=(n == 0), stop=(n == 1))
                for n in range(8):
                    ins = pe.matmul(bank[0:EMB, 4, P:P + B * TOK2], w_l2[:, n, :],
                                    got_t[:, 2:4, n * TOK2:(n + 1) * TOK2], start=(n == 0), stop=(n == 7))
                ins.then_inc(s("t_emb12"), 1)

            def fuse_coarse():
                pe.wait_ge(s("a_emb12"), 2)
                for b in range(B):
                    pe.matmul(bank[0:TOK1, 5, b * D:(b + 1) * D], emb1[:, b * TOK1:(b + 1) * TOK1],
                              w_fuse12[:, 0, :], start=True, stop=True)
                    ins = pe.matmul(bank[64:64 + TOK2, 5, b * D:(b + 1) * D],
                                    emb2[:, b * TOK2:(b + 1) * TOK2], w_fuse12[:, 1, :],
                                    start=True, stop=True)
                ins.then_inc(s("t_coarse"), 1)

            def fuse_fine(b, c):
                pe.matmul(bank[:, 4 + b, c * D:(c + 1) * D], emb0[:, c * P:(c + 1) * P], w_fuse0[:, b, :],
                          start=True, stop=False)

            def fuse_interp(b, c):
                return pe.matmul(bank[:, 4 + b, c * D:(c + 1) * D], interp[:, c * P:(c + 1) * P],
                                 coarse[:, b, :], start=False, stop=True)

            def fuse():
                pe.wait_ge(s("a_emb0"), 1)
                pe.wait_ge(s("ld_fuse"), 64)
                fuse_fine(0, 0)
                pe.wait_ge(s("a_coarse"), 1)
                for b in range(B):
                    if b:
                        fuse_fine(b, 0)
                    fuse_interp(b, 0)
                    fuse_fine(b, 1)
                    fuse_interp(b, 1).then_inc(s("t_h"), 1)

            def turn(i):
                pe.wait_ge(s("v_xn"), 4 * (i + 1))
                for c in range(3):
                    rows = P if c < 2 else 2
                    cols = slice(c * P, c * P + rows)
                    pe.transpose(bank[:, TURN[i][0], cols], xn[0:rows, c, 0:P], ident[0:rows, 0:rows])
                    ins = pe.transpose(bank[:, TURN[i][1], cols], xn[0:rows, c, P:], ident[0:rows, 0:rows])
                ins.then_inc(s("t_turned"), 1)

            def w_att(cols):
                return lambda part, half: (wq_lo if part else wq_hi)[:, half, cols]

            def w_ffn(cols):
                return lambda part, half: (wf_lo if part else wf_hi)[:, half, cols]

            def x_of(b, cols):
                return lambda part: xt[:, b, part, cols]

            def proj_qk(b, i):
                if i == 0:
                    pe.wait_ge(s("a_xhi"), 2 * (b + 1))
                    pe.wait_ge(s("p_split"), 2)
                if b:
                    pe.wait_ge(s("v_qk"), i + 1)
                cols = slice(i * P, (i + 1) * P)
                project(bank[:, QKB[i], 0:N], w_att(cols), x_of(b, slice(0, N)), False,
                        2 * (b + 1) if i == 0 else None)\
                    .then_inc(s("t_qk"), 1)

            def proj_v(b):
                cols = slice(2 * D, 3 * D)
                for c in range(CHUNKS):
                    ins = project(bank[:, VB[b], c * D:(c + 1) * D], w_att(cols),
                                  x_of(b, slice(c * P, (c + 1) * P)), True)
                ins.then_inc(s("t_v"), 1)
                if b == 0:
                    pe.wait_ge(s("v_xlo"), 4)
                    project(bank[0:NH, 7, 0:D], w_att(cols),
                            lambda part: xt[:, 0, part, CLS:CLS + 1].to_broadcast([P, NH]), True)\
                        .then_inc(s("t_vcls"), 1)
                    pe.wait_ge(s("v_qk"), QKT)
                    for to in (0, D2):
                        ins = pe.matmul(bank[to:to + D2, 7, TOK:TOK + 1], ident[:, D2 - to:P - to],
                                        qk[:, 0, 2, CLS:CLS + 1], start=True, stop=True)
                    ins.then_inc(s("t_clsrest"), 1)

            def cls_scores(b):
                pe.wait_ge(s("v_qk"), QKT * (b + 1))
                pe.wait_ge(s("v_clsblk"), 4)
                pe.wait_ge(s("v_v"), 2)
                pe.wait_ge(s("v_vcls"), 1)
                if b:
                    pe.wait_ge(s("a_cls"), b)
                    pe.wait_ge(s("a_clsraw"), b)
                for half in range(2):
                    pe.matmul(bank[0:NH, CLSB[0], 0:N], q_cls[:, half, :], qk[:, b, 1 + half, :],
                              start=(half == 0), stop=(half == 1))
                for half in range(2):
                    ins = pe.matmul(bank[0:NH, CLSB[1], 0:TOK], k_cls[:, half, :], qk[:, b, 2 * half, 0:TOK],
                                    start=(half == 0), stop=(half == 1))
                ins.then_inc(s("t_clsscores"), 1)

            def scores_for_max(b, u):
                n = UNITS * b + u
                c, pair = MAX_UNITS[u]
                if u in (0, EARLY):
                    pe.wait_ge(s(f"stack_in{b}_{u // EARLY}"), 32)
                if u == 0:
                    pe.wait_ge(s("p_stack"), 4)
                if n == 0:
                    pe.wait_ge(s("v_v"), 4)
                    pe.wait_ge(s("v_qk"), 2 * QKT)
                if b or n >= 3:
                    pe.wait_ge(s("v_max"), n - (1 if b else 2))
                for j in range(2):
                    h = 2 * pair + j
                    ins = pe.matmul(bank[:, MAXB[b][u % len(MAXB[b])] + j, 0:N],
                                    q_stack[0:K_STACK, b, h, c * P:(c + 1) * P],
                                    k_stack[0:K_STACK, b, h, :], start=True, stop=True)
                ins.then_inc(s("t_formax"), 1)

            def turn_maxima(b):
                pe.wait_ge(s("v_max"), UNITS * (b + 1))
                pe.wait_ge(s("a_clsraw"), B)
                for c in range(CHUNKS):
                    ins = pe.transpose(bank[0:NH, MISC[b], c * P:(c + 1) * P], negmax[:, b, c, :], ident[:])
                ins.then_inc(s("t_nm"), 1)

            def scores(b, h):
                n = NH * b + h
                if h == 0:
                    pe.wait_ge(s(f"nm_in{b}"), 32)
                if h >= len(SCORE[b]):
                    pe.wait_ge(s("a_exp"), n - len(SCORE[b]) + 1)
                elif b and h:
                    pe.wait_ge(s("a_exp"), NH - 2 + h)
                for c in range(CHUNKS):
                    ins = pe.matmul(bank[:, SCORE[b][h % len(SCORE[b])], c * TOK:(c + 1) * TOK],
                                    k_stack[0:K_STACK, b, h, c * P:(c + 1) * P],
                                    q_stack[0:K_STACK, b, h, 0:TOK], start=True, stop=True)
                ins.then_inc(s("t_scores"), 1)

            def weigh(b, h):
                n = NH * b + h
                g, j = divmod(h, 4)
                if j == 0:
                    pe.wait_ge(s("a_clskey"), b + 1)
                    if b == 0 and g == 0:
                        pe.wait_ge(s("v_vcls"), 3)
                    if g == 1 and b == 0:
                        pe.wait_ge(s("v_max"), B * UNITS)
                    if g == 1 and b == 1:
                        pe.wait_ge(s("v_attn_t"), 2)
                    if g == 2:
                        pe.wait_ge(s("v_attn_t"), 3 * b + 1)
                    pe.matmul(bank[:, ACC_OF[b][g], 0:TOK],
                              v_block[:, 4 * g:4 * g + 4, :].rearrange("p j m -> p (j m)"),
                              clskey_probs[:, b, :], start=True, stop=False, skip_group_check=True)
                pe.wait_ge(s("a_exp"), n + 1)
                for c in range(CHUNKS):
                    ins = pe.matmul(bank[32 * j:32 * j + HD + 1, ACC_OF[b][g], 0:TOK], vals[:, b, c, h, :],
                                    probs[:, h % PT_RING, c, :], start=False, stop=(c == CHUNKS - 1),
                                    skip_group_check=True)
                ins.then_inc(s("t_pv"), 1)

            def cls_turn(b):
                pe.wait_ge(s("v_clskey"), b + 1)
                pe.wait_ge(s("a_cls"), b + 1)
                for c in range(CHUNKS):
                    ins = pe.transpose(bank[:, MISC[b], c * NH:(c + 1) * NH], cls_probs[:, b, c * P:(c + 1) * P],
                                       ident[0:NH, 0:NH])
                ins.then_inc(s("t_clsprobs"), 1)

            def cls_weigh(b):
                pe.wait_ge(s("v_clsprobs"), b + 1)
                for c in range(CHUNKS):
                    ins = pe.matmul(bank[0:NH, MISC[b], 0:D], cls_probs_t[:, c * NH:(c + 1) * NH],
                                    vals[:, b, c, :, 0:HD], start=(c == 0), stop=(c == CHUNKS - 1))
                ins.then_inc(s("t_clssum"), 1)

            def cls_row(b):
                pe.wait_ge(s("v_clssum"), 2 * (b + 1))
                pe.wait_ge(s("p_const"), 3)
                pe.matmul(bank[0:1, MISC[b], 0:D], ones[:, 0:1], cls_sumv[:, 1, :], start=True, stop=True)\
                    .then_inc(s("t_clsrow"), 1)

            def turn_attn(b):
                pe.wait_ge(s("v_attn_t"), 3 * (b + 1))
                pe.wait_ge(s("v_clsrow"), b + 1)
                for c, into in enumerate((MISC[b], ACC[b])):
                    for g in range(3):
                        ins = pe.transpose(bank[:, into, g * P:(g + 1) * P], attn_t[:, g, c * P:(c + 1) * P],
                                           ident[:])
                    ins.then_inc(s("t_attn"), 1)

            def gate(b):
                pe.wait_ge(s("a_xhi"), 2 * (B + b + 1))
                pe.wait_ge(s("v_xlo"), 2 * (B + b + 1))
                pe.wait_ge(s("p_split"), 10)
                cols = slice(GATE, GATE + E)
                for c in range(3):
                    rows = P if c < 2 else 2
                    ins = project(bank[0:rows, GATEB[b], c * E:(c + 1) * E], w_ffn(cols),
                                  x_of(b, slice(c * P, c * P + rows)), True)
                ins.then_inc(s("t_gate"), 1)

            def cls_shares(b):
                pe.wait_ge(s("v_gate"), b + 1)
                pe.wait_ge(s("v_xlo"), 2 * B * B)
                pe.matmul(bank[:, SHAREB, b * E:(b + 1) * E], ones[0:1, :], cw[0:1, b, 2, :],
                          start=True, stop=True).then_inc(s("t_share"), 1)

            def up(b, k):
                n = (E + 1) * b + k
                if n == 0:
                    pe.wait_ge(s("a_exp"), B * NH - 2)
                    pe.wait_ge(s("v_attn_t"), 5)
                if n == 1:
                    pe.wait_ge(s("a_exp"), B * NH)
                if n >= 2:
                    pe.wait_ge(s("v_gate_up"), n - 1)
                if k == 0:
                    pe.wait_ge(s("v_xlo"), 2 * (B + b + 1))
                for j in range(2):
                    cols = slice((2 * k + j) * INTER, (2 * k + j + 1) * INTER)
                    project(bank[:, FFB[n % 2][j], 0:N], w_ffn(cols), x_of(b, slice(0, N)), False)\
                        .then_inc(s("t_up"), 1)

            def down(b, k):
                n = (E + 1) * b + k
                pe.wait_ge(s("v_gate_up"), n + 1)
                if n == 0:
                    pe.wait_ge(s("ld_down"), 16)
                if n == 1:
                    pe.wait_ge(s("a_gate"), 2)
                if n >= 3:
                    pe.wait_ge(s("v_acc"), summed(*divmod(n - 3, E + 1), 1))
                for c in range(CHUNKS):
                    ins = pe.matmul(bank[:, YB[n % 3], c * D:(c + 1) * D], hidden[:, b, k, c * P:(c + 1) * P],
                                    w_down[:, k, :], start=True, stop=True)
                ins.then_inc(s("t_down"), 1)

            def down_cls():
                pe.wait_ge(s("a_gate"), 2 * B)
                pe.wait_ge(s("v_hcls"), 2 * B)
                for k in range(E + 1):
                    at = 32 * (k % 4)
                    ins = pe.matmul(bank[at:at + 32, YCLS, 0:D], hidden_cls[:, k, :], w_down[:, k, :],
                                    start=(k < 4), stop=(k > E - 4), skip_group_check=True)
                ins.then_inc(s("t_downcls"), 1)

            def sum_cls():
                pe.wait_ge(s("v_downcls"), 1)
                pe.matmul(bank[0:B, YCLS, 0:D], cst[:, 4:4 + B], down_rows[:], start=True, stop=True)\
                    .then_inc(s("t_sumcls"), 1)

            for c in range(STEPS0):
                pick(c)
                if c == STEPS0 - 1:
                    turn_gathered()
                if c >= 1:
                    embed0(c - 1)
            embed12()
            embed0(STEPS0 - 1)
            fuse_coarse()
            fuse()
            turn(0)
            proj_qk(0, 0)
            proj_qk(0, 1)
            proj_qk(0, 2)
            turn(1)
            proj_v(0)
            for i in range(QKT):
                proj_qk(1, i)
            proj_v(1)
            cls_scores(0)
            for u in range(UNITS):
                scores_for_max(0, u)
                if u == 3:
                    cls_scores(1)
            turn_maxima(0)
            for u in range(AHEAD):
                scores_for_max(1, u)
            for h in range(NH + 2):
                if h < NH:
                    scores(0, h)
                else:
                    scores(1, h - NH)
                if AHEAD + 2 * h < UNITS:
                    scores_for_max(1, AHEAD + 2 * h)
                if h >= 2:
                    weigh(0, h - 2)
                if AHEAD + 2 * h + 1 < UNITS:
                    scores_for_max(1, AHEAD + 2 * h + 1)
                if h == 4:
                    turn_maxima(1)
                    cls_turn(0)
                if h == 6:
                    cls_weigh(0)
                if h == 10:
                    cls_row(0)
            for h in range(2, NH + 2):
                if h < NH:
                    scores(1, h)
                if h == 2:
                    turn_attn(0)
                if h >= 2:
                    weigh(1, h - 2)
                if h == 4:
                    cls_turn(1)
                if h == 6:
                    turn(2)
                if h == 7:
                    cls_weigh(1)
                if h == 10:
                    gate(0)
                if h == 11:
                    cls_row(1)
                    up(0, 0)
            for n in range(B * (E + 1)):
                if n == 0:
                    turn_attn(1)
                else:
                    up(*divmod(n, E + 1))
                if n in (2, 3):
                    down(0, n - 2)
                if n == 3:
                    turn(3)
                if n == 6:
                    gate(1)
                if n == 15:
                    cls_shares(0)
                    cls_shares(1)
                if n >= LAG + 2:
                    down(*divmod(n - LAG, E + 1))
            for n in range(B * (E + 1) - LAG, B * (E + 1) - 1):
                down(*divmod(n, E + 1))
                if n == B * (E + 1) - 3:
                    down_cls()
            sum_cls()
            down(B - 1, E)

        @block.vector
        def _(dve):
            v = nc.vector
            dve.wait_ge(s("ld_gidx"), 16)
            for cols, last in ((slice(0, 8), TOK1 * GP - 1), (slice(8, 10), TOK2 * GP - 1)):
                v.tensor_scalar(gidx[:, cols], gidx_raw[:, cols], last, None, ALU.bitwise_and)\
                    .then_inc(s("v_gidx"), 1)
            dve.wait_ge(s("ld_pix"), 16)
            v.tensor_copy(pix_part[:, 0], pix[:]).then_inc(s("v_pix"), 1)
            dve.wait_ge(s("v_pix"), 1)
            v.tensor_tensor(pix_part[:, 1], pix[:], pix_part[:, 0].bitcast(F32), ALU.subtract)\
                .then_inc(s("v_pix"), 1)

            def one_hot(c):
                cols = slice(c * COLS0, (c + 1) * COLS0)
                if c in (0, 1, 2, 4):
                    dve.wait_ge(s(f"ld_idx{(0, 1, 2, 0, 3)[c]}"), 16)
                if c >= 2:
                    dve.wait_ge(s("v_onehot"), c - 1)
                    dve.wait_ge(s("a_apart"), c - 1)
                v.tensor_scalar(hi_idx[:, c % 2, :], idx_all[:, cols], NPIX - 1, 4, ALU.bitwise_and,
                                ALU.logical_shift_right).then_inc(s("v_parts"), 1)
                if c >= 2:
                    dve.wait_ge(s("v_picked"), c - 1)
                v.tensor_scalar(lo_idx[:, c % 2, :], idx_all[:, cols], LOW - 1, None, ALU.bitwise_and)\
                    .then_inc(s("v_parts"), 1)
                dve.wait_ge(s("v_parts"), 2 * c + 1)
                if c == 0:
                    dve.wait_ge(s("ld_cst"), 16)
                if c >= 2:
                    dve.wait_ge(s("t_picked"), c - 1)
                v.tensor_scalar(onehot[:, c % 2, 0, :], hi_idx[:, c % 2, :], cst[:, 0:1], None, ALU.is_equal)\
                    .then_inc(s("v_onehot"), 1)

            def choose(c):
                dve.wait_ge(s("t_picked"), c + 1)
                dve.wait_ge(s("v_parts"), 2 * c + 2)
                if c >= 3:
                    dve.wait_ge(s("t_emb0"), c - 2)
                v.scalar_tensor_tensor(out=picked[0:ROWS0, c % 3, :], in0=lo_idx[0:ROWS0, c % 2, :],
                                       scalar=cst[0:ROWS0, 2:3], in1=bank[0:ROWS0, c % 2, :],
                                       op0=ALU.is_equal, op1=ALU.mult).then_inc(s("v_picked"), 1)

            for c in range(STEPS0):
                one_hot(c)
                if c >= 1:
                    choose(c - 1)
            choose(STEPS0 - 1)

            def take_h(b):
                dve.wait_ge(s("t_h"), b + 1)
                v.tensor_copy(hres[:, b, 0:2, :].rearrange("p c d -> p (c d)"), bank[:, 4 + b, 0:2 * D])\
                    .then_inc(s("v_h"), 1)

            def mean_var(i):
                b = i % B
                if i < B:
                    dve.wait_ge(s("t_h"), b + 1)
                    dve.wait_ge(s("ld_cls"), 32)
                else:
                    dve.wait_ge(s("v_hattn"), 2 * (b + 1))
                    dve.wait_ge(s("v_clsrow"), b + 1)
                if i:
                    dve.wait_ge(s("v_xn"), 4 * i)
                for c in range(3):
                    h = bank[:, 4 + b, c * D:(c + 1) * D] if i < B and c < CHUNKS else hres[:, b, c, :]
                    v.bn_stats(stats[:, c, :], h).then_inc(s("v_stats"), 1)
                for c in range(3):
                    dve.wait_ge(s("v_stats"), 3 * i + c + 1)
                    v.bn_aggr(meanvar[:, c, :], stats[:, c, :]).then_inc(s("v_meanvar"), 1)

            def normalise(i):
                b = i % B
                dve.wait_ge(s("a_rstd"), 2 * (i + 1))
                if i < B:
                    dve.wait_ge(s("v_h"), b + 1)
                if i:
                    dve.wait_ge(s("t_turned"), i)
                for c in range(3):
                    v.tensor_scalar(xn[:, c, 0:D], hres[:, b, c, :], meanvar[:, c, 0:1], rstd[:, c:c + 1],
                                    ALU.subtract, ALU.mult).then_inc(s("v_xn"), 1)
                dve.wait_ge(s("v_xn"), 4 * i + 3)
                v.tensor_copy(xn[:, :, D:], xn[:, :, P:D]).then_inc(s("v_xn"), 1)

            def x_low(i):
                b = i % B
                dve.wait_ge(s("a_xhi"), 2 * (i + 1))
                v.tensor_tensor(xt[:, b, 1, :], bank[:, TURN[i][0], 0:N], xt[:, b, 0, :].bitcast(F32),
                                ALU.subtract).then_inc(s("v_xlo"), 1)
                v.tensor_tensor(xt[D2:P, b, 2, :], bank[D2:P, TURN[i][1], 0:N],
                                xt[D2:P, b, 2, :].bitcast(F32), ALU.subtract).then_inc(s("v_xlo"), 1)

            def take_qk(b, i):
                if b == 0 and i == 0:
                    dve.wait_ge(s("ld_att"), 64)
                dve.wait_ge(s("t_qk"), QKT * b + i + 1)
                v.tensor_scalar(qk[:, b, i, :], bank[:, QKB[i], 0:N], bias_qk[:, i:i + 1], cst[:, 6 + i:7 + i],
                                ALU.add, ALU.mult).then_inc(s("v_qk"), 1)

            def qk_low(b, i):
                dve.wait_ge(s("a_qkhi"), QKT * b + i + 1)
                v.tensor_tensor(qk_part[:, i, 1, :], qk[:, b, i, :], qk_part[:, i, 0, :].bitcast(F32),
                                ALU.subtract)\
                    .then_inc(s("v_qklo"), 1)

            def take_v(b):
                dve.wait_ge(s("t_v"), b + 1)
                dve.wait_ge(s("p_const"), 1)
                for c in range(CHUNKS):
                    v.tensor_tensor(vals[:, b, c, :, 0:HD],
                                    bank[:, VB[b], c * D:(c + 1) * D].rearrange("p (h d) -> p h d", h=NH),
                                    bias_v[:].rearrange("p (h d) -> p h d", h=NH), ALU.add)\
                        .then_inc(s("v_v"), 1)

            def cls_blocks():
                dve.wait_ge(s("t_clsrest"), 1)
                v.tensor_copy(cls_rest[:], bank[:, 7, TOK:TOK + 1]).then_inc(s("v_clsrest"), 1)
                dve.wait_ge(s("v_qk"), QKT)
                for dst, first in ((q_cls, 0), (k_cls, 1)):
                    v.tensor_scalar(dst[:, 0, :], headmask[:, 0, :], qk[:, 0, first, CLS:CLS + 1], None,
                                    ALU.mult).then_inc(s("v_clsblk"), 1)
                dve.wait_ge(s("v_clsrest"), 1)
                for dst, mask in ((q_cls, 1), (k_cls, 2)):
                    v.tensor_scalar(dst[:, 1, :], headmask[:, mask, :], cls_rest[:, 0:1], None, ALU.mult)\
                        .then_inc(s("v_clsblk"), 1)
                dve.wait_ge(s("t_vcls"), 1)
                v.tensor_tensor(v_cls[:], bank[0:NH, 7, 0:D], bias_v[0:NH, :], ALU.add)\
                    .then_inc(s("v_vcls"), 1)
                dve.wait_ge(s("v_vcls"), 1)
                dve.wait_ge(s("p_const"), 2)
                v.tensor_tensor(v_block[0:NH, :, 0:HD], v_cls[:].rearrange("p (h d) -> p h d", h=NH),
                                blockmask[:].rearrange("p (h d) -> p h d", h=NH), ALU.mult)\
                    .then_inc(s("v_vcls"), 1)
                dve.wait_ge(s("ld_ident"), 16)
                v.tensor_copy(v_block[0:NH, :, HD], ident[0:NH, 0:NH]).then_inc(s("v_vcls"), 1)

            def cls_max(b):
                dve.wait_ge(s("t_clsscores"), b + 1)
                v.tensor_reduce(cls_neg[:, b:b + 1], bank[0:NH, CLSB[0], 0:TOK + 1], AX.X, ALU.max,
                                negate=True).then_inc(s("v_clsmax"), 1)

            def maxima(b, u):
                n = UNITS * b + u
                c, pair = MAX_UNITS[u]
                dve.wait_ge(s("t_formax"), n + 1)
                two = MAXB[b][u % len(MAXB[b])]
                v.tensor_reduce(negmax[:, b, c, 2 * pair:2 * pair + 2], bank[:, two:two + 2, 0:TOK + 1],
                                AX.X, ALU.max, negate=True).then_inc(s("v_max"), 1)

            def nm_parts(b):
                src = bank[0:NH, MISC[b], 0:TOK]
                dve.wait_ge(s("a_nm"), b + 1)
                v.tensor_tensor(nm_part[:, b, 1, :], src, nm_part[:, b, 0, :].bitcast(F32), ALU.subtract)\
                    .then_inc(s("v_nm"), 1)

            def clskey_arg(b):
                dve.wait_ge(s("a_clsraw"), b + 1)
                if b:
                    dve.wait_ge(s("a_clskey"), b)
                v.tensor_tensor(clskey_in[:], bank[0:NH, MISC[b], 0:TOK], clskey_raw[:, b, :], ALU.add)\
                    .then_inc(s("v_clskey"), 1)

            def take_attn(b, g):
                dve.wait_ge(s("t_pv"), NH * b + 4 * (g + 1))
                if b:
                    dve.wait_ge(s("t_attn"), 2 * b)
                v.tensor_copy(attn_t[:, g, :], bank[:, ACC_OF[b][g], 0:TOK]).then_inc(s("v_attn_t"), 1)

            def cls_probs_copy(b):
                dve.wait_ge(s("t_clsprobs"), b + 1)
                v.tensor_copy(cls_probs_t[:], bank[:, MISC[b], 0:CHUNKS * NH]).then_inc(s("v_clsprobs"), 1)
                v.reciprocal(cls_rsum[:, b:b + 1], cls_sum[:, b:b + 1]).then_inc(s("v_clsrsum"), 1)

            def cls_sums(b):
                dve.wait_ge(s("t_clssum"), b + 1)
                v.scalar_tensor_tensor(out=cls_sumv[:, 0, :], in0=v_cls[:], scalar=cls_probs[:, b, CLS:CLS + 1],
                                       in1=bank[0:NH, MISC[b], 0:D], op0=ALU.mult, op1=ALU.add)\
                    .then_inc(s("v_clssum"), 1)
                dve.wait_ge(s("v_clssum"), 2 * b + 1)
                dve.wait_ge(s("v_clsrsum"), b + 1)
                v.scalar_tensor_tensor(out=cls_sumv[:, 1, :], in0=cls_sumv[:, 0, :], scalar=cls_rsum[:, b:b + 1],
                                       in1=blockmask[:], op0=ALU.mult, op1=ALU.mult)\
                    .then_inc(s("v_clssum"), 1)

            def cls_add(b):
                dve.wait_ge(s("t_clsrow"), b + 1)
                row = hres[0:1, b, 2, :]
                v.tensor_tensor(row, bank[0:1, MISC[b], 0:D], row, ALU.add).then_inc(s("v_clsrow"), 1)

            def add_attn(b):
                for c, into in enumerate((MISC[b], ACC[b])):
                    n = 2 * b + c
                    dve.wait_ge(s("t_attn"), n + 1)
                    src = bank[:, into, 0:3 * P].rearrange("p (h m) -> p h m", h=NH)
                    v.reciprocal(rsum[:, c, :], src[:, :, HD]).then_inc(s("v_rsum"), 1)
                    dve.wait_ge(s("v_rsum"), n + 1)
                    v.tensor_tensor(attn[:, c, :].rearrange("p (h d) -> p h d", h=NH), src[:, :, 0:HD],
                                    rsum[:, c, :].unsqueeze(2).to_broadcast([P, NH, HD]), ALU.mult)\
                        .then_inc(s("v_attn"), 1)
                for c in range(CHUNKS):
                    dve.wait_ge(s("v_attn"), 2 * b + c + 1)
                    v.tensor_tensor(hres[:, b, c, :], hres[:, b, c, :], attn[:, c, :], ALU.add)\
                        .then_inc(s("v_hattn"), 1)

            chain = [0]

            def link(ins):
                chain[0] += 1
                ins.then_inc(s("v_chain"), 1)
                dve.wait_ge(s("v_chain"), chain[0])

            def route_scores(b):
                dve.wait_ge(s("a_gate"), 2 * (b + 1))
                dve.wait_ge(s("ld_gate"), 32)
                if b:
                    dve.wait_ge(s("p_picked"), b)
                link(v.tensor_scalar(gden[:], gexp[:], 1.0, None, ALU.add))
                link(v.reciprocal(gsc[:], gden[:]))
                link(v.tensor_tensor(gsb[:], gsc[:], gbias[:], ALU.add))
                v.tensor_tensor(ggrp[:], by_group[:, :, :, 0], by_group[:, :, :, 1], ALU.add)\
                    .then_inc(s("v_route"), 1)

            def shares(b):
                dve.wait_ge(s("p_picked"), b + 1)
                link(v.reciprocal(grsum[:], gsum[:]))
                v.tensor_tensor(cw[:, b, :, :], gpick[:], grsum[:].unsqueeze(2).to_broadcast([P, 3, E]), ALU.mult)\
                    .then_inc(s("v_gate"), 1)

            def gate_up(b, k):
                n = (E + 1) * b + k
                dve.wait_ge(s("a_silu"), n + 1)
                dve.wait_ge(s("t_up"), 2 * n + 2)
                v.tensor_tensor(hidden[:, b, k, :], bank[:, FFB[n % 2][1], 0:N], silu[:, n % 2, :], ALU.mult)\
                    .then_inc(s("v_gate_up"), 1)

            def add_down(b, k):
                dve.wait_ge(s("t_down"), (E + 1) * b + k + 1)
                y = bank[:, YB[((E + 1) * b + k) % 3], 0:CHUNKS * D]
                if k == 0:
                    res = hres[:, b, 0:2, :].rearrange("p c d -> p (c d)")
                    v.tensor_tensor(res, y, res, ALU.add).then_inc(s("v_acc"), 1)
                    return
                dve.wait_ge(s("v_gate"), b + 1)
                for c in range(CHUNKS):
                    dve.wait_ge(s("v_acc"), summed(b, k - 1, c))
                    v.scalar_tensor_tensor(out=hres[:, b, c, :], in0=y[:, c * D:(c + 1) * D],
                                           scalar=cw[:, b, c, k - 1:k], in1=hres[:, b, c, :],
                                           op0=ALU.mult, op1=ALU.add).then_inc(s("v_acc"), 1)

            def share_cls(b):
                dve.wait_ge(s("t_share"), b + 1)
                dve.wait_ge(s("v_gate_up"), (E + 1) * (b + 1))
                dve.wait_ge(s("p_const"), 6)
                v.tensor_copy(hidden_cls[:, 0, b:b + 1], hidden[:, b, 0, CLS:CLS + 1]).then_inc(s("v_hcls"), 1)
                v.tensor_tensor(hidden_cls[:, 1:, b], hidden[:, b, 1:, CLS], bank[:, SHAREB, b * E:(b + 1) * E],
                                ALU.mult).then_inc(s("v_hcls"), 1)

            mean_var(0)
            take_h(0)
            normalise(0)
            mean_var(1)
            take_h(1)
            x_low(0)
            normalise(1)
            take_qk(0, 0)
            take_qk(0, 1)
            qk_low(0, 0)
            take_qk(0, 2)
            qk_low(0, 1)
            qk_low(0, 2)
            x_low(1)
            take_v(0)
            cls_blocks()
            for i in range(QKT):
                take_qk(1, i)
            take_v(1)
            for i in range(QKT):
                qk_low(1, i)
            cls_max(0)
            for u in range(UNITS):
                maxima(0, u)
                if u == 3:
                    cls_max(1)
            nm_parts(0)
            maxima(1, 0)
            maxima(1, 1)
            clskey_arg(0)
            for u in range(2, UNITS):
                maxima(1, u)
            take_attn(0, 0)
            nm_parts(1)
            clskey_arg(1)
            cls_probs_copy(0)
            cls_sums(0)
            take_attn(0, 1)
            cls_add(0)
            take_attn(0, 2)
            add_attn(0)
            mean_var(2)
            take_attn(1, 0)
            normalise(2)
            cls_probs_copy(1)
            x_low(2)
            take_attn(1, 1)
            cls_sums(1)
            route_scores(0)
            cls_add(1)
            take_attn(1, 2)
            gate_up(0, 0)
            add_attn(1)
            mean_var(3)
            gate_up(0, 1)
            normalise(3)
            gate_up(0, 2)
            gate_up(0, 3)
            x_low(3)
            for n in range(4, B * (E + 1)):
                gate_up(*divmod(n, E + 1))
                if n == 6:
                    shares(0)
                if n == 7:
                    route_scores(1)
                if n == 14:
                    shares(1)
                if n == 16:
                    share_cls(0)
                if n >= LAG:
                    add_down(*divmod(n - LAG, E + 1))
            share_cls(1)
            for n in range(B * (E + 1) - LAG, B * (E + 1) - 1):
                add_down(*divmod(n, E + 1))
                if n == B * (E + 1) - 3:
                    dve.wait_ge(s("t_downcls"), 1)
                    v.tensor_copy(down_rows[:], bank[:, YCLS, 0:D]).then_inc(s("v_downcls"), 1)
            dve.wait_ge(s("t_sumcls"), 1)
            dve.wait_ge(s("cls_in"), 16)
            v.tensor_tensor(out_cls[:], bank[0:B, YCLS, 0:D], res_cls[:], ALU.add).then_inc(s("v_outcls"), 1)
            add_down(B - 1, E)


def kernel(**x):
    import numpy as np
    import concourse.bacc as bacc
    from concourse import mybir as _mybir
    from concourse.bass_utils import run_bass_kernel_spmd

    a = {k: np.asarray(v) for k, v in x.items()}
    f32 = np.float32

    def rows_twice(w):
        return np.stack([w[:P], np.concatenate([w[P:], w[P:]])])

    def pad_rows(w):
        return np.concatenate([w, np.zeros((P - w.shape[0],) + w.shape[1:], w.dtype)])

    img = a["x"]

    def patches(p):
        h = img.shape[2] // p
        q = img.reshape(B, CH, h, p, h, p).transpose(2, 4, 0, 3, 5, 1)
        return q.reshape(h * h, B * p * p * CH)

    t = {}
    t["pix"] = patches(1).reshape(2, P, LOW, B * CH).transpose(1, 0, 3, 2).reshape(P, 2, ROWS0)
    t["pix1"] = patches(2)
    t["pix2"] = patches(4)
    t["idx0"] = a["L0_tok_idx0"].reshape(TOK, GP).T.reshape(-1)
    idx1 = a["L0_tok_idx1"].reshape(TOK1, 2, 8).transpose(1, 0, 2).reshape(P, 8)
    idx2 = a["L0_tok_idx2"].reshape(TOK2, 8, 2).transpose(1, 0, 2).reshape(P, 2)
    t["gidx"] = np.concatenate([idx1, idx2], axis=1)
    w0 = a["L0_tok_W0"].reshape(EMB, GP, CH).transpose(2, 1, 0)
    big = np.zeros((B, CH, LOW, GP, B, EMB), f32)
    for b in range(B):
        big[b, :, :, :, b, :] = w0[:, None]
    t["w_l0"] = big.reshape(ROWS0, GP, B * EMB)
    t["w_l1"] = a["L0_tok_W1"].T.reshape(2, 96, EMB).transpose(1, 0, 2)
    t["w_l2"] = a["L0_tok_W2"].T.reshape(8, 96, EMB).transpose(1, 0, 2)
    b0 = a["L0_tok_b0"]
    t["bias_l"] = np.stack([np.concatenate([b0, b0]), pad_rows(a["L0_tok_b1"]), pad_rows(a["L0_tok_b2"])], axis=1)
    wf = a["L0_tok_Wf"].T.reshape(3, EMB, D)
    zero = np.zeros((EMB, D), f32)
    t["w_fuse0"] = np.stack([np.concatenate([wf[0], zero]), np.concatenate([zero, wf[0]])], axis=1)
    t["w_fuse12"] = wf[1:].transpose(1, 0, 2)
    t["bf"] = a["L0_tok_bf"][None]
    interp = np.zeros((P, TOK), f32)
    for at, n in ((0, TOK1), (64, TOK2)):
        pos = np.clip((np.arange(TOK) + 0.5) * (n / TOK) - 0.5, 0.0, n - 1)
        lo = np.floor(pos).astype(int)
        hi = np.minimum(lo + 1, n - 1)
        for i in range(TOK):
            interp[at + lo[i], i] += 1.0 - (pos[i] - lo[i])
            interp[at + hi[i], i] += pos[i] - lo[i]
    interp[96] = 1.0
    t["interp"] = interp
    t["cls"] = a["cls_tok"].reshape(1, D)
    wq, wk, bq, bk = a["L0_attn_Wq"], a["L0_attn_Wk"], a["L0_attn_bq"], a["L0_attn_bk"]
    wqkv = np.concatenate([wq[:P], wk[:P], wq[P:], wk[P:], a["L0_attn_Wv"]]).T
    t["w_qkv"] = rows_twice(wqkv)
    t["bqk"] = np.stack([bq[:P], bk[:P], np.concatenate([bq[P:], bk[P:]])], axis=1)
    t["bv"] = a["L0_attn_bv"]
    ups = np.stack([np.concatenate([a["L0_ffn_sw1"][None], a["L0_ffn_w1"]]),
                    np.concatenate([a["L0_ffn_sw3"][None], a["L0_ffn_w3"]])], axis=1)
    wff = np.concatenate([ups.reshape(GATE, D), a["L0_ffn_gate_weight"]]).T
    t["w_ff"] = rows_twice(wff).reshape(2, P, SLICES, RAW).transpose(2, 1, 0, 3)
    t["w_down"] = np.concatenate([a["L0_ffn_sw2"][None], a["L0_ffn_w2"]]).transpose(2, 0, 1)
    t["gbias"] = np.tile(a["L0_ffn_gate_bias"], 3)
    head = (np.arange(2 * P)[:, None] // HD == np.arange(NH)[None]).astype(f32)
    t["headmask"] = np.stack([head[:P], np.concatenate([0 * head[P:D], head[P:D]]),
                              np.concatenate([head[P:D], 0 * head[P:D]])], axis=1)
    t["blockmask"] = head[:D].T
    t["ident"] = np.eye(P, dtype=f32)
    lower = [np.tril(np.ones((n, n), f32), -1).reshape(-1) for n in (GROUPS, E)]
    upper = [np.triu(np.ones((n, n), f32), 1).reshape(-1) for n in (GROUPS, E)]
    t["order"] = np.stack([np.concatenate(m) for m in (lower, upper)]).reshape(-1)
    p = np.arange(P)
    cst = np.zeros((P, 9), f32)
    cst[:, 0], cst[:, 1], cst[:, 2], cst[:, 3] = p, -(p + P), p % LOW, EPS
    cst[:, 4], cst[:, 5] = p % 32 == 0, p % 32 == 1
    cst[:, 6:9] = np.stack([p < P, p < 0, p < D - P], axis=1) * (SCALE - 1.0) + 1.0
    t["cst"] = cst

    nc = bacc.Bacc("TRN2", target_bir_lowering=False, num_devices=1)
    t = {k: np.ascontiguousarray(v) for k, v in t.items()}
    aps = {k: nc.dram_tensor(f"in_{k}", v.shape, _mybir.dt.from_np(v.dtype), kind="ExternalInput").ap()
           for k, v in t.items()}
    shape = (B, 1 + TOK, D)
    out = nc.dram_tensor("out_tokens", shape, _mybir.dt.float32, kind="ExternalOutput").ap()
    build(nc, aps, out)
    return run_bass_kernel_spmd(nc, [{f"in_{k}": v for k, v in t.items()}], core_ids=[0]).results[0]["out_tokens"]
```
